# Optimizing a Trainium2 kernel written in Bass

```python
import numpy as np
import jax
import jax.numpy as jnp

def _softmax(x, axis=-1):
    return jax.nn.softmax(x, axis=axis)

def _gelu(x):
    return jax.nn.gelu(x, approximate=True)

def _silu(x):
    return jax.nn.silu(x)

def _sigmoid(x):
    return jax.nn.sigmoid(x)

def _layernorm(x, axis=-1, eps=1e-05):
    m = jnp.mean(x, axis=axis, keepdims=True)
    v = jnp.var(x, axis=axis, keepdims=True)
    return (x - m) / jnp.sqrt(v + eps)

def _scatter_add(tgt, idx, src, axis=0):
    return tgt.at[idx].add(src)

def _segment_sum(src, seg, n):
    return jax.ops.segment_sum(src, seg, n)
kernel_name = 'mk_perceiver_d1_seqx_r8_464c55'

def setup_inputs(seed: int=0):
    np.random.seed(seed)
    _w = jnp.asarray

    def _rec_inputs():
        import jax
        import jax.numpy as jnp
        _rk = jax.random.key(seed)
        x = -0.0005146 + 1 * jax.random.normal(jax.random.fold_in(_rk, 1), (2, 32, 512), jnp.float32)
        _lenS = 32 - jax.random.randint(jax.random.fold_in(_rk, 7), (2,), 0, max(1, 32 // 4) + 1, jnp.int32)
        _lenS2 = 512 - jax.random.randint(jax.random.fold_in(_rk, 8), (2,), 0, max(1, 512 // 4) + 1, jnp.int32)
        _ctx_4096P = jax.random.normal(jax.random.fold_in(_rk, 11), (2, 16, 512), jnp.float32)
        _ctx_4096c = jax.random.dirichlet(jax.random.fold_in(_rk, 511), 0.3 * jnp.ones((16,), jnp.float32), (2, 512))
        _ctx_4096t = jnp.einsum('bsk,bkd->bsd', _ctx_4096c, _ctx_4096P)
        _ctx_4096t = _ctx_4096t * jax.lax.rsqrt(jnp.mean(jnp.square(_ctx_4096t)) + 1e-12) * 0.953939
        ctx_4096 = -0.0142356 + 1.00583 * (_ctx_4096t + 0.3 * jax.random.normal(jax.random.fold_in(_rk, 611), (2, 512, 512), jnp.float32))
        return (x, ctx_4096)
    x, ctx_4096 = _rec_inputs()

    def _L0_xattn_setup():
        import jax, jax.numpy as jnp
        import numpy as np
        K = 10
        NUM_BITS = 10
        M_METHODS = 4

        def _quantize(coords, num_bits=NUM_BITS):
            cmin = coords.min(axis=1, keepdims=True)
            cmax = coords.max(axis=1, keepdims=True)
            scale = (2 ** num_bits - 1) / (cmax - cmin + 1e-06)
            q = jnp.floor((coords - cmin) * scale)
            return jnp.clip(q, 0, 2 ** num_bits - 1).astype(jnp.int32)

        def _morton_key(q):
            x, y, z = (q[..., 0], q[..., 1], q[..., 2])
            key = jnp.zeros(x.shape, dtype=jnp.int32)
            for b in range(NUM_BITS):
                key = key | (x >> b & 1) << 3 * b + 2 | (y >> b & 1) << 3 * b + 1 | (z >> b & 1) << 3 * b
            return key

        def _hilbert_key(q, num_bits=NUM_BITS):
            n = 3
            X = [q[..., i] for i in range(n)]
            M = 1 << num_bits - 1
            Q = M
            while Q > 1:
                P = Q - 1
                for i in range(n):
                    cond = X[i] & Q > 0
                    t = (X[0] ^ X[i]) & P
                    new_X0 = jnp.where(cond, X[0] ^ P, X[0] ^ t)
                    if i != 0:
                        X[i] = jnp.where(cond, X[i], X[i] ^ t)
                    X[0] = new_X0
                Q >>= 1
            for i in range(1, n):
                X[i] = X[i] ^ X[i - 1]
            t = jnp.zeros_like(X[0])
            Q = M
            while Q > 1:
                t = jnp.where(X[n - 1] & Q > 0, t ^ Q - 1, t)
                Q >>= 1
            X = [xi ^ t for xi in X]
            key = jnp.zeros(X[0].shape, dtype=jnp.int32)
            for b in range(num_bits - 1, -1, -1):
                for i in range(n):
                    key = key << 1 | X[i] >> b & 1
            return key

        def _sorted_indices(coords_bn3):
            q = _quantize(coords_bn3)
            qt = q[..., jnp.array([1, 0, 2])]
            keys = [_morton_key(q), _morton_key(qt), _hilbert_key(q), _hilbert_key(qt)]
            return [jnp.argsort(kk, axis=1) for kk in keys]

        def _window_inds(sorted_idx, k=K):
            B, N = sorted_idx.shape
            i = jnp.arange(N)
            start = jnp.maximum(0, i - k // 2)
            end = jnp.minimum(N, i + k // 2 + 1)
            pos = jnp.minimum(start[:, None] + jnp.arange(k)[None, :], (end - 1)[:, None])
            return jnp.take(sorted_idx, pos, axis=1)

        def _get_graph_features(feats, inds_list, perm, W_lin, b_lin, k=K):
            B, N, C = feats.shape
            center = feats[:, :, None, :]
            gather = jax.vmap(lambda f, idx: f[idx])
            per_method = []
            for inds in inds_list:
                neigh = gather(feats, inds)
                gf = jnp.concatenate([jnp.broadcast_to(center, (B, N, k, C)), neigh - center], axis=-1)
                per_method.append(gf)
            allf = jnp.stack(per_method, axis=-1)
            allf = allf[..., perm]
            total = 2 * C * M_METHODS
            x = allf.reshape(B * N, k, total)
            x16 = x.astype(jnp.float16).astype(jnp.float32)
            headdim = min(32, total)
            nheads = total // headdim
            qh = x16.reshape(B * N, k, nheads, headdim)
            scores = jnp.einsum('bihd,bjhd->bhij', qh, qh) / np.float32(np.sqrt(headdim))
            attn = jax.nn.softmax(scores, axis=-1)
            out = jnp.einsum('bhij,bjhd->bihd', attn, qh).reshape(B * N, k, total)
            fused = out @ W_lin.T + b_lin
            return fused.reshape(B, N, k, 64)

        def _instance_norm(x, axes):
            mu = x.mean(axis=axes, keepdims=True)
            var = x.var(axis=axes, keepdims=True)
            return (x - mu) / jnp.sqrt(var + 1e-05)

        def _lrelu(x):
            return jnp.where(x > 0, x, 0.2 * x)
        key = jax.random.key(seed)
        ks = jax.random.split(key, 8)
        B, N, C = (2, 512, 32)
        tot = M_METHODS * 2 * C
        s = 0.02
        return {'coords': jax.random.normal(ks[0], (B, 3, N), jnp.float32), 'feats': jax.random.normal(ks[1], (B, C, N), jnp.float32), 'W_lin1': jax.random.normal(ks[2], (64, tot), jnp.float32) * s, 'b_lin1': jnp.zeros((64,), jnp.float32), 'W_lin2': jax.random.normal(ks[3], (64, tot), jnp.float32) * s, 'b_lin2': jnp.zeros((64,), jnp.float32), 'W_conv1': jax.random.normal(ks[4], (C, 2 * C), jnp.float32) * s, 'W_conv2': jax.random.normal(ks[5], (2 * C, 2 * C), jnp.float32) * s, 'W_conv3': jax.random.normal(ks[6], (C, 4 * C), jnp.float32) * s}
    _L0_xattn_all = _L0_xattn_setup()
    _L0_xattn_in = {k: v for k, v in _L0_xattn_all.items() if k in ('W_lin1', 'b_lin1', 'W_lin2', 'b_lin2', 'W_conv1', 'W_conv2', 'W_conv3')}
    del _L0_xattn_all

    def _L0_attn_setup():
        import jax, jax.numpy as jnp
        import numpy as np
        B, T, H, S, F, G = (2, 256, 512, 128, 1248, 6)
        GRAD_ORDER_MIN = 4
        THD = 2.5
        key = jax.random.key(seed)
        ks = jax.random.split(key, 9)
        sc = 0.02
        hidden_states = jax.random.normal(ks[0], (B, T, H), jnp.float32)
        up_w = jax.random.normal(ks[1], (S, H), jnp.float32) * sc
        gate_w = jax.random.normal(ks[2], (S, H), jnp.float32) / np.sqrt(H)
        local_point = jax.random.normal(ks[3], (S,), jnp.float32)
        local_approx_output = jax.random.normal(ks[4], (H, S), jnp.float32) * sc
        fuse_weight = jax.random.normal(ks[5], (H, S, G), jnp.float32) * sc
        discount_factor = jnp.asarray(np.cumsum(np.log(np.arange(1, G + 1, dtype=np.float64))), jnp.float32)
        ffn_gate_w = jax.random.normal(ks[6], (F, H), jnp.float32) * sc
        ffn_up_w = jax.random.normal(ks[7], (F, H), jnp.float32) * sc
        ffn_down_w = jax.random.normal(ks[8], (H, F), jnp.float32) * sc
        return {'hidden_states': hidden_states, 'up_w': up_w, 'gate_w': gate_w, 'local_point': local_point, 'local_approx_output': local_approx_output, 'fuse_weight': fuse_weight, 'discount_factor': discount_factor, 'ffn_gate_w': ffn_gate_w, 'ffn_up_w': ffn_up_w, 'ffn_down_w': ffn_down_w}
    _L0_attn_all = _L0_attn_setup()
    _L0_attn_in = {k: v for k, v in _L0_attn_all.items() if k in ('up_w', 'gate_w', 'local_point', 'local_approx_output', 'fuse_weight', 'discount_factor', 'ffn_gate_w', 'ffn_up_w', 'ffn_down_w')}
    del _L0_attn_all

    def _L0_ffn_setup():
        import jax, jax.numpy as jnp
        import numpy as np
        B, S, IN, OUT = (4, 256, 512, 512)
        E, K, R = (8, 2, 16)
        CAP_FACTOR = 3.0
        ALPHA = 1.0 / R
        LN_EPS = 1e-05
        key = jax.random.key(seed)
        ks = jax.random.split(key, 6)
        return {'x': jax.random.normal(ks[0], (B, S, IN), dtype=jnp.float32), 'weight': jax.random.normal(ks[1], (OUT, IN), dtype=jnp.float32) * 0.02, 'lora_A': jax.random.normal(ks[2], (E, IN, R), dtype=jnp.float32) / np.sqrt(R), 'lora_B': jax.random.normal(ks[3], (E, R, OUT), dtype=jnp.float32) * 0.02, 'gw1': jax.random.normal(ks[4], (4 * E, IN), dtype=jnp.float32) * 0.02, 'gb1': jnp.zeros((4 * E,), dtype=jnp.float32), 'ln_gamma': jnp.ones((4 * E,), dtype=jnp.float32), 'ln_beta': jnp.zeros((4 * E,), dtype=jnp.float32), 'gw2': jax.random.normal(ks[5], (E, 4 * E), dtype=jnp.float32) * 0.02, 'gb2': jnp.zeros((E,), dtype=jnp.float32)}
    _L0_ffn_all = _L0_ffn_setup()
    _L0_ffn_in = {k: v for k, v in _L0_ffn_all.items() if k in ('weight', 'lora_A', 'lora_B', 'gw1', 'gb1', 'ln_gamma', 'ln_beta', 'gw2', 'gb2')}
    del _L0_ffn_all
    return {'x': x, 'ctx_4096': ctx_4096, 'L0_xattn_W_lin1': _L0_xattn_in['W_lin1'], 'L0_xattn_b_lin1': _L0_xattn_in['b_lin1'], 'L0_xattn_W_lin2': _L0_xattn_in['W_lin2'], 'L0_xattn_b_lin2': _L0_xattn_in['b_lin2'], 'L0_xattn_W_conv1': _L0_xattn_in['W_conv1'], 'L0_xattn_W_conv2': _L0_xattn_in['W_conv2'], 'L0_xattn_W_conv3': _L0_xattn_in['W_conv3'], 'L0_attn_up_w': _L0_attn_in['up_w'], 'L0_attn_gate_w': _L0_attn_in['gate_w'], 'L0_attn_local_point': _L0_attn_in['local_point'], 'L0_attn_local_approx_output': _L0_attn_in['local_approx_output'], 'L0_attn_fuse_weight': _L0_attn_in['fuse_weight'], 'L0_attn_discount_factor': _L0_attn_in['discount_factor'], 'L0_attn_ffn_gate_w': _L0_attn_in['ffn_gate_w'], 'L0_attn_ffn_up_w': _L0_attn_in['ffn_up_w'], 'L0_attn_ffn_down_w': _L0_attn_in['ffn_down_w'], 'L0_ffn_weight': _L0_ffn_in['weight'], 'L0_ffn_lora_A': _L0_ffn_in['lora_A'], 'L0_ffn_lora_B': _L0_ffn_in['lora_B'], 'L0_ffn_gw1': _L0_ffn_in['gw1'], 'L0_ffn_gb1': _L0_ffn_in['gb1'], 'L0_ffn_ln_gamma': _L0_ffn_in['ln_gamma'], 'L0_ffn_ln_beta': _L0_ffn_in['ln_beta'], 'L0_ffn_gw2': _L0_ffn_in['gw2'], 'L0_ffn_gb2': _L0_ffn_in['gb2']}

def reference(x, ctx_4096, L0_xattn_W_lin1, L0_xattn_b_lin1, L0_xattn_W_lin2, L0_xattn_b_lin2, L0_xattn_W_conv1, L0_xattn_W_conv2, L0_xattn_W_conv3, L0_attn_up_w, L0_attn_gate_w, L0_attn_local_point, L0_attn_local_approx_output, L0_attn_fuse_weight, L0_attn_discount_factor, L0_attn_ffn_gate_w, L0_attn_ffn_up_w, L0_attn_ffn_down_w, L0_ffn_weight, L0_ffn_lora_A, L0_ffn_lora_B, L0_ffn_gw1, L0_ffn_gb1, L0_ffn_ln_gamma, L0_ffn_ln_beta, L0_ffn_gw2, L0_ffn_gb2):
    import jax
    import jax.numpy as jnp

    def _L0_xattn_ref(coords, feats, W_lin1, b_lin1, W_lin2, b_lin2, W_conv1, W_conv2, W_conv3):
        import jax, jax.numpy as jnp
        import numpy as np
        K = 10
        NUM_BITS = 10
        M_METHODS = 4

        def _quantize(coords, num_bits=NUM_BITS):
            cmin = coords.min(axis=1, keepdims=True)
            cmax = coords.max(axis=1, keepdims=True)
            scale = (2 ** num_bits - 1) / (cmax - cmin + 1e-06)
            q = jnp.floor((coords - cmin) * scale)
            return jnp.clip(q, 0, 2 ** num_bits - 1).astype(jnp.int32)

        def _morton_key(q):
            x, y, z = (q[..., 0], q[..., 1], q[..., 2])
            key = jnp.zeros(x.shape, dtype=jnp.int32)
            for b in range(NUM_BITS):
                key = key | (x >> b & 1) << 3 * b + 2 | (y >> b & 1) << 3 * b + 1 | (z >> b & 1) << 3 * b
            return key

        def _hilbert_key(q, num_bits=NUM_BITS):
            n = 3
            X = [q[..., i] for i in range(n)]
            M = 1 << num_bits - 1
            Q = M
            while Q > 1:
                P = Q - 1
                for i in range(n):
                    cond = X[i] & Q > 0
                    t = (X[0] ^ X[i]) & P
                    new_X0 = jnp.where(cond, X[0] ^ P, X[0] ^ t)
                    if i != 0:
                        X[i] = jnp.where(cond, X[i], X[i] ^ t)
                    X[0] = new_X0
                Q >>= 1
            for i in range(1, n):
                X[i] = X[i] ^ X[i - 1]
            t = jnp.zeros_like(X[0])
            Q = M
            while Q > 1:
                t = jnp.where(X[n - 1] & Q > 0, t ^ Q - 1, t)
                Q >>= 1
            X = [xi ^ t for xi in X]
            key = jnp.zeros(X[0].shape, dtype=jnp.int32)
            for b in range(num_bits - 1, -1, -1):
                for i in range(n):
                    key = key << 1 | X[i] >> b & 1
            return key

        def _sorted_indices(coords_bn3):
            q = _quantize(coords_bn3)
            qt = q[..., jnp.array([1, 0, 2])]
            keys = [_morton_key(q), _morton_key(qt), _hilbert_key(q), _hilbert_key(qt)]
            return [jnp.argsort(kk, axis=1) for kk in keys]

        def _window_inds(sorted_idx, k=K):
            B, N = sorted_idx.shape
            i = jnp.arange(N)
            start = jnp.maximum(0, i - k // 2)
            end = jnp.minimum(N, i + k // 2 + 1)
            pos = jnp.minimum(start[:, None] + jnp.arange(k)[None, :], (end - 1)[:, None])
            return jnp.take(sorted_idx, pos, axis=1)

        def _get_graph_features(feats, inds_list, perm, W_lin, b_lin, k=K):
            B, N, C = feats.shape
            center = feats[:, :, None, :]
            gather = jax.vmap(lambda f, idx: f[idx])
            per_method = []
            for inds in inds_list:
                neigh = gather(feats, inds)
                gf = jnp.concatenate([jnp.broadcast_to(center, (B, N, k, C)), neigh - center], axis=-1)
                per_method.append(gf)
            allf = jnp.stack(per_method, axis=-1)
            allf = allf[..., perm]
            total = 2 * C * M_METHODS
            x = allf.reshape(B * N, k, total)
            x16 = x.astype(jnp.float16).astype(jnp.float32)
            headdim = min(32, total)
            nheads = total // headdim
            qh = x16.reshape(B * N, k, nheads, headdim)
            scores = jnp.einsum('bihd,bjhd->bhij', qh, qh) / np.float32(np.sqrt(headdim))
            attn = jax.nn.softmax(scores, axis=-1)
            out = jnp.einsum('bhij,bjhd->bihd', attn, qh).reshape(B * N, k, total)
            fused = out @ W_lin.T + b_lin
            return fused.reshape(B, N, k, 64)

        def _instance_norm(x, axes):
            mu = x.mean(axis=axes, keepdims=True)
            var = x.var(axis=axes, keepdims=True)
            return (x - mu) / jnp.sqrt(var + 1e-05)

        def _lrelu(x):
            return jnp.where(x > 0, x, 0.2 * x)
        inds_sorted = _sorted_indices(coords.transpose(0, 2, 1))
        inds_list = [_window_inds(s) for s in inds_sorted]
        perm1 = jnp.array([2, 0, 3, 1])
        perm2 = jnp.array([1, 3, 0, 2])
        f0 = feats.transpose(0, 2, 1)
        g1 = _get_graph_features(f0, inds_list, perm1, W_lin1, b_lin1)
        h1 = jnp.einsum('oc,bnkc->bonk', W_conv1, g1)
        h1 = _lrelu(_instance_norm(h1, (2, 3)))
        feats1 = h1.max(axis=-1)
        g2 = _get_graph_features(feats1.transpose(0, 2, 1), inds_list, perm2, W_lin2, b_lin2)
        h2 = jnp.einsum('oc,bnkc->bonk', W_conv2, g2)
        h2 = _lrelu(_instance_norm(h2, (2, 3)))
        feats2 = h2.max(axis=-1)
        f3 = jnp.concatenate([feats, feats1, feats2], axis=1)
        h3 = jnp.einsum('oc,bcn->bon', W_conv3, f3)
        return _lrelu(_instance_norm(h3, (2,)))

    def _L0_attn_ref(hidden_states, up_w, gate_w, local_point, local_approx_output, fuse_weight, discount_factor, ffn_gate_w, ffn_up_w, ffn_down_w):
        import jax, jax.numpy as jnp
        import numpy as np
        B, T, H, S, F, G = (2, 256, 512, 128, 1248, 6)
        GRAD_ORDER_MIN = 4
        THD = 2.5
        approx_up = hidden_states @ up_w.T
        gate_pre = hidden_states @ gate_w.T
        delta = gate_pre - local_point
        neg_factor = jnp.where(delta > 0, 1.0, -1.0).astype(hidden_states.dtype)
        delta_abs = jnp.abs(delta)
        log_delta = jnp.log(delta_abs)
        keep = (delta_abs <= THD).astype(hidden_states.dtype)
        approx_out = approx_up @ local_approx_output.T
        for idx in range(G):
            m = idx + 1
            dterm = jnp.exp(log_delta * m - discount_factor[idx])
            if m % 2 == 1:
                dterm = dterm * neg_factor
            tmp = dterm * approx_up
            if m > GRAD_ORDER_MIN:
                tmp = tmp * keep
            approx_out = approx_out + tmp @ fuse_weight[:, :, idx].T
        ffn_out = jax.nn.silu(hidden_states @ ffn_gate_w.T) * (hidden_states @ ffn_up_w.T) @ ffn_down_w.T
        return approx_out + ffn_out

    def _L0_ffn_ref(x, weight, lora_A, lora_B, gw1, gb1, ln_gamma, ln_beta, gw2, gb2):
        import jax, jax.numpy as jnp
        import numpy as np
        B, S, IN, OUT = (4, 256, 512, 512)
        E, K, R = (8, 2, 16)
        CAP_FACTOR = 3.0
        ALPHA = 1.0 / R
        LN_EPS = 1e-05
        orig_shape = x.shape
        xf = x.reshape(-1, orig_shape[-1])
        N = xf.shape[0]
        capacity = int(CAP_FACTOR * N / E)
        h = xf @ gw1.T + gb1
        mu = jnp.mean(h, axis=-1, keepdims=True)
        var = jnp.mean((h - mu) ** 2, axis=-1, keepdims=True)
        h = (h - mu) * jax.lax.rsqrt(var + LN_EPS) * ln_gamma + ln_beta
        h = jax.nn.relu(h)
        gates = h @ gw2.T + gb2
        top_v, top_i = jax.lax.top_k(gates, K)
        top_g = jax.nn.softmax(top_v, axis=-1)
        onehot = (top_i[..., None] == jnp.arange(E)).astype(xf.dtype)
        counts = onehot.sum(axis=0)
        allowed = (counts <= capacity).astype(xf.dtype)
        w = jnp.einsum('nke,nk,ke->ne', onehot, top_g, allowed)
        main = xf @ weight.T
        tmp = jnp.einsum('ni,eir->enr', xf, lora_A)
        tmp = tmp * w.T[:, :, None]
        lora = jnp.einsum('enr,ero->no', tmp, lora_B) * ALPHA
        out = main + lora
        return out.reshape(*orig_shape[:-1], weight.shape[0])
    x = x + _L0_xattn_ref(ctx_4096, _layernorm(x, axis=-1), L0_xattn_W_lin1, L0_xattn_b_lin1, L0_xattn_W_lin2, L0_xattn_b_lin2, L0_xattn_W_conv1, L0_xattn_W_conv2, L0_xattn_W_conv3)
    x = x + _L0_attn_ref(_layernorm(x, axis=-1), L0_attn_up_w, L0_attn_gate_w, L0_attn_local_point, L0_attn_local_approx_output, L0_attn_fuse_weight, L0_attn_discount_factor, L0_attn_ffn_gate_w, L0_attn_ffn_up_w, L0_attn_ffn_down_w)
    x = x + _L0_ffn_ref(_layernorm(x, axis=-1), L0_ffn_weight, L0_ffn_lora_A, L0_ffn_lora_B, L0_ffn_gw1, L0_ffn_gb1, L0_ffn_ln_gamma, L0_ffn_ln_beta, L0_ffn_gw2, L0_ffn_gb2)
    return x

_drawn_inputs = setup_inputs


def setup_inputs(seed=0):
    import zlib

    import numpy as np

    out = dict(_drawn_inputs(seed))
    spreads = {'L0_xattn_b_lin1': (0.0, 0.8),
     'L0_xattn_b_lin2': (0.0, 0.8),
     'L0_ffn_gb1': (0.0, 0.8),
     'L0_ffn_ln_gamma': (1.0, 0.6),
     'L0_ffn_ln_beta': (0.0, 0.8),
     'L0_ffn_gb2': (0.0, 0.655)}
    factors = {'L0_ffn_lora_A': 6.648, 'L0_ffn_lora_B': 6.613, 'L0_ffn_gw1': 7.549, 'L0_ffn_gw2': 7.414}
    for name, (base, spread) in spreads.items():
        noise = np.random.default_rng([zlib.crc32(name.encode()), seed]).standard_normal(out[name].shape)
        drawn = base * np.exp(spread * noise) if base else spread * noise
        out[name] = jnp.asarray(drawn.astype(out[name].dtype))
    for name, factor in factors.items():
        out[name] = (out[name] * factor).astype(out[name].dtype)
    return out
```

```python
import concourse.bass as bass
from concourse import mybir
from contextlib import ExitStack

F32 = mybir.dt.float32
F16 = mybir.dt.float16
BF16 = mybir.dt.bfloat16
I32 = mybir.dt.int32
ALU = mybir.AluOpType
ACT = mybir.ActivationFunctionType
AX = mybir.AxisListType.X

P = 128
B, C, N = 2, 32, 512
K = 10
LEFT = K // 2
M = 4
BITS = 10
NK = N // P
PB = 3
SLOT = 32
BLOCKS = 43
PIECES = 4
PTS = BLOCKS * PB
PTS_LAST = N - (PIECES - 1) * PTS
COLS = BLOCKS * SLOT
NC = BLOCKS * K
STEPS = 2 * B * PIECES
PERMS = ([2, 0, 3, 1], [1, 3, 0, 2])
THIRDS = [(0, 16), (16, 16), (32, 11)]
FSW = LEFT + PIECES * PTS + K
OUT_CH = [C, 2 * C]
PASSES_BEFORE = [0, 3, 6, 12, 18]
TAIL_AT = [PIECES * (i + 1) + 2 for i in range(2 * B)]
F = 1248
FCH = [(i * P, min(P, F - i * P)) for i in range((F + P - 1) // P)]
NF = len(FCH)
S = 128
G = 6
E = 8
R = 16
T = B * C
CAP = int(3.0 * T / E)
EPS = 1e-5
CONST_WIDTHS = [("own", PB), ("i10", K), ("negblk", P), ("posblk", P), ("eps", 1), ("nhalf", 1), ("point", 32),
                ("digit_w", 16), ("rep", P), ("mean0", P), ("mean1", P), ("ones", P)]
CONST_AT = {name: (sum(w for _, w in CONST_WIDTHS[:i]), w) for i, (name, w) in enumerate(CONST_WIDTHS)}
CONST_W = sum(w for _, w in CONST_WIDTHS)


def gu_bank(banks, i):
    return banks[(2, 5, 6)[i % 3]]


def perceiver_layer(nc, x, coords, consts, ident, wlin, wconv, blin, wc3, upgate, local, fuse, gate, up, ffn2a, ffn2b,
                    moe1, moe2, moe3, rowc, gw2, out):
    ctx = ExitStack()
    with ctx:
        def sb(name, shape, dt=F32):
            return ctx.enter_context(nc.sbuf_tensor(name, shape, dt))

        def sem(name):
            return ctx.enter_context(nc.semaphore(name))

        def view(t, p0, np_, off, dims):
            base = t[p0:p0 + np_, :]
            return bass.AP(base.tensor, base.offset + off, [list(base.ap[0])] + [list(d) for d in dims])

        cst = sb("cst", [P, CONST_W])

        def const(name):
            a, w = CONST_AT[name]
            return cst[:, a:a + w]

        id_sb = sb("id_sb", [P, P])
        iota16 = sb("iota16", [P, N], F16)
        negones = const("negblk")
        posones = const("posblk")

        x_sb = sb("x_sb", [C, B, N])
        co_sb = sb("co_sb", [6, N])
        wlin_sb = sb("wlin_sb", [64, 2, 256])
        wconv_sb = sb("wconv_sb", [64, 2, 128])
        blin_sb = sb("blin_sb", [64, 2])
        wc3_sb = sb("wc3_sb", [64, 3, C])
        upgate_sb = sb("upgate_sb", [P, NK, 2 * S])
        local_sb = sb("local_sb", [P, 1 + G])
        gate_sb = sb("gate_sb", [P, NK, F])
        rowc_sb = sb("rowc_sb", [T, 3 * 32 + E + E])
        gw2_sb = sb("gw2_sb", [32, E])
        oh = sb("oh", [P, B * NK * M * N], BF16)
        qbd = sb("qbd", [P, 2 * BLOCKS * P], F16)
        qtbd = sb("qtbd", [P, 2 * BLOCKS * P], F16)
        fz = sb("fz", [P, 3 * NK * M * P], BF16)
        ot = sb("ot", [P, PIECES * BLOCKS * PB * K])
        qc = sb("qc", [P, 2 * COLS], F16)
        qt = sb("qt", [P, COLS], F16)
        fs = sb("fs", [P, B * FSW])
        f4 = sb("f4", [P, B * PIECES * PTS])
        f16h = sb("f16h", [P, N], F16)
        f16f = sb("f16f", [P, B * PIECES * PTS])
        sc = sb("sc", [P, NC])
        mx = sb("mx", [P, BLOCKS])
        md = sb("md", [P, NC])
        ex = sb("ex", [P, 2 * NC])
        ri = sb("ri", [P, NC])
        pn = sb("pn", [P, NC])
        ph = sb("ph", [P, 2 * NC], F16)
        px = sb("px", [P, 2 * 2 * COLS], F16)
        hm = sb("hm", [P, 2 * PTS])
        hn = sb("hn", [P, 2 * PTS])
        bst = sb("bst", [P, 8 * 6])
        mv = sb("mv", [P, 8])
        wn_sb = sb("wn_sb", [P, 2, 2, 64])
        bv_sb = sb("bv_sb", [P, 2])
        ft = [sb("ft0", [C, B, N]), sb("ft1", [C, B, N]), sb("ft2", [2 * C, B, N])]
        fparts = sb("fparts", [P, 2 * P])
        fpartb = sb("fpartb", [P, 3 * P], BF16)
        qv = sb("qv", [P, 3 * 24])
        qvi = sb("qvi", [P, 24], I32)
        rk = sb("rk", [P, 32])
        sg = sb("sg", [P, 16])
        qs = sb("qs", [6, 8])
        rhs2, src2, *junk = (px[:, i * N:(i + 1) * N].bitcast(BF16) for i in range(6))
        px_words = px[:, :].bitcast(F32)
        kx = px_words[:, 1536:1632].bitcast(I32)
        kt = px_words[:, 1632:2016].bitcast(I32)
        dg = px_words[:, 2016:2016 + NK * 40]
        actT = fs[:, 0:NF * T].rearrange("p (a b) -> p a b", a=NF)
        xnT = fs[:, NF * T:(NF + NK) * T].rearrange("p (a b) -> p a b", a=NK)
        sig = fs[:, (NF + NK) * T:(NF + NK + 2) * T]
        hT, tT = f4[0:32, 0:T], f4[:, T:2 * T]
        moe1_w = E * R + 32
        moe1_sb = oh[:, 2 * (NF + NK) * N:2 * (NF + NK) * N + 2 * NK * moe1_w].bitcast(F32)
        moe3_sb = qtbd[:, 2 * (G + 1) * N:2 * (G + 2) * N].bitcast(F32)
        up_sb = qbd[:, 0:2 * NK * F].bitcast(F32)
        ot_at = [0]

        def over_ot(parts, *dims):
            w = 1
            for d in dims:
                w *= d
            ot_at[0] += w
            t = ot[0:parts, ot_at[0] - w:ot_at[0]]
            return t if len(dims) == 1 else t.rearrange("p (a b) -> p a b", a=dims[0])

        x1, h3 = over_ot(C, B, N), over_ot(C, B, N)
        xr, x2, xn2, mo = (over_ot(T, N) for _ in range(4))
        gp = over_ot(P, 12 * T)
        lw = ot[:, 0:16 * 256].bitcast(BF16)
        ffn2_sb = oh[:, 0:2 * NF * N].bitcast(F32)
        moe2_sb = oh[:, 2 * NF * N:2 * NF * N + 2 * NK * N].bitcast(F32)
        fuse_sb = qtbd[:, 0:2 * (G + 1) * N].bitcast(F32)
        edf = sb("edf", [P, G])
        rst = sb("rst", [T, 16])

        s_ps = ctx.enter_context(nc.psum_tensor("s_ps", [P, 3 * 512], F32))
        o_ps = ctx.enter_context(nc.psum_tensor("o_ps", [P, 2 * 512], F32))
        mt_ps = ctx.enter_context(nc.psum_tensor("mt_ps", [P, 512], F32))
        r_ps = ctx.enter_context(nc.psum_tensor("r_ps", [P, 512], F32))
        z_ps = ctx.enter_context(nc.psum_tensor("z_ps", [P, 512], F32))
        banks = [s_ps[:, 0:512], s_ps[:, 512:1024], s_ps[:, 1024:1536], o_ps[:, 0:512], o_ps[:, 512:1024],
                 mt_ps[:, :], r_ps[:, :], z_ps[:, :]]

        ld_first = sem("ld_first")
        ld_const = sem("ld_const")
        ld_graph = sem("ld_graph")
        ld_ffn = sem("ld_ffn")
        ld_late = sem("ld_late")
        ld_fuse = sem("ld_fuse")
        ld_up = sem("ld_up")
        stored = sem("stored")
        dve_step = sem("dve_step")
        act_step = sem("act_step")
        pool_step = sem("pool_step")
        pads_set = sem("pads_set")
        scaled_co = sem("scaled_co")
        co_turned = sem("co_turned")
        digits_ready = sem("digits_ready")
        digits_turned = sem("digits_turned")
        weights_ready = sem("weights_ready")
        diff_ready = sem("diff_ready")
        counted_a = sem("counted_a")
        counted_d = sem("counted_d")
        ranks_ready = sem("ranks_ready")
        onehot_ready = sem("onehot_ready")
        var_ready = sem("var_ready")
        rstd_ready = sem("rstd_ready")
        ft_ready = sem("ft_ready")
        ft_turned = sem("ft_turned")
        fz_ready = sem("fz_ready")
        rep_ready = sem("rep_ready")
        rep_used = sem("rep_used")
        sorted_ready = sem("sorted_ready")
        fs_ready = sem("fs_ready")
        fold_ready = sem("fold_ready")
        fold_used = sem("fold_used")
        q_ready = sem("q_ready")
        bd_ready = sem("bd_ready")
        s_ready = sem("s_ready")
        max_ready = sem("max_ready")
        md_ready = sem("md_ready")
        mt_ready = sem("mt_ready")
        sub_ready = sem("sub_ready")
        exp_ready = sem("exp_ready")
        sum_ready = sem("sum_ready")
        probs_ready = sem("probs_ready")
        av_ready = sem("av_ready")
        ot_ready = sem("ot_ready")
        h_ready = sem("h_ready")
        h_used = sem("h_used")
        stat_in = sem("stat_in")
        stat_mean = sem("stat_mean")
        stat_mean_used = sem("stat_mean_used")
        h3_ready = sem("h3_ready")
        xn_ready = sem("xn_ready")
        xn_turned = sem("xn_turned")
        xnT_ready = sem("xnT_ready")
        gp_ready = sem("gp_ready")
        edf_ready = sem("edf_ready")
        tmp_ready = sem("tmp_ready")
        gu_ready = sem("gu_ready")
        gu_exp = sem("gu_exp")
        gu_used = sem("gu_used")
        y_ready = sem("y_ready")
        xr_ready = sem("xr_ready")
        xn2_ready = sem("xn2_ready")
        xn2_turned = sem("xn2_turned")
        xn2T_ready = sem("xn2T_ready")
        moe_h = sem("moe_h")
        moe_relu = sem("moe_relu")
        moe_relu_turned = sem("moe_relu_turned")
        moe_hT = sem("moe_hT")
        moe_gates = sem("moe_gates")
        top_exp_in = sem("top_exp_in")
        top_exp = sem("top_exp")
        picks_ready = sem("picks_ready")
        counts_ready = sem("counts_ready")
        lora_ready = sem("lora_ready")
        lora_turned = sem("lora_turned")
        lora_T = sem("lora_T")
        moe_out = sem("moe_out")
        y_out = sem("y_out")

        block = ctx.enter_context(nc.Block())

        @block.sync
        def _(sp):
            sp.dma_start(co_sb[:], coords).then_inc(ld_first, 16)
            sp.dma_start(x_sb[:], x).then_inc(ld_first, 16)
            sp.dma_start(id_sb[:], ident).then_inc(ld_first, 16)
            sp.dma_start(cst[:], consts).then_inc(ld_const, 16)
            sp.dma_start(wlin_sb[:], wlin).then_inc(ld_graph, 16)
            sp.dma_start(wconv_sb[:], wconv).then_inc(ld_graph, 16)
            sp.dma_start(blin_sb[:], blin).then_inc(ld_graph, 16)
            sp.dma_start(wc3_sb[:], wc3).then_inc(ld_graph, 16)
            sp.dma_start(upgate_sb[:], upgate).then_inc(ld_ffn, 16)
            sp.dma_start(local_sb[:], local).then_inc(ld_ffn, 16)
            sp.dma_start(gate_sb[:], gate).then_inc(ld_ffn, 16)
            sp.dma_start(rowc_sb[:], rowc).then_inc(ld_ffn, 16)
            sp.dma_start(gw2_sb[:], gw2).then_inc(ld_ffn, 16)
            sp.wait_ge(sorted_ready, 4)
            sp.dma_start(ffn2_sb[:, 0:(NF - 1) * N], ffn2a).then_inc(ld_late, 16)
            sp.dma_start(ffn2_sb[0:FCH[-1][1], (NF - 1) * N:NF * N], ffn2b).then_inc(ld_late, 16)
            sp.dma_start(moe2_sb, moe2).then_inc(ld_late, 16)
            sp.dma_start(moe1_sb, moe1).then_inc(ld_late, 16)
            sp.wait_ge(s_ready, STEPS)
            sp.dma_start(up_sb, up).then_inc(ld_up, 16)
            sp.wait_ge(av_ready, 3 * STEPS)
            sp.dma_start(fuse_sb, fuse).then_inc(ld_fuse, 16)
            sp.dma_start(moe3_sb, moe3).then_inc(ld_fuse, 16)
            sp.wait_ge(y_out, 1)
            sp.dma_start(out, xn2).then_inc(stored, 16)
            sp.wait_ge(stored, 16)

        @block.gpsimd
        def _(pool):
            step = [0]

            def link(ins):
                step[0] += 1
                ins.then_inc(pool_step, 1)
                pool.wait_ge(pool_step, step[0])

            pool.memset(bst[:], 0.0).then_inc(pads_set, 1)
            pool.iota(iota16[:], [[1, N]], base=0, channel_multiplier=0,
                      allow_small_or_imprecise_dtypes=True).then_inc(pads_set, 1)
            pool.memset(src2, 0.0).then_inc(pads_set, 1)
            pool.memset(rhs2, 0.0).then_inc(pads_set, 1)
            pool.memset(fz[:].bitcast(F32), 0.0).then_inc(pads_set, 1)
            pool.memset(fs[:], 0.0).then_inc(pads_set, 1)
            pool.memset(f4[:], 0.0).then_inc(pads_set, 1)
            pool.memset(f16f[:], 0.0).then_inc(pads_set, 1)
            pool.memset(qc[:].bitcast(F32), 0.0).then_inc(pads_set, 1)
            pool.memset(qbd[:].bitcast(F32), 0.0).then_inc(pads_set, 1)
            pool.memset(qtbd[:].bitcast(F32), 0.0).then_inc(pads_set, 1)
            pool.wait_ge(ld_const, 16)

            def rstd(n, col, np_):
                pool.wait_ge(var_ready, n + 1)
                t, w = col
                link(pool.tensor_tensor(t, t, eps_of(np_, w), ALU.add))
                pool.tensor_tensor(t, t, half_of(np_, w), ALU.pow).then_inc(rstd_ready, 1)

            def eps_of(np_, w):
                return view(cst, 0, np_, CONST_AT["eps"][0], [[0, w]])

            def half_of(np_, w):
                return view(cst, 0, np_, CONST_AT["nhalf"][0], [[0, w]])

            def windows(g):
                lb, q = divmod(g, PIECES)
                b = lb % B
                pool.wait_ge(fs_ready, 2 * (lb + 1))
                if g >= 2:
                    pool.wait_ge(bd_ready, 8 * (g - 1))
                    pool.wait_ge(s_ready, g - 1)
                first = q * PTS
                qo = (g % 2) * COLS
                near = view(fs, 0, P, b * FSW + first, [[PB, BLOCKS], [1, PB], [1, K]])
                mid = view(f4, 0, P, b * PIECES * PTS + first, [[PB, BLOCKS], [1, PB], [0, K]])
                dst = view(qc, 0, P, qo, [[SLOT, BLOCKS], [K, PB], [1, K]])
                main = pool.tensor_tensor(dst, near, mid, ALU.subtract)
                if q > 0:
                    main.then_inc(q_ready, 1)
                    return
                link(main)
                for i in range(LEFT):
                    w = LEFT - i
                    at = qo + (i // PB) * SLOT + (i % PB) * K
                    last = pool.tensor_tensor(view(qc, 0, P, at, [[1, w]]),
                                              view(fs, 0, P, b * FSW + LEFT + i + LEFT, [[0, w]]),
                                              view(f4, 0, P, b * PIECES * PTS + i, [[0, w]]), ALU.subtract)
                    if i < LEFT - 1:
                        link(last)
                last.then_inc(q_ready, 1)

            def spread_max(g):
                pool.wait_ge(max_ready, g + 1)
                if g >= 1:
                    pool.wait_ge(mt_ready, g)
                pool.tensor_tensor(view(md, 0, P, 0, [[K, BLOCKS], [1, K]]),
                                   view(mx, 0, P, 0, [[1, BLOCKS], [0, K]]),
                                   view(cst, 0, P, CONST_AT["i10"][0], [[0, BLOCKS], [1, K]]),
                                   ALU.mult).then_inc(md_ready, 1)

            rstd(0, (mv[0:C, 1:4:2], 2), C)
            windows(0)
            for t in range(STEPS + 3):
                if 1 <= t <= STEPS:
                    spread_max(t - 1)
                if t in TAIL_AT:
                    rstd(1 + TAIL_AT.index(t), (mv[:, 3:4], 1), P)
                if t + 1 < STEPS:
                    windows(t + 1)
            rstd(5, (mv[0:C, 1:4:2], 2), C)
            rstd(6, (mv[0:C, 1:4:2], 2), C)
            rstd(7, (rst[:, 1:2], 1), T)
            rstd(8, (rst[:, 3:4], 1), T)

        @block.scalar
        def _(act):
            step = [0]

            def link(ins):
                step[0] += 1
                ins.then_inc(act_step, 1)
                act.wait_ge(act_step, step[0])

            for i in range(16):
                act.wait_ge(diff_ready, 2 * i + 1)
                if i >= 2:
                    act.wait_ge(counted_a, i - 1)
                act.activation(junk[i % 2], banks[(2 * i) % 8], ACT.Sign, accum_out=sg[:, i:i + 1])\
                   .then_inc(counted_a, 1)

            def features(lb):
                b = lb % B
                act.wait_ge(rep_ready, lb + 1)
                if lb >= 2:
                    act.wait_ge(q_ready, 4 * (lb - 1))
                    act.wait_ge(h_ready, PASSES_BEFORE[lb - 1])
                at = b * PIECES * PTS
                link(act.activation(f4[:, at:at + N], z_ps[:, :], ACT.Copy))
                link(act.activation(f16h[:], z_ps[:, :], ACT.Copy))
                act.activation(f16f[:, at:at + N], f16h[:], ACT.Copy).then_inc(rep_used, 1)
                act.wait_ge(sorted_ready, lb + 1)
                at = b * FSW
                act.activation(fs[:, at + LEFT:at + LEFT + N], z_ps[:, :], ACT.Copy).then_inc(fs_ready, 1)
                act.activation(fs[:, at + LEFT + N:at + FSW], view(z_ps, 0, P, N - 1, [[0, FSW - LEFT - N]]),
                               ACT.Copy).then_inc(fs_ready, 1)

            def exps(g):
                act.wait_ge(sub_ready, g + 1)
                if g >= 2:
                    act.wait_ge(probs_ready, g - 1)
                e = (g % 2) * NC
                act.activation(ex[:, e:e + NC], sc[:], ACT.Exp, scale=float(1.0 / 32 ** 0.5)).then_inc(exp_ready, 1)

            def evacuate(g):
                lb, q = divmod(g, PIECES)
                if q == 0 and lb >= 1:
                    act.wait_ge(h_ready, PASSES_BEFORE[lb])
                for j, (t0, n) in enumerate(THIRDS):
                    i = 3 * g + j
                    act.wait_ge(av_ready, i + 1)
                    bank = (i % 2) * 512
                    dst = view(ot, 0, P, (q * BLOCKS + t0) * PB * K, [[PB * K, n], [1, PB * K]])
                    act.activation(dst, view(o_ps, 0, P, bank, [[SLOT, n], [1, PB * K]]), ACT.Copy)\
                       .then_inc(ot_ready, 1)

            act.wait_ge(pads_set, 11)
            features(0)
            features(1)
            for t in range(STEPS + 3):
                if 2 <= t < STEPS + 2:
                    evacuate(t - 2)
                if t in TAIL_AT[:2]:
                    features(2 + TAIL_AT.index(t))
                if 1 <= t <= STEPS:
                    exps(t - 1)

            act.wait_ge(ld_ffn, 80)
            act.activation(edf[:], local_sb[:, 1:1 + G], ACT.Exp, scale=-1.0).then_inc(edf_ready, 1)
            for i, (f0, n) in enumerate(FCH):
                act.wait_ge(gu_ready, i + 1)
                if i >= 2:
                    act.wait_ge(gu_used, i - 1)
                act.activation(sig[0:n, (i % 2) * T:(i % 2) * T + T], gu_bank(banks, i)[0:n, 0:T], ACT.Exp,
                               scale=-1.0).then_inc(gu_exp, 1)
            act.wait_ge(top_exp_in, 1)
            act.activation(mo[:, 200:201], mo[:, 199:200], ACT.Exp).then_inc(top_exp, 1)

        @block.vector
        def _(dve):
            step = [0]

            def link(ins):
                step[0] += 1
                ins.then_inc(dve_step, 1)
                dve.wait_ge(dve_step, step[0])

            v = dve
            norm = [0]

            def wait_rstd():
                norm[0] += 1
                dve.wait_ge(rstd_ready, norm[0])

            dve.wait_ge(ld_first, 48)
            lo, hi, rng, rc, sca, er = (qs[:, i:i + 1] for i in range(6))
            link(v.tensor_reduce(lo, co_sb[:], AX, ALU.min))
            link(v.tensor_reduce(hi, co_sb[:], AX, ALU.max))
            link(v.tensor_tensor(rng, hi, lo, ALU.subtract))
            link(v.tensor_scalar(rng, rng, 1e-6, None, ALU.add))
            link(v.reciprocal(rc, rng))
            link(v.tensor_scalar(sca, rc, float(2 ** BITS - 1), None, ALU.mult))
            v.tensor_scalar(co_sb[:], co_sb[:], lo, sca, ALU.subtract, ALU.mult).then_inc(scaled_co, 1)

            def ln_stats(src):
                for b in range(B):
                    link(v.bn_stats(bst[0:C, 6 * b:6 * b + 6], src[:, b, :]))
                    v.bn_aggr(mv[0:C, 2 * b:2 * b + 2], bst[0:C, 6 * b:6 * b + 6]).then_inc(
                        var_ready if b == B - 1 else dve_step, 1)
                    if b < B - 1:
                        step[0] += 1
                        dve.wait_ge(dve_step, step[0])

            dve.wait_ge(pads_set, 1)
            ln_stats(x_sb)

            dve.wait_ge(co_turned, 1)
            vq, vf, vg = (qv[:, 24 * i:24 * i + 24] for i in range(3))
            link(v.tensor_copy(vq, z_ps[:, 0:24]))
            link(v.tensor_copy(qvi[:], vq))
            link(v.tensor_copy(vf, qvi[:]))
            link(v.tensor_tensor(vg, vf, vq, ALU.is_gt))
            link(v.tensor_tensor(vf, vf, vg, ALU.subtract))
            link(v.tensor_scalar(vf, vf, 0.0, float(2 ** BITS - 1), ALU.max, ALU.min))
            for c in range(3):
                for o in range(2):
                    d = c if c == 2 else c ^ o
                    link(v.tensor_copy(view(kx, 0, P, 32 * c + 8 * o, [[16, 2], [4, B], [1, NK]]),
                                       view(qv, 0, P, 24 + d, [[0, 2], [3, B], [6, NK]])))

            X = [kx[:, 32 * c + 16:32 * c + 32] for c in range(3)]
            ma, mb, mc = (kt[:, 32 * i:32 * i + 16] for i in range(3))

            def bit_mask(dst, src, b):
                link(v.tensor_scalar(dst, src, 31 - b, 31, ALU.logical_shift_left, ALU.arith_shift_right))

            for b in range(BITS - 1, 0, -1):
                low = (1 << b) - 1
                bit_mask(ma, X[0], b)
                link(v.scalar_tensor_tensor(X[0], ma, low, X[0], ALU.bitwise_and, ALU.bitwise_xor))
                for c in (1, 2):
                    bit_mask(ma, X[c], b)
                    link(v.tensor_tensor(mb, X[0], X[c], ALU.bitwise_xor))
                    link(v.tensor_tensor(mb, mb, ma, ALU.bitwise_or))
                    link(v.scalar_tensor_tensor(X[0], mb, low, X[0], ALU.bitwise_and, ALU.bitwise_xor))
                    link(v.tensor_tensor(mb, mb, ma, ALU.bitwise_xor))
                    link(v.scalar_tensor_tensor(X[c], mb, low, X[c], ALU.bitwise_and, ALU.bitwise_xor))
            link(v.tensor_tensor(X[1], X[1], X[0], ALU.bitwise_xor))
            link(v.tensor_tensor(X[2], X[2], X[1], ALU.bitwise_xor))
            link(v.tensor_scalar(ma, X[2], 1, None, ALU.logical_shift_right))
            for sh in (1, 2, 4, 8):
                link(v.scalar_tensor_tensor(mb, ma, sh, ma, ALU.logical_shift_right, ALU.bitwise_xor))
                ma, mb = mb, ma
            for c in range(3):
                link(v.tensor_tensor(X[c], X[c], ma, ALU.bitwise_xor))
            ka, kb = kx, kt[:, 96:192]
            for sh, mask in ((16, 0x030000FF), (8, 0x0300F00F), (4, 0x030C30C3), (2, 0x09249249)):
                link(v.scalar_tensor_tensor(kb, ka, sh, ka, ALU.logical_shift_left, ALU.bitwise_or))
                link(v.tensor_scalar(ka, kb, mask, None, ALU.bitwise_and))
            key, ky2 = kt[:, 0:32], kt[:, 32:64]
            link(v.scalar_tensor_tensor(ky2, kx[:, 0:32], 1, kx[:, 32:64], ALU.logical_shift_left, ALU.bitwise_or))
            link(v.scalar_tensor_tensor(key, ky2, 1, kx[:, 64:96], ALU.logical_shift_left, ALU.bitwise_or))
            dve.wait_ge(ld_const, 16)
            low14 = kt[:, 64:96]
            link(v.tensor_scalar(low14, key, 0x3FFF, 9, ALU.bitwise_and, ALU.logical_shift_left))
            link(v.tensor_tensor(low14, low14, const("point").bitcast(I32), ALU.bitwise_or))
            digs = [(low14, 0, 255), (low14, 8, 255), (low14, 16, 127), (key, 14, 255), (key, 22, 255)]
            for i, (src, sh, mask) in enumerate(digs):
                link(v.tensor_scalar(kt[:, 96 + 32 * i:128 + 32 * i], src, sh, mask,
                                     ALU.logical_shift_right, ALU.bitwise_and))
            for i in range(5):
                ins = v.tensor_copy(view(dg, 0, P, 8 * i, [[1, M], [4, B], [40, NK]]),
                                    view(kt, 0, P, 96 + 32 * i, [[8, M], [4, B], [1, NK]]))
                if i < 4:
                    link(ins)
            ins.then_inc(digits_ready, 1)

            dve.wait_ge(digits_turned, 1)
            dve.wait_ge(pads_set, 4)
            link(v.tensor_copy(rhs2[0:40, :], z_ps[0:40, :]))
            link(v.tensor_scalar(rhs2[64:128, :], rhs2[64:128, :], 1.0, None, ALU.add))
            link(v.tensor_copy(src2[64:104, :], z_ps[0:40, :]))
            link(v.tensor_scalar(src2[0:40, :], src2[0:40, :], 1.0, None, ALU.add))
            sw0 = CONST_AT["digit_w"][0]
            for i in range(16):
                v.tensor_scalar(lw[:, i * N:(i + 1) * N], src2, cst[:, sw0 + i:sw0 + i + 1], None, ALU.mult)\
                 .then_inc(weights_ready, 1)

            def ln_apply(dst, src):
                wait_rstd()
                for b in range(B):
                    yield v.tensor_scalar(dst[:, b, :], src[:, b, :], mv[0:C, 2 * b:2 * b + 1],
                                          mv[0:C, 2 * b + 1:2 * b + 2], ALU.subtract, ALU.mult)

            for ins in ln_apply(ft[0], x_sb):
                ins.then_inc(ft_ready, 1)

            for i in range(16):
                dve.wait_ge(diff_ready, 2 * i + 2)
                if i >= 2:
                    dve.wait_ge(counted_d, i - 1)
                v.tensor_scalar(junk[2 + i % 2], banks[(2 * i + 1) % 8], 0.0, 0.0, ALU.is_lt, ALU.add,
                                accum_out=rk[:, 2 * i + 1:2 * i + 2]).then_inc(counted_d, 1)
            dve.wait_ge(counted_a, 16)
            dve.wait_ge(counted_d, 16)
            link(v.tensor_scalar(view(rk, 0, P, 0, [[2, 16]]), sg[:], -0.5, (N - 1) / 2, ALU.mult, ALU.add))
            for b in range(B):
                for m in range(M):
                    for k in range(NK):
                        i = (b * M + m) * NK + k
                        at = ((b * NK + k) * M + m) * N
                        v.tensor_scalar(oh[:, at:at + N], iota16[:], rk[:, i:i + 1], None, ALU.is_equal)\
                         .then_inc(onehot_ready, 1)

            def split_features(lb):
                dve.wait_ge(ft_turned, lb + 1)
                if lb >= 1:
                    dve.wait_ge(sorted_ready, lb)
                src = z_ps[:, 0:P]
                part = [fpartb[:, i * P:(i + 1) * P] for i in range(3)]
                rest = [fparts[:, i * P:(i + 1) * P] for i in range(2)]
                link(v.tensor_copy(part[0], src))
                link(v.tensor_tensor(rest[0], src, part[0], ALU.subtract))
                link(v.tensor_copy(part[1], rest[0]))
                link(v.tensor_tensor(rest[1], rest[0], part[1], ALU.subtract))
                link(v.tensor_copy(part[2], rest[1]))
                for i in range(3):
                    for m in range(M):
                        ins = v.tensor_copy(view(fz, 0, P, i * NK * M * P + m * (P + 1), [[M * P, NK], [M, C]]),
                                            view(fpartb, 0, P, i * P, [[C, NK], [1, C]]))
                        ins.then_inc(fz_ready, 1)

            def front(g):
                dve.wait_ge(q_ready, g + 1)
                if g >= 2:
                    dve.wait_ge(s_ready, g - 1)
                o = (g % 2) * COLS
                d = (g % 2) * BLOCKS * P
                for src, so, dst in ((qc, o, qbd), (qt, 0, qtbd)):
                    if src is qt:
                        if g >= 1:
                            dve.wait_ge(bd_ready, 8 * g)
                        link(v.transpose(qt[:], qc[:, o:o + COLS]))
                        if g >= 2:
                            dve.wait_ge(av_ready, 3 * (g - 1))
                    for h in range(4):
                        ins = v.tensor_copy(view(dst, 32 * h, 32, d + 32 * h, [[P, BLOCKS], [1, SLOT]]),
                                            view(src, 32 * h, 32, so, [[SLOT, BLOCKS], [1, SLOT]]))
                        ins.then_inc(bd_ready, 1)

            def compact(g):
                dve.wait_ge(s_ready, g + 1)
                if g >= 1:
                    dve.wait_ge(exp_ready, g)
                    dve.wait_ge(md_ready, g)
                m0 = CONST_AT["own"][0]
                flat = view(sc, 0, P, 0, [[K, BLOCKS], [1, K]])
                link(v.tensor_scalar(flat, view(s_ps, 0, P, 0, [[SLOT, BLOCKS], [1, K]]), cst[:, m0:m0 + 1], None,
                                     ALU.mult))
                for j in (1, 2):
                    link(v.scalar_tensor_tensor(flat, view(s_ps, 0, P, j * K, [[SLOT, BLOCKS], [1, K]]),
                                                cst[:, m0 + j:m0 + j + 1], flat, ALU.mult, ALU.add))
                v.tensor_reduce(mx[:], flat, AX, ALU.max).then_inc(max_ready, 1)

            def subtract(g):
                dve.wait_ge(mt_ready, g + 1)
                v.tensor_tensor(sc[:], sc[:], mt_ps[:, 0:NC], ALU.add).then_inc(sub_ready, 1)

            def normalise(g):
                dve.wait_ge(sum_ready, g + 1)
                if g >= 1:
                    dve.wait_ge(probs_ready, g)
                e = (g % 2) * NC
                link(v.reciprocal(ri[:], r_ps[:, 0:NC]))
                link(v.tensor_tensor(pn[:], ri[:], ex[:, e:e + NC], ALU.mult))
                link(v.tensor_copy(ph[:, 0:NC], pn[:]))
                link(v.tensor_tensor(ph[:, NC:2 * NC], pn[:], ph[:, 0:NC], ALU.subtract))
                m0 = CONST_AT["own"][0]
                if g >= 2:
                    dve.wait_ge(av_ready, 3 * (g - 1))
                for j in range(3):
                    ins = v.tensor_scalar(view(px, 0, P, (g % 2) * 2 * COLS + j * K, [[SLOT, 2 * BLOCKS], [1, K]]),
                                          view(ph, 0, P, 0, [[K, 2 * BLOCKS], [1, K]]),
                                          cst[:, m0 + j:m0 + j + 1], None, ALU.mult)
                    if j < 2:
                        link(ins)
                ins.then_inc(probs_ready, 1)

            def stats_chain(lb):
                l = lb // B
                nst = 4 if l == 0 else 7
                link(v.bn_aggr(mv[:, 0:2], bst[:, 0:6 * nst]))
                v.tensor_copy(mv[:, 2:3], mv[:, 0:1]).then_inc(stat_in, 1)
                dve.wait_ge(stat_mean, 2 * lb + 1)
                link(v.tensor_copy(mv[:, 4:5], z_ps[:, 0:1]))
                link(v.tensor_tensor(mv[:, 5:6], mv[:, 0:1], mv[:, 4:5], ALU.subtract))
                link(v.scalar_tensor_tensor(mv[:, 6:7], mv[:, 5:6], mv[:, 5:6], mv[:, 1:2], ALU.mult, ALU.add))
                v.tensor_copy(mv[:, 2:3], mv[:, 6:7]).then_inc(stat_in, 1)
                dve.wait_ge(stat_mean, 2 * lb + 2)
                link(v.tensor_tensor(mv[:, 4:5], mv[:, 4:5], bv_sb[:, l:l + 1], ALU.add))
                v.tensor_copy(mv[:, 3:4], z_ps[:, 0:1]).then_inc(var_ready, 1)

            def tail(lb):
                l, b = divmod(lb, B)
                dve.wait_ge(ft_ready, 2 + lb)
                halves = 1 if l == 0 else 2
                i = PASSES_BEFORE[lb]
                st = 0
                for half in range(halves):
                    for j, (t0, n) in enumerate(THIRDS):
                        i += 1
                        dve.wait_ge(h_ready, i)
                        link(v.tensor_reduce(hm[:, half * PTS + PB * t0:half * PTS + PB * (t0 + n)],
                                             view(z_ps, 0, P, 0, [[K, PB * n], [1, K]]), AX, ALU.max))
                        full = half == halves - 1 and j == 2
                        cols = (PTS_LAST - PB * t0) * K if full else n * PB * K
                        ins = v.bn_stats(bst[:, 6 * st:6 * st + 6], z_ps[:, 0:cols])
                        st += 1
                        if full:
                            link(ins)
                            whole = P - P // (PIECES if l == 0 else 2)
                            ins = v.bn_stats(bst[0:whole, 6 * st:6 * st + 6], z_ps[0:whole, cols:n * PB * K])
                            st += 1
                        ins.then_inc(h_used, 1)
                dve.wait_ge(h_used, PASSES_BEFORE[lb + 1])
                stats_chain(lb)
                w = halves * PTS
                link(v.tensor_scalar(hm[:, 0:w], hm[:, 0:w], bv_sb[:, l:l + 1], None, ALU.add))
                wait_rstd()
                link(v.tensor_scalar(hn[:, 0:w], hm[:, 0:w], mv[:, 4:5], mv[:, 3:4], ALU.subtract, ALU.mult))
                oc = OUT_CH[l]
                for q in range(PIECES):
                    p0 = 32 * q if l == 0 else 64 * (q % 2)
                    o = 0 if l == 0 else (q // 2) * PTS
                    n = PTS if q < PIECES - 1 else PTS_LAST
                    src = hn[p0:p0 + oc, o:o + n]
                    ins = v.scalar_tensor_tensor(ft[l + 1][:, b, q * PTS:q * PTS + n], src, 0.2, src,
                                                 ALU.mult, ALU.max)
                    if q < PIECES - 1:
                        link(ins)
                ins.then_inc(ft_ready, 1)

            dve.wait_ge(pads_set, 11)
            for l in range(2):
                dve.wait_ge(fold_ready, l + 1)
                for s_ in range(2):
                    link(v.tensor_copy(wn_sb[:, l, s_, 0:OUT_CH[l]], z_ps[:, s_ * 64:s_ * 64 + OUT_CH[l]]))
                v.tensor_copy(bv_sb[:, l:l + 1], z_ps[:, 128:129]).then_inc(fold_used, 1)
            split_features(0)
            split_features(1)
            for t in range(STEPS + 3):
                if 2 <= t < STEPS + 2:
                    normalise(t - 2)
                if 1 <= t <= STEPS:
                    compact(t - 1)
                if t in TAIL_AT:
                    tail(TAIL_AT.index(t))
                    if t in TAIL_AT[:2]:
                        split_features(2 + TAIL_AT.index(t))
                if t < STEPS:
                    front(t)
                if 1 <= t <= STEPS:
                    subtract(t - 1)

            def row_stats(src):
                ln_stats(src)

            dve.wait_ge(h3_ready, 1)
            for b in range(B):
                link(v.tensor_copy(h3[:, b, :], banks[b][0:C, :]))
            ln_stats(h3)
            for ins in ln_apply(h3, h3):
                link(ins)
            for b in range(B):
                link(v.scalar_tensor_tensor(h3[:, b, :], h3[:, b, :], 0.2, h3[:, b, :], ALU.mult, ALU.max))
                link(v.tensor_tensor(x1[:, b, :], x_sb[:, b, :], h3[:, b, :], ALU.add))
            ln_stats(x1)
            for ins in ln_apply(h3, x1):
                ins.then_inc(xn_ready, 1)
            for b in range(B):
                link(v.tensor_copy(xr[C * b:C * b + C, :], x1[:, b, :]))
            dve.wait_ge(xn_turned, 1)
            v.tensor_copy(xnT, view(o_ps, 0, P, 0, [[T, NK], [1, T]])).then_inc(xnT_ready, 1)

            dve.wait_ge(gp_ready, 1)
            dve.wait_ge(edf_ready, 1)
            col = [gp[:, i * T:(i + 1) * T] for i in range(12)]
            up, delta, power, keep, tmp = col[0], col[1], col[2], col[3], col[4:4 + G]
            link(v.tensor_copy(up, banks[0][:, 0:T]))
            link(v.tensor_scalar(delta, banks[1][:, 0:T], local_sb[:, 0:1], None, ALU.subtract))
            link(v.scalar_tensor_tensor(keep, delta, -2.5, up, ALU.is_ge, ALU.mult))
            link(v.scalar_tensor_tensor(keep, delta, 2.5, keep, ALU.is_le, ALU.mult))
            link(v.tensor_copy(power, delta))
            for m in range(G):
                if m:
                    link(v.tensor_tensor(power, power, delta, ALU.mult))
                ins = v.scalar_tensor_tensor(tmp[m], power, edf[:, m:m + 1], up if m < 4 else keep,
                                             ALU.mult, ALU.mult)
                if m < G - 1:
                    link(ins)
            ins.then_inc(tmp_ready, 1)
            for i, (f0, n) in enumerate(FCH):
                bank = gu_bank(banks, i)
                dve.wait_ge(gu_exp, i + 1)
                s_ = sig[0:n, (i % 2) * T:(i % 2) * T + T]
                link(v.tensor_scalar(s_, s_, 1.0, None, ALU.add))
                link(v.reciprocal(s_, s_))
                link(v.tensor_tensor(s_, bank[0:n, 0:T], s_, ALU.mult))
                v.tensor_tensor(actT[0:n, i, :], bank[0:n, 256:256 + T], s_, ALU.mult).then_inc(gu_used, 1)
            dve.wait_ge(y_ready, 1)
            link(v.tensor_tensor(x2, z_ps[0:T, :], xr, ALU.add))
            link(v.bn_stats(rst[:, 4:10], x2))
            v.bn_aggr(rst[:, 0:2], rst[:, 4:10]).then_inc(var_ready, 1)
            wait_rstd()
            v.tensor_scalar(xn2, x2, rst[:, 0:1], rst[:, 1:2], ALU.subtract, ALU.mult).then_inc(xn2_ready, 1)
            dve.wait_ge(xn2_turned, 1)
            v.tensor_copy(xnT, view(o_ps, 0, P, 0, [[T, NK], [1, T]])).then_inc(xn2T_ready, 1)

            dve.wait_ge(moe_h, 1)
            h = mo[:, 0:32]
            g_b1, gam, bet, g_b2, rev = (rowc_sb[:, a:a + w] for a, w in ((0, 32), (32, 32), (64, 32), (96, E), (96 + E, E)))
            link(v.tensor_tensor(h, banks[0][0:T, E * R:E * R + 32], g_b1, ALU.add))
            link(v.bn_stats(rst[:, 4:10], h))
            v.bn_aggr(rst[:, 2:4], rst[:, 4:10]).then_inc(var_ready, 1)
            wait_rstd()
            link(v.tensor_scalar(h, h, rst[:, 2:3], rst[:, 3:4], ALU.subtract, ALU.mult))
            link(v.tensor_tensor(h, h, gam, ALU.mult))
            link(v.tensor_tensor(h, h, bet, ALU.add))
            v.tensor_scalar(h, h, 0.0, None, ALU.max).then_inc(moe_relu, 1)
            dve.wait_ge(moe_relu_turned, 1)
            v.tensor_copy(hT, banks[1][0:32, 0:T]).then_inc(moe_hT, 1)
            dve.wait_ge(moe_gates, 1)
            gt = mo[:, 32:40]
            top = mo[:, 40:48]
            link(v.tensor_tensor(gt, banks[2][0:T, 0:E], g_b2, ALU.add))
            link(v.max(top, gt))
            eq, pk, one = mo[:, 48:56], mo[:, 56:64], mo[:, 64:80]
            free = mo[:, 96:104]
            for k in range(2):
                link(v.tensor_scalar(eq, gt, top[:, k:k + 1], None, ALU.is_equal))
                if k == 1:
                    link(v.tensor_tensor(eq, eq, free, ALU.mult))
                link(v.tensor_tensor(pk, eq, rev, ALU.mult))
                link(v.tensor_reduce(mo[:, 80 + k:81 + k], pk, AX, ALU.max))
                link(v.tensor_scalar(one[:, 8 * k:8 * k + 8], rev, mo[:, 80 + k:81 + k], None, ALU.is_equal))
                if k == 0:
                    link(v.tensor_scalar(free, one[:, 0:8], -1.0, 1.0, ALU.mult, ALU.add))
            v.tensor_copy(mo[:, 110:126], one).then_inc(picks_ready, 1)
            v.tensor_tensor(mo[:, 199:200], top[:, 1:2], top[:, 0:1], ALU.subtract).then_inc(top_exp_in, 1)
            dve.wait_ge(top_exp, 1)
            link(v.tensor_scalar(mo[:, 201:202], mo[:, 200:201], 1.0, None, ALU.add))
            link(v.reciprocal(mo[:, 202:203], mo[:, 201:202]))
            link(v.tensor_tensor(mo[:, 203:204], mo[:, 202:203], mo[:, 200:201], ALU.mult))
            dve.wait_ge(counts_ready, 1)
            allow = mo[:, 130:146]
            link(v.tensor_scalar(allow, banks[3][0:T, 0:16], float(CAP), 1.0 / R, ALU.is_le, ALU.mult))
            link(v.tensor_tensor(allow, allow, one, ALU.mult))
            link(v.tensor_scalar(allow[:, 0:8], allow[:, 0:8], mo[:, 202:203], None, ALU.mult))
            link(v.scalar_tensor_tensor(allow[:, 0:8], allow[:, 8:16], mo[:, 203:204], allow[:, 0:8],
                                        ALU.mult, ALU.add))
            v.tensor_tensor(view(mo, 0, T, 256, [[R, E], [1, R]]), view(s_ps, 0, T, 0, [[R, E], [1, R]]),
                            view(mo, 0, T, 130, [[1, E], [0, R]]), ALU.mult).then_inc(lora_ready, 1)
            dve.wait_ge(lora_turned, 1)
            v.tensor_copy(tT, banks[1][:, 128:128 + T]).then_inc(lora_T, 1)
            dve.wait_ge(moe_out, 1)
            v.tensor_tensor(xn2, z_ps[0:T, :], x2, ALU.add).then_inc(y_out, 1)

        @block.tensor
        def _(pe):
            mm = pe.matmul
            pe.wait_ge(ld_first, 48)
            pe.wait_ge(scaled_co, 1)
            for k in range(NK):
                last = pe.transpose(z_ps[:, 6 * k:6 * k + 6], co_sb[:, k * P:(k + 1) * P], id_sb[0:6, 0:6])
            last.then_inc(co_turned, 1)
            pe.wait_ge(digits_ready, 1)
            for k in range(NK):
                last = pe.transpose(z_ps[0:40, k * P:(k + 1) * P], dg[:, 40 * k:40 * k + 40], id_sb[:, :])
            last.then_inc(digits_turned, 1)
            pe.wait_ge(weights_ready, 16)
            for i in range(32):
                bm, k = divmod(i, NK)
                if i >= 8:
                    if i % 2 == 0:
                        pe.wait_ge(counted_a, (i - 8) // 2 + 1)
                    else:
                        pe.wait_ge(counted_d, (i - 8) // 2 + 1)
                for part in range(2):
                    at = (part * 8 + bm) * N + k * P
                    last = mm(banks[i % 8], lw[:, at:at + P], rhs2, start=part == 0, stop=part == 1)
                last.then_inc(diff_ready, 1)
            pe.wait_ge(counted_a, 16)
            pe.wait_ge(counted_d, 16)
            pe.wait_ge(ld_graph, 64)
            for l in range(2):
                if l:
                    pe.wait_ge(fold_used, 1)
                oc = OUT_CH[l]
                for s_ in range(2):
                    mm(z_ps[:, s_ * 64:s_ * 64 + oc], wlin_sb[:, l, s_ * P:(s_ + 1) * P], wconv_sb[:, l, 0:oc],
                       start=True, stop=True)
                last = mm(z_ps[:, 128:129], wconv_sb[:, l, :], blin_sb[:, l:l + 1], start=True, stop=True)
                last.then_inc(fold_ready, 1)
            pe.wait_ge(fold_used, 2)

            def features(lb):
                l, b = divmod(lb, B)
                src = ft[l]
                pe.wait_ge(ft_ready, lb + 1)
                if lb == 1:
                    pe.wait_ge(fs_ready, 2)
                for k in range(NK):
                    last = pe.transpose(z_ps[:, k * C:(k + 1) * C], src[:, b, k * P:(k + 1) * P], id_sb[0:C, 0:C])
                last.then_inc(ft_turned, 1)
                pe.wait_ge(fz_ready, 12 * (lb + 1))
                rep = const("rep")[0:C, :]
                mm(z_ps[:, :], rep, src[:, b, :], start=True, stop=True).then_inc(rep_ready, 1)
                pe.wait_ge(rep_used, lb + 1)
                if lb < 2:
                    pe.wait_ge(onehot_ready, 16 * (b + 1))
                n = 0
                for k in range(NK):
                    for m in range(M):
                        method = PERMS[l][m]
                        for part in range(3):
                            z = part * NK * M * P + (k * M + m) * P
                            o = ((b * NK + k) * M + method) * N
                            last = mm(z_ps[:, :], fz[:, z:z + P], oh[:, o:o + N], start=n == 0, stop=n == 47)
                            n += 1
                last.then_inc(sorted_ready, 1)

            def scores(g):
                pe.wait_ge(bd_ready, 8 * g + 4)
                if g >= 1:
                    pe.wait_ge(max_ready, g)
                d, o = (g % 2) * BLOCKS * P, (g % 2) * COLS
                for t in range(BLOCKS):
                    last = mm(s_ps[:, t * SLOT:t * SLOT + PB * K], qbd[:, d + t * P:d + (t + 1) * P],
                              qc[:, o + t * SLOT:o + t * SLOT + PB * K], start=True, stop=True)
                last.then_inc(s_ready, 1)

            def row_max(g):
                pe.wait_ge(md_ready, g + 1)
                if g >= 1:
                    pe.wait_ge(sub_ready, g)
                mm(mt_ps[:, 0:NC], negones, md[:], start=True, stop=True).then_inc(mt_ready, 1)

            def row_sum(g):
                pe.wait_ge(exp_ready, g + 1)
                if g >= 1:
                    pe.wait_ge(probs_ready, g)
                e = (g % 2) * NC
                mm(r_ps[:, 0:NC], posones, ex[:, e:e + NC], start=True, stop=True).then_inc(sum_ready, 1)

            def attend(g):
                pe.wait_ge(probs_ready, g + 1)
                pe.wait_ge(bd_ready, 8 * (g + 1))
                d = (g % 2) * BLOCKS * P
                for j, (t0, n) in enumerate(THIRDS):
                    i = 3 * g + j
                    if i >= 2:
                        pe.wait_ge(ot_ready, i - 1)
                    for t in range(n):
                        w = qtbd[:, d + (t0 + t) * P:d + (t0 + t + 1) * P]
                        o = o_ps[:, (i % 2) * 512 + t * SLOT:(i % 2) * 512 + t * SLOT + PB * K]
                        for part in range(2):
                            a = (g % 2) * 2 * COLS + part * COLS + (t0 + t) * SLOT
                            last = mm(o, w, px[:, a:a + PB * K], start=part == 0, stop=part == 1)
                    last.then_inc(av_ready, 1)

            def project(lb):
                l, b = divmod(lb, B)
                oc = OUT_CH[l]
                side = P // oc
                i = PASSES_BEFORE[lb]
                pe.wait_ge(ot_ready, 12 * (lb + 1))
                pe.wait_ge(ft_ready, 2 + lb)
                pe.wait_ge(fs_ready, min(2 * (lb + 2), 8))
                for half in range(PIECES // side):
                    for t0, n in THIRDS:
                        if i > PASSES_BEFORE[lb]:
                            pe.wait_ge(h_used, i)
                        for s_ in range(side):
                            q = half * side + s_
                            dst = z_ps[oc * s_:oc * s_ + oc, 0:n * PB * K]
                            mm(dst, wn_sb[:, l, 0, 0:oc],
                               view(f16f, 0, P, b * PIECES * PTS + q * PTS + PB * t0, [[1, PB * n], [0, K]]),
                               start=True, stop=False)
                            a = (q * BLOCKS + t0) * PB * K
                            last = mm(dst, wn_sb[:, l, 1, 0:oc], ot[:, a:a + n * PB * K], start=False, stop=True)
                        last.then_inc(h_ready, 1)
                        i += 1

            def average(lb):
                l = lb // B
                for r in range(2):
                    pe.wait_ge(stat_in, 2 * lb + r + 1)
                    mm(z_ps[:, 0:1], const(f"mean{l}"), mv[:, 2:3], start=True, stop=True).then_inc(stat_mean, 1)

            features(0)
            features(1)
            for t in range(STEPS + 3):
                if t in TAIL_AT:
                    project(TAIL_AT.index(t))
                if 2 <= t < STEPS + 2:
                    attend(t - 2)
                if 1 <= t <= STEPS:
                    row_max(t - 1)
                if t in TAIL_AT:
                    average(TAIL_AT.index(t))
                if t in TAIL_AT[:2]:
                    features(2 + TAIL_AT.index(t))
                if t < STEPS:
                    scores(t)
                if 1 <= t <= STEPS:
                    row_sum(t - 1)

            pe.wait_ge(ft_ready, 6)
            for b in range(B):
                for j in range(3):
                    kk = 64 if j == 2 else 32
                    last = mm(banks[b][0:C, :], wc3_sb[0:kk, j, :], ft[j][0:kk, b, :], start=j == 0, stop=j == 2)
            last.then_inc(h3_ready, 1)
            pe.wait_ge(xn_ready, 2)
            for b in range(B):
                for k in range(NK):
                    last = pe.transpose(o_ps[:, k * T + b * C:k * T + b * C + C], h3[:, b, k * P:(k + 1) * P],
                                        id_sb[0:C, 0:C])
            last.then_inc(xn_turned, 1)
            pe.wait_ge(xnT_ready, 1)
            pe.wait_ge(ld_ffn, 80)
            for j in range(2):
                for k in range(NK):
                    last = mm(banks[j][:, 0:T], upgate_sb[:, k, j * S:(j + 1) * S], xnT[:, k, :],
                              start=k == 0, stop=k == NK - 1)
            last.then_inc(gp_ready, 1)
            pe.wait_ge(ld_up, 16)
            for i, (f0, n) in enumerate(FCH):
                bank = gu_bank(banks, i)
                if i >= 3:
                    pe.wait_ge(gu_used, i - 2)
                for j in range(2):
                    for k in range(NK):
                        w = gate_sb[:, k, f0:f0 + n] if j == 0 else up_sb[:, k * F + f0:k * F + f0 + n]
                        last = mm(bank[0:n, 256 * j:256 * j + T], w,
                                  xnT[:, k, :], start=k == 0, stop=k == NK - 1)
                last.then_inc(gu_ready, 1)
            pe.wait_ge(tmp_ready, 1)
            pe.wait_ge(ld_fuse, 32)
            for m in range(G + 1):
                w = fuse_sb[:, m * N:(m + 1) * N]
                lhs = gp[:, 0:T] if m == 0 else gp[:, (3 + m) * T:(4 + m) * T]
                mm(z_ps[0:T, :], lhs, w, start=m == 0, stop=False)
            pe.wait_ge(ld_late, 64)
            for i, (f0, n) in enumerate(FCH):
                pe.wait_ge(gu_used, i + 1)
                last = mm(z_ps[0:T, :], actT[0:n, i, :], ffn2_sb[0:n, i * N:(i + 1) * N],
                          start=False, stop=i == NF - 1)
            last.then_inc(y_ready, 1)
            pe.wait_ge(xn2_ready, 1)
            for k in range(NK):
                last = pe.transpose(o_ps[:, k * T:(k + 1) * T], xn2[:, k * P:(k + 1) * P], id_sb[0:T, 0:T])
            last.then_inc(xn2_turned, 1)
            pe.wait_ge(xn2T_ready, 1)
            for k in range(NK):
                last = mm(banks[0][0:T, 0:E * R + 32], xnT[:, k, :], moe1_sb[:, k * moe1_w:(k + 1) * moe1_w], start=k == 0, stop=k == NK - 1)
            last.then_inc(moe_h, 1)
            for k in range(NK):
                mm(z_ps[0:T, :], xnT[:, k, :], moe2_sb[:, k * N:(k + 1) * N], start=k == 0, stop=False)
            pe.wait_ge(moe_relu, 1)
            pe.transpose(banks[1][0:32, 0:T], mo[:, 0:32], id_sb[0:T, 0:T]).then_inc(moe_relu_turned, 1)
            pe.wait_ge(moe_hT, 1)
            mm(banks[2][0:T, 0:E], hT, gw2_sb[:], start=True, stop=True).then_inc(moe_gates, 1)
            pe.wait_ge(picks_ready, 1)
            mm(banks[3][0:T, 0:16], const("ones")[0:T, 0:T], mo[:, 110:126], start=True, stop=True)\
                .then_inc(counts_ready, 1)
            pe.wait_ge(lora_ready, 1)
            pe.transpose(banks[1][:, 128:128 + T], mo[:, 256:256 + P], id_sb[0:T, 0:T]).then_inc(lora_turned, 1)
            pe.wait_ge(lora_T, 1)
            mm(z_ps[0:T, :], tT, moe3_sb, start=False, stop=True).then_inc(moe_out, 1)


def constants():
    import numpy as np
    p = np.arange(P)
    slot = p % SLOT
    point, o10 = slot // K, slot % K
    head = p // SLOT
    c = {}
    c["own"] = (point[:, None] == np.arange(PB)[None]).astype(np.float32)
    c["i10"] = (o10[:, None] == np.arange(K)[None]).astype(np.float32)
    same = (head[:, None] == head[None]) & (point[:, None] == point[None])
    c["posblk"] = same.astype(np.float32)
    c["negblk"] = -c["posblk"]
    c["eps"] = np.full((P, 1), EPS, np.float32)
    c["nhalf"] = np.full((P, 1), -0.5, np.float32)
    n = np.zeros((P, M, B, NK), np.int32)
    n[:] = p[:, None, None, None] + P * np.arange(NK)
    c["point"] = n.reshape(P, 32).view(np.float32)
    w = np.zeros((P, 2, B * M), np.float32)
    for bm in range(B * M):
        for digit, (part, value) in enumerate(((1, 1.0), (1, 256.0), (1, 65536.0), (0, 2.0 ** 23), (0, 2.0 ** 31))):
            w[8 * digit + bm, part, bm] = value
            w[64 + 8 * digit + bm, part, bm] = -value
    c["digit_w"] = w.reshape(P, 16)
    rep = np.zeros((P, P), np.float32)
    rep[p // M, p] = 1.0
    c["rep"] = rep
    for l in range(2):
        oc = OUT_CH[l]
        side = P // oc
        size = np.zeros(side)
        for q in range(PIECES):
            size[q % side] += PTS if q < PIECES - 1 else PTS_LAST
        c[f"mean{l}"] = ((p[:, None] % oc == p[None] % oc) * (size[p // oc] / N)[:, None]).astype(np.float32)
    c["ones"] = np.ones((P, P), np.float32)
    return np.ascontiguousarray(np.concatenate([c[name] for name, _ in CONST_WIDTHS], axis=1))


def kernel(**inputs):
    import numpy as np
    import concourse.bacc as bacc
    from concourse.bass_utils import run_bass_kernel_spmd as run

    a = {k: np.asarray(v) for k, v in inputs.items()}

    def chunks(w):
        return w.reshape(-1, P, w.shape[1]).transpose(1, 0, 2).reshape(P, -1)

    def rows(v):
        return np.broadcast_to(v, (T, v.shape[0]))

    wc3 = np.zeros((64, 3, C), np.float32)
    w3 = a["L0_xattn_W_conv3"].T
    wc3[0:32, 0], wc3[0:32, 1], wc3[:, 2] = w3[0:32], w3[32:64], w3[64:128]
    wd = a["L0_attn_ffn_down_w"].T
    whole = (NF - 1) * P
    lora_a = a["L0_ffn_lora_A"].transpose(1, 0, 2).reshape(N, E * R)
    df = a["L0_attn_discount_factor"]
    laid = {
        "x": a["x"].transpose(1, 0, 2),
        "coords": a["ctx_4096"][:, 0:3, :].reshape(6, N),
        "consts": constants(),
        "ident": np.eye(P, dtype=np.float32),
        "wlin": np.stack([a["L0_xattn_W_lin1"], a["L0_xattn_W_lin2"]], axis=1),
        "wconv": np.stack([np.tile(a["L0_xattn_W_conv1"].T, (1, 4)), np.tile(a["L0_xattn_W_conv2"].T, (1, 2))], axis=1),
        "blin": np.stack([a["L0_xattn_b_lin1"], a["L0_xattn_b_lin2"]], axis=1),
        "wc3": wc3,
        "upgate": chunks(np.concatenate([a["L0_attn_up_w"].T, a["L0_attn_gate_w"].T], axis=1)).reshape(P, NK, 2 * S),
        "local": np.concatenate([a["L0_attn_local_point"][:, None], np.broadcast_to(df, (P, G))], axis=1),
        "fuse": np.concatenate([a["L0_attn_local_approx_output"].T[:, None],
                                a["L0_attn_fuse_weight"].transpose(1, 2, 0)], axis=1).reshape(P, (G + 1) * N),
        "gate": chunks(a["L0_attn_ffn_gate_w"].T).reshape(P, NK, F),
        "up": chunks(a["L0_attn_ffn_up_w"].T),
        "ffn2a": chunks(wd[:whole]),
        "ffn2b": wd[whole:],
        "moe1": chunks(np.concatenate([lora_a, a["L0_ffn_gw1"].T], axis=1)),
        "moe2": chunks(a["L0_ffn_weight"].T),
        "moe3": a["L0_ffn_lora_B"].reshape(E * R, N),
        "rowc": np.concatenate([rows(a["L0_ffn_gb1"]), rows(a["L0_ffn_ln_gamma"]), rows(a["L0_ffn_ln_beta"]),
                                rows(a["L0_ffn_gb2"]), rows(np.arange(E, 0, -1).astype(np.float32))], axis=1),
        "gw2": a["L0_ffn_gw2"].T,
    }
    nc = bacc.Bacc("TRN2", target_bir_lowering=False, num_devices=1)
    arrays, args = {}, {}
    for name, value in laid.items():
        value = np.ascontiguousarray(value)
        arrays[f"in_{name}"] = value
        args[name] = nc.dram_tensor(f"in_{name}", value.shape, mybir.dt.from_np(value.dtype), kind="ExternalInput").ap()
    out = nc.dram_tensor("out_x", (T, N), F32, kind="ExternalOutput").ap()
    perceiver_layer(nc, out=out, **args)
    result = run(nc, [arrays], core_ids=[0])
    return result.results[0]["out_x"].reshape(B, C, N)
```

```python
import concourse.bass as bass
from concourse import mybir
from contextlib import ExitStack

F32 = mybir.dt.float32
F16 = mybir.dt.float16
BF16 = mybir.dt.bfloat16
I32 = mybir.dt.int32
ALU = mybir.AluOpType
ACT = mybir.ActivationFunctionType
AX = mybir.AxisListType.X

P = 128
B, C, N = 2, 32, 512
K = 10
LEFT = K // 2
M = 4
BITS = 10
NK = N // P
PB = 3
SLOT = 32
BLOCKS = 43
PIECES = 4
PTS = BLOCKS * PB
PTS_LAST = N - (PIECES - 1) * PTS
COLS = BLOCKS * SLOT
NC = BLOCKS * K
STEPS = 2 * B * PIECES
PERMS = ([2, 0, 3, 1], [1, 3, 0, 2])
THIRDS = [(0, 16), (16, 16), (32, 11)]
FSW = LEFT + PIECES * PTS + K
OUT_CH = [C, 2 * C]
LAST_AT = PIECES + 3
RANKS_LATER = [range(0, 6), range(6, 11), range(11, 16)]
TAIL_AT = [PIECES * i + LAST_AT for i in range(2 * B)]

def value_chunks(g):
    first = B * PIECES
    return 3 * min(g, first) + 6 * max(0, g - first)


F = 1248
FCH = [(i * P, min(P, F - i * P)) for i in range((F + P - 1) // P)]
NF = len(FCH)
S = 128
G = 6
E = 8
R = 16
T = B * C
CAP = int(3.0 * T / E)
EPS = 1e-5
CONST_WIDTHS = [("own", PB), ("i10", K), ("negblk", P), ("posblk", P), ("eps", 1), ("nhalf", 1), ("point", 32),
                ("digit_w", 16), ("rep", P), ("mean0", P), ("mean1", P), ("ones", P)]
CONST_AT = {name: (sum(w for _, w in CONST_WIDTHS[:i]), w) for i, (name, w) in enumerate(CONST_WIDTHS)}
CONST_W = sum(w for _, w in CONST_WIDTHS)


def gu_bank(banks, i):
    return banks[(2, 5, 6)[i % 3]]


def perceiver_layer(nc, x, coords, consts, ident, wlin, wconv, blin, wc3, upgate, local, fuse, gate, up, ffn2a, ffn2b,
                    moe1, moe2, moe3, rowc, gw2, out):
    ctx = ExitStack()
    with ctx:
        def sb(name, shape, dt=F32):
            return ctx.enter_context(nc.sbuf_tensor(name, shape, dt))

        def sem(name):
            return ctx.enter_context(nc.semaphore(name))

        def view(t, p0, np_, off, dims):
            base = t[p0:p0 + np_, :]
            return bass.AP(base.tensor, base.offset + off, [list(base.ap[0])] + [list(d) for d in dims])

        cst = sb("cst", [P, CONST_W])

        def const(name):
            a, w = CONST_AT[name]
            return cst[:, a:a + w]

        id_sb = sb("id_sb", [P, P])
        iota16 = sb("iota16", [P, N], F16)
        negones = const("negblk")
        posones = const("posblk")

        x_sb = sb("x_sb", [C, B, N])
        co_sb = sb("co_sb", [6, N])
        wlin_sb = sb("wlin_sb", [64, 2, 256])
        wconv_sb = sb("wconv_sb", [64, 2, 128])
        blin_sb = sb("blin_sb", [64, 2])
        wc3_sb = sb("wc3_sb", [64, 3, C])
        upgate_sb = sb("upgate_sb", [P, NK, 2 * S])
        local_sb = sb("local_sb", [P, 1 + G])
        gate_sb = sb("gate_sb", [P, NK, F])
        rowc_sb = sb("rowc_sb", [T, 3 * 32 + E + E])
        gw2_sb = sb("gw2_sb", [32, E])
        oh = sb("oh", [P, B * NK * M * N], BF16)
        qbd = sb("qbd", [P, 2 * BLOCKS * P], F16)
        vt = sb("vt", [P, 2 * 2 * COLS])
        hs = sb("hs", [P, 2 * PTS * K])
        qc = sb("qc", [P, 3 * COLS], F16)
        wv = sb("wv", [P, 3 * 3 * P], BF16)
        wparts = sb("wparts", [P, 3 * 96], BF16)
        gs = sb("gs", [P, NK * P])
        fs = sb("fs", [P, B * FSW])
        f4 = sb("f4", [P, B * PIECES * PTS])
        f16h = sb("f16h", [P, N], F16)
        f16f = sb("f16f", [P, PIECES * PTS])
        sc = sb("sc", [P, NC])
        mx = sb("mx", [P, BLOCKS])
        md = sb("md", [P, NC])
        ex = sb("ex", [P, 2 * NC])
        ri = sb("ri", [P, NC])
        pn = sb("pn", [P, NC])
        px = sb("px", [P, 2 * COLS])
        hm = sb("hm", [P, 2 * PTS])
        hn = sb("hn", [P, 2 * PTS])
        gc = sb("gc", [P, B * 2 * PTS])
        hb = sb("hb", [P, 2 * PTS])
        hu = sb("hu", [P, 2 * PTS])
        bst = sb("bst", [P, 7 * 6])
        bsm = sb("bsm", [P, 2 * 3 * 6])
        mv = sb("mv", [P, 16])
        wn_sb = sb("wn_sb", [P, 2, 64])
        wnb = sb("wnb", [P, 96])
        bv_sb = sb("bv_sb", [P, 2])
        ft = [sb("ft0", [C, B, N]), sb("ft1", [C, B, N]), sb("ft2", [2 * C, B, N])]
        frest = sb("frest", [P, 2 * P])
        fpartb = sb("fpartb", [P, 3 * P], BF16)
        qv = sb("qv", [P, 3 * 24])
        qvi = sb("qvi", [P, 24], I32)
        rhs2 = sb("rhs2", [P, N], BF16)
        rk = sb("rk", [P, 32])
        sg = sb("sg", [P, 24])
        qs = sb("qs", [6, 8])
        px_halves = px[:, :].bitcast(BF16)
        src2, *junk = (px_halves[:, i * N:(i + 1) * N] for i in range(3))
        junk_sign = [gs[:, 0:256].bitcast(BF16), gs[:, 256:512].bitcast(BF16)]
        kx = px[:, 1536:1632].bitcast(I32)
        kt = px[:, 1632:2016].bitcast(I32)
        dg = px[:, 2016:2016 + NK * 40]
        lw = [t[:, 0:8 * 256].bitcast(BF16) for t in (vt, hs)]

        def laid_over(t, *shapes):
            at, tiles = 0, []
            for parts, *dims in shapes:
                w = 1
                for d in dims:
                    w *= d
                v = t[0:parts, at:at + w]
                tiles.append(v if len(dims) == 1 else v.rearrange("p (a b) -> p a b", a=dims[0]))
                at += w
            return tiles

        moe1_w = E * R + 32
        fuse_sb, moe2_sb, moe3_sb, moe1_sb = laid_over(oh[:, :].bitcast(F32), (P, (G + 1) * N), (P, NK * N), (P, N),
                                                       (P, NK * moe1_w))
        up_sb, = laid_over(qbd[:, :].bitcast(F32), (P, NK * F))
        ffn2_sb, = laid_over(vt, (P, NF * N))
        x1, h3, xr = laid_over(hs, (C, B, N), (C, B, N), (T, N))
        x2, xn2, mo, gp = laid_over(px, (T, N), (T, N), (T, N), (P, 12 * T))
        actT, xnT, sig = laid_over(fs, (P, NF, T), (P, NK, T), (P, 2 * T))
        hT, tT = laid_over(f4, (32, T), (P, T))
        edf = sb("edf", [P, G])
        rst = sb("rst", [T, 16])

        s_ps = ctx.enter_context(nc.psum_tensor("s_ps", [P, 3 * 512], F32))
        v_ps = ctx.enter_context(nc.psum_tensor("v_ps", [P, 2 * 512], F32))
        mt_ps = ctx.enter_context(nc.psum_tensor("mt_ps", [P, 512], F32))
        r_ps = ctx.enter_context(nc.psum_tensor("r_ps", [P, 512], F32))
        z_ps = ctx.enter_context(nc.psum_tensor("z_ps", [P, 512], F32))
        banks = [s_ps[:, 0:512], s_ps[:, 512:1024], s_ps[:, 1024:1536], v_ps[:, 0:512], v_ps[:, 512:1024],
                 mt_ps[:, :], r_ps[:, :], z_ps[:, :]]

        ld_first = sem("ld_first")
        ld_const = sem("ld_const")
        ld_graph = sem("ld_graph")
        ld_ffn = sem("ld_ffn")
        ld_late = sem("ld_late")
        ld_down = sem("ld_down")
        ld_up = sem("ld_up")
        stored = sem("stored")
        dve_step = sem("dve_step")
        act_step = sem("act_step")
        pool_step = sem("pool_step")
        pads_set = sem("pads_set")
        scaled_co = sem("scaled_co")
        co_turned = sem("co_turned")
        digits_ready = sem("digits_ready")
        digits_turned = sem("digits_turned")
        weights_ready = sem("weights_ready")
        diff_a_ready = sem("diff_a_ready")
        diff_d_ready = sem("diff_d_ready")
        counted_a = sem("counted_a")
        counted_d = sem("counted_d")
        ranks_ready = sem("ranks_ready")
        onehot_ready = sem("onehot_ready")
        var_ready = sem("var_ready")
        rstd_ready = sem("rstd_ready")
        ft_ready = sem("ft_ready")
        ft_turned = sem("ft_turned")
        parts_ready = sem("parts_ready")
        wv_ready = sem("wv_ready")
        turned_ready = sem("turned_ready")
        gathered = sem("gathered")
        rep_ready = sem("rep_ready")
        rep_used = sem("rep_used")
        sorted_ready = sem("sorted_ready")
        fs_ready = sem("fs_ready")
        fold_ready = sem("fold_ready")
        fold_used = sem("fold_used")
        q_ready = sem("q_ready")
        bd_ready = sem("bd_ready")
        s_ready = sem("s_ready")
        max_ready = sem("max_ready")
        md_ready = sem("md_ready")
        mt_ready = sem("mt_ready")
        sub_ready = sem("sub_ready")
        exp_ready = sem("exp_ready")
        sum_ready = sem("sum_ready")
        probs_ready = sem("probs_ready")
        spread_ready = sem("spread_ready")
        part0_ready = sem("part0_ready")
        v_ready = sem("v_ready")
        vt_ready = sem("vt_ready")
        h_ready = sem("h_ready")
        hs_ready = sem("hs_ready")
        hs_used = sem("hs_used")
        centre_ready = sem("centre_ready")
        gc_ready = sem("gc_ready")
        stat_in = sem("stat_in")
        stat_mean = sem("stat_mean")
        stat_mean_used = sem("stat_mean_used")
        h3_ready = sem("h3_ready")
        xn_ready = sem("xn_ready")
        xn_turned = sem("xn_turned")
        xnT_ready = sem("xnT_ready")
        gp_ready = sem("gp_ready")
        edf_ready = sem("edf_ready")
        tmp_ready = sem("tmp_ready")
        gu_ready = sem("gu_ready")
        gu_exp = sem("gu_exp")
        gu_used = sem("gu_used")
        y_ready = sem("y_ready")
        xr_ready = sem("xr_ready")
        xn2_ready = sem("xn2_ready")
        xn2_turned = sem("xn2_turned")
        xn2T_ready = sem("xn2T_ready")
        moe_h = sem("moe_h")
        moe_relu = sem("moe_relu")
        moe_relu_turned = sem("moe_relu_turned")
        moe_hT = sem("moe_hT")
        moe_gates = sem("moe_gates")
        top_exp_in = sem("top_exp_in")
        top_exp = sem("top_exp")
        picks_ready = sem("picks_ready")
        counts_ready = sem("counts_ready")
        lora_ready = sem("lora_ready")
        lora_turned = sem("lora_turned")
        lora_T = sem("lora_T")
        moe_out = sem("moe_out")
        y_out = sem("y_out")

        block = ctx.enter_context(nc.Block())

        @block.sync
        def _(sp):
            sp.dma_start(co_sb[:], coords).then_inc(ld_first, 16)
            sp.dma_start(x_sb[:], x).then_inc(ld_first, 16)
            sp.dma_start(id_sb[:], ident).then_inc(ld_first, 16)
            sp.dma_start(cst[:], consts).then_inc(ld_const, 16)
            sp.dma_start(wlin_sb[:], wlin).then_inc(ld_graph, 16)
            sp.dma_start(wconv_sb[:], wconv).then_inc(ld_graph, 16)
            sp.dma_start(blin_sb[:], blin).then_inc(ld_graph, 16)
            sp.dma_start(wc3_sb[:], wc3).then_inc(ld_graph, 16)
            sp.dma_start(upgate_sb[:], upgate).then_inc(ld_ffn, 16)
            sp.dma_start(local_sb[:], local).then_inc(ld_ffn, 16)
            sp.dma_start(gate_sb[:], gate).then_inc(ld_ffn, 16)
            sp.dma_start(rowc_sb[:], rowc).then_inc(ld_ffn, 16)
            sp.dma_start(gw2_sb[:], gw2).then_inc(ld_ffn, 16)
            sp.wait_ge(gathered, 4)
            sp.dma_start(fuse_sb, fuse).then_inc(ld_late, 16)
            sp.dma_start(moe1_sb, moe1).then_inc(ld_late, 16)
            sp.dma_start(moe2_sb, moe2).then_inc(ld_late, 16)
            sp.dma_start(moe3_sb, moe3).then_inc(ld_late, 16)
            sp.wait_ge(s_ready, STEPS)
            sp.dma_start(up_sb, up).then_inc(ld_up, 16)
            sp.wait_ge(h_ready, 3 * STEPS)
            sp.dma_start(ffn2_sb[:, 0:(NF - 1) * N], ffn2a).then_inc(ld_down, 16)
            sp.dma_start(ffn2_sb[0:FCH[-1][1], (NF - 1) * N:NF * N], ffn2b).then_inc(ld_down, 16)
            sp.wait_ge(y_out, 1)
            sp.dma_start(out, xn2).then_inc(stored, 16)
            sp.wait_ge(stored, 16)

        @block.gpsimd
        def _(pool):
            step = [0]

            def link(ins):
                step[0] += 1
                ins.then_inc(pool_step, 1)
                pool.wait_ge(pool_step, step[0])

            pool.memset(bst[:], 0.0).then_inc(pads_set, 1)
            pool.memset(bsm[:], 0.0).then_inc(pads_set, 1)
            pool.iota(iota16[:], [[1, N]], base=0, channel_multiplier=0,
                      allow_small_or_imprecise_dtypes=True).then_inc(pads_set, 1)
            pool.memset(src2, 0.0).then_inc(pads_set, 1)
            pool.memset(rhs2[:], 0.0).then_inc(pads_set, 1)
            pool.memset(wv[:], 0.0).then_inc(pads_set, 1)
            pool.memset(fs[:], 0.0).then_inc(pads_set, 1)
            pool.memset(f4[:], 0.0).then_inc(pads_set, 1)
            pool.memset(f16f[:], 0.0).then_inc(pads_set, 1)
            pool.memset(qc[:].bitcast(F32), 0.0).then_inc(pads_set, 1)
            pool.memset(qbd[:].bitcast(F32), 0.0).then_inc(pads_set, 1)
            pool.wait_ge(ld_const, 16)

            def rstd(n, col, np_):
                pool.wait_ge(var_ready, n + 1)
                t, w = col
                link(pool.tensor_tensor(t, t, eps_of(np_, w), ALU.add))
                pool.tensor_tensor(t, t, half_of(np_, w), ALU.pow).then_inc(rstd_ready, 1)

            def eps_of(np_, w):
                return view(cst, 0, np_, CONST_AT["eps"][0], [[0, w]])

            def half_of(np_, w):
                return view(cst, 0, np_, CONST_AT["nhalf"][0], [[0, w]])

            def windows(g):
                lb, q = divmod(g, PIECES)
                b = lb % B
                pool.wait_ge(fs_ready, 2 * (lb + 1))
                if g >= 3:
                    pool.wait_ge(bd_ready, 4 * (g - 2))
                    pool.wait_ge(v_ready, value_chunks(g - 2))
                first = q * PTS
                qo = (g % 3) * COLS
                near = view(fs, 0, P, b * FSW + first, [[PB, BLOCKS], [1, PB], [1, K]])
                mid = view(f4, 0, P, b * PIECES * PTS + first, [[PB, BLOCKS], [1, PB], [0, K]])
                dst = view(qc, 0, P, qo, [[SLOT, BLOCKS], [K, PB], [1, K]])
                main = pool.tensor_tensor(dst, near, mid, ALU.subtract)
                if q > 0:
                    main.then_inc(q_ready, 1)
                    return
                link(main)
                for i in range(LEFT):
                    w = LEFT - i
                    at = qo + (i // PB) * SLOT + (i % PB) * K
                    last = pool.tensor_tensor(view(qc, 0, P, at, [[1, w]]),
                                              view(fs, 0, P, b * FSW + LEFT + i + LEFT, [[0, w]]),
                                              view(f4, 0, P, b * PIECES * PTS + i, [[0, w]]), ALU.subtract)
                    if i < LEFT - 1:
                        link(last)
                last.then_inc(q_ready, 1)

            def spread_max(g):
                pool.wait_ge(max_ready, g + 1)
                if g >= 1:
                    pool.wait_ge(mt_ready, g)
                pool.tensor_tensor(view(md, 0, P, 0, [[K, BLOCKS], [1, K]]),
                                   view(mx, 0, P, 0, [[1, BLOCKS], [0, K]]),
                                   view(cst, 0, P, CONST_AT["i10"][0], [[0, BLOCKS], [1, K]]),
                                   ALU.mult).then_inc(md_ready, 1)

            def spread_probs(g):
                pool.wait_ge(probs_ready, g + 1)
                if g >= 2:
                    pool.wait_ge(h_ready, 3 * (g - 1))
                o = CONST_AT["own"][0]
                pool.tensor_tensor(view(px, 0, P, (g % 2) * COLS, [[SLOT, BLOCKS], [K, PB], [1, K]]),
                                   view(pn, 0, P, 0, [[K, BLOCKS], [0, PB], [1, K]]),
                                   view(cst, 0, P, o, [[0, BLOCKS], [1, PB], [0, K]]),
                                   ALU.mult).then_inc(spread_ready, 1)

            rstd(0, (mv[0:C, 1:4:2], 2), C)
            windows(0)
            for t in range(STEPS + LAST_AT - PIECES + 1):
                if 1 <= t <= STEPS:
                    spread_max(t - 1)
                if 2 <= t < STEPS + 2:
                    spread_probs(t - 2)
                if t in TAIL_AT:
                    rstd(1 + TAIL_AT.index(t), (mv[:, 3:4], 1), P)
                if t + 1 < STEPS:
                    windows(t + 1)
            rstd(5, (mv[0:C, 1:4:2], 2), C)
            rstd(6, (mv[0:C, 1:4:2], 2), C)
            rstd(7, (rst[:, 1:2], 1), T)
            rstd(8, (rst[:, 3:4], 1), T)

        @block.scalar
        def _(act):
            step = [0]

            def link(ins):
                step[0] += 1
                ins.then_inc(act_step, 1)
                act.wait_ge(act_step, step[0])

            counted = [0]

            def count_smaller(i, bank):
                n = counted[0]
                act.wait_ge(diff_a_ready, n + 1)
                if n >= 2:
                    act.wait_ge(counted_a, n - 1)
                act.activation(junk_sign[n % 2], bank, ACT.Sign, accum_out=sg[:, i:i + 1]).then_inc(counted_a, 1)
                counted[0] += 1

            def features(lb):
                b = lb % B
                act.wait_ge(rep_ready, lb + 1)
                if lb >= 2:
                    act.wait_ge(q_ready, 4 * (lb - 1))
                    act.wait_ge(centre_ready, lb - 1)
                at = b * PIECES * PTS
                link(act.activation(f4[:, at:at + N], z_ps[:, :], ACT.Copy))
                link(act.activation(f16h[:], z_ps[:, :], ACT.Copy))
                act.activation(f16f[:, 0:N], f16h[:], ACT.Copy).then_inc(rep_used, 1)
                act.wait_ge(gathered, lb + 1)
                act.activation(view(gs, 0, P, 0, [[P, NK], [1, M], [M, C]]),
                               view(z_ps, 0, P, 0, [[P, NK], [C, M], [1, C]]), ACT.Copy).then_inc(turned_ready, 1)
                act.wait_ge(sorted_ready, lb + 1)
                at = b * FSW
                act.activation(fs[:, at + LEFT:at + LEFT + N], z_ps[:, :], ACT.Copy).then_inc(fs_ready, 1)
                act.activation(fs[:, at + LEFT + N:at + FSW], view(z_ps, 0, P, N - 1, [[0, FSW - LEFT - N]]),
                               ACT.Copy).then_inc(fs_ready, 1)
                act.wait_ge(centre_ready, lb + 1)
                if lb >= 2:
                    act.wait_ge(hs_used, lb - 1)
                w = 2 * PTS if lb >= B else PTS
                act.activation(gc[:, b * 2 * PTS:b * 2 * PTS + w], z_ps[:, 0:w], ACT.Copy).then_inc(gc_ready, 1)

            def front(g, h):
                act.wait_ge(q_ready, g + 1)
                if g >= 2:
                    act.wait_ge(s_ready, g - 1)
                act.activation(view(qbd, 32 * h, 32, (g % 2) * BLOCKS * P + 32 * h, [[P, BLOCKS], [1, SLOT]]),
                               view(qc, 32 * h, 32, (g % 3) * COLS, [[SLOT, BLOCKS], [1, SLOT]]),
                               ACT.Copy).then_inc(bd_ready, 1)

            def first_of_three(g):
                act.wait_ge(s_ready, g + 1)
                if g >= 1:
                    act.wait_ge(exp_ready, g)
                o = CONST_AT["own"][0]
                act.activation(view(sc, 0, P, 0, [[K, BLOCKS], [1, K]]),
                               view(s_ps, 0, P, 0, [[SLOT, BLOCKS], [1, K]]), ACT.Copy,
                               scale=cst[:, o:o + 1]).then_inc(part0_ready, 1)

            def exps(g):
                act.wait_ge(sub_ready, g + 1)
                if g >= 2:
                    act.wait_ge(probs_ready, g - 1)
                e = (g % 2) * NC
                act.activation(ex[:, e:e + NC], sc[:], ACT.Exp, scale=float(1.0 / 32 ** 0.5)).then_inc(exp_ready, 1)

            def evacuate(g, j):
                lb, q = divmod(g, PIECES)
                oc = OUT_CH[lb // B]
                side = P // oc
                t0, n = THIRDS[j]
                if q == 0 and j == 0 and lb >= 1:
                    act.wait_ge(hs_used, lb)
                p0 = oc * (q % side)
                act.wait_ge(h_ready, 3 * g + j + 1)
                o = (q // side) * PTS * K + t0 * PB * K
                act.activation(hs[p0:p0 + oc, o:o + n * PB * K], z_ps[p0:p0 + oc, 0:n * PB * K], ACT.Copy)\
                   .then_inc(hs_ready, 1)

            for i in range(8):
                count_smaller(i, banks[2 * i % 8])
            act.wait_ge(pads_set, 11)
            features(0)
            for t in range(STEPS + LAST_AT - PIECES + 1):
                if 1 <= t <= STEPS:
                    first_of_three(t - 1)
                for h in range(4):
                    if 3 <= t < STEPS + 3 and h < 3:
                        evacuate(t - 3, h)
                    if t < STEPS:
                        front(t, h)
                if 1 <= t <= STEPS:
                    exps(t - 1)
                if t == 3:
                    features(1)
                if t in TAIL_AT[:2]:
                    features(2 + TAIL_AT.index(t))
                if t < 3:
                    for i in RANKS_LATER[t]:
                        count_smaller(8 + i, z_ps[:, :])

            act.wait_ge(ld_ffn, 80)
            act.activation(edf[:], local_sb[:, 1:1 + G], ACT.Exp, scale=-1.0).then_inc(edf_ready, 1)
            for i, (f0, n) in enumerate(FCH):
                act.wait_ge(gu_ready, i + 1)
                if i >= 2:
                    act.wait_ge(gu_used, i - 1)
                act.activation(sig[0:n, (i % 2) * T:(i % 2) * T + T], gu_bank(banks, i)[0:n, 0:T], ACT.Exp,
                               scale=-1.0).then_inc(gu_exp, 1)
            act.wait_ge(top_exp_in, 1)
            act.activation(mo[:, 200:201], mo[:, 199:200], ACT.Exp).then_inc(top_exp, 1)

        @block.vector
        def _(dve):
            step = [0]

            def link(ins):
                step[0] += 1
                ins.then_inc(dve_step, 1)
                dve.wait_ge(dve_step, step[0])

            v = dve
            norm = [0]

            def wait_rstd():
                norm[0] += 1
                dve.wait_ge(rstd_ready, norm[0])

            dve.wait_ge(ld_first, 48)
            lo, hi, rng, rc, sca, er = (qs[:, i:i + 1] for i in range(6))
            link(v.tensor_reduce(lo, co_sb[:], AX, ALU.min))
            link(v.tensor_reduce(hi, co_sb[:], AX, ALU.max))
            link(v.tensor_tensor(rng, hi, lo, ALU.subtract))
            link(v.tensor_scalar(rng, rng, 1e-6, None, ALU.add))
            link(v.reciprocal(rc, rng))
            link(v.tensor_scalar(sca, rc, float(2 ** BITS - 1), None, ALU.mult))
            v.tensor_scalar(co_sb[:], co_sb[:], lo, sca, ALU.subtract, ALU.mult).then_inc(scaled_co, 1)

            def ln_stats(src):
                for b in range(B):
                    link(v.bn_stats(bst[0:C, 6 * b:6 * b + 6], src[:, b, :]))
                    v.bn_aggr(mv[0:C, 2 * b:2 * b + 2], bst[0:C, 6 * b:6 * b + 6]).then_inc(
                        var_ready if b == B - 1 else dve_step, 1)
                    if b < B - 1:
                        step[0] += 1
                        dve.wait_ge(dve_step, step[0])

            dve.wait_ge(pads_set, 1)
            ln_stats(x_sb)

            dve.wait_ge(co_turned, 1)
            vq, vf, vg = (qv[:, 24 * i:24 * i + 24] for i in range(3))
            link(v.tensor_copy(vq, z_ps[:, 0:24]))
            link(v.tensor_copy(qvi[:], vq))
            link(v.tensor_copy(vf, qvi[:]))
            link(v.tensor_tensor(vg, vf, vq, ALU.is_gt))
            link(v.tensor_tensor(vf, vf, vg, ALU.subtract))
            link(v.tensor_scalar(vf, vf, 0.0, float(2 ** BITS - 1), ALU.max, ALU.min))
            for c in range(3):
                for o in range(2):
                    d = c if c == 2 else c ^ o
                    link(v.tensor_copy(view(kx, 0, P, 32 * c + 8 * o, [[16, 2], [4, B], [1, NK]]),
                                       view(qv, 0, P, 24 + d, [[0, 2], [3, B], [6, NK]])))

            X = [kx[:, 32 * c + 16:32 * c + 32] for c in range(3)]
            ma, mb, mc = (kt[:, 32 * i:32 * i + 16] for i in range(3))

            def bit_mask(dst, src, b):
                link(v.tensor_scalar(dst, src, 31 - b, 31, ALU.logical_shift_left, ALU.arith_shift_right))

            for b in range(BITS - 1, 0, -1):
                low = (1 << b) - 1
                bit_mask(ma, X[0], b)
                link(v.scalar_tensor_tensor(X[0], ma, low, X[0], ALU.bitwise_and, ALU.bitwise_xor))
                for c in (1, 2):
                    bit_mask(ma, X[c], b)
                    link(v.tensor_tensor(mb, X[0], X[c], ALU.bitwise_xor))
                    link(v.tensor_tensor(mb, mb, ma, ALU.bitwise_or))
                    link(v.scalar_tensor_tensor(X[0], mb, low, X[0], ALU.bitwise_and, ALU.bitwise_xor))
                    link(v.tensor_tensor(mb, mb, ma, ALU.bitwise_xor))
                    link(v.scalar_tensor_tensor(X[c], mb, low, X[c], ALU.bitwise_and, ALU.bitwise_xor))
            link(v.tensor_tensor(X[1], X[1], X[0], ALU.bitwise_xor))
            link(v.tensor_tensor(X[2], X[2], X[1], ALU.bitwise_xor))
            link(v.tensor_scalar(ma, X[2], 1, None, ALU.logical_shift_right))
            for sh in (1, 2, 4, 8):
                link(v.scalar_tensor_tensor(mb, ma, sh, ma, ALU.logical_shift_right, ALU.bitwise_xor))
                ma, mb = mb, ma
            for c in range(3):
                link(v.tensor_tensor(X[c], X[c], ma, ALU.bitwise_xor))
            ka, kb = kx, kt[:, 96:192]
            for sh, mask in ((16, 0x030000FF), (8, 0x0300F00F), (4, 0x030C30C3), (2, 0x09249249)):
                link(v.scalar_tensor_tensor(kb, ka, sh, ka, ALU.logical_shift_left, ALU.bitwise_or))
                link(v.tensor_scalar(ka, kb, mask, None, ALU.bitwise_and))
            key, ky2 = kt[:, 0:32], kt[:, 32:64]
            link(v.scalar_tensor_tensor(ky2, kx[:, 0:32], 1, kx[:, 32:64], ALU.logical_shift_left, ALU.bitwise_or))
            link(v.scalar_tensor_tensor(key, ky2, 1, kx[:, 64:96], ALU.logical_shift_left, ALU.bitwise_or))
            dve.wait_ge(ld_const, 16)
            low14 = kt[:, 64:96]
            link(v.tensor_scalar(low14, key, 0x3FFF, 9, ALU.bitwise_and, ALU.logical_shift_left))
            link(v.tensor_tensor(low14, low14, const("point").bitcast(I32), ALU.bitwise_or))
            digs = [(low14, 0, 255), (low14, 8, 255), (low14, 16, 127), (key, 14, 255), (key, 22, 255)]
            for i, (src, sh, mask) in enumerate(digs):
                link(v.tensor_scalar(kt[:, 96 + 32 * i:128 + 32 * i], src, sh, mask,
                                     ALU.logical_shift_right, ALU.bitwise_and))
            for i in range(5):
                ins = v.tensor_copy(view(dg, 0, P, 8 * i, [[1, M], [4, B], [40, NK]]),
                                    view(kt, 0, P, 96 + 32 * i, [[8, M], [4, B], [1, NK]]))
                if i < 4:
                    link(ins)
            ins.then_inc(digits_ready, 1)

            dve.wait_ge(fold_ready, 1)
            for l in range(2):
                oc = OUT_CH[l]
                link(v.tensor_copy(wn_sb[:, l, 0:oc], r_ps[:, 192 * l:192 * l + oc]))
                link(v.tensor_copy(bv_sb[:, l:l + 1], r_ps[:, 192 * l + 128:192 * l + 129]))
                link(v.tensor_copy(wnb[:, 32 * l:32 * l + oc], r_ps[:, 192 * l + 64:192 * l + 64 + oc]))

            dve.wait_ge(digits_turned, 1)
            dve.wait_ge(pads_set, 5)
            link(v.tensor_copy(rhs2[0:40, :], z_ps[0:40, :]))
            link(v.tensor_scalar(rhs2[64:128, :], rhs2[64:128, :], 1.0, None, ALU.add))
            link(v.tensor_copy(src2[64:104, :], rhs2[0:40, :]))
            link(v.tensor_scalar(src2[0:40, :], src2[0:40, :], 1.0, None, ALU.add))

            def key_weights(b):
                for i in range(2 * M):
                    m, part = divmod(i, 2)
                    at = CONST_AT["digit_w"][0] + part * B * M + b * M + m
                    v.tensor_scalar(lw[b][:, i * N:(i + 1) * N], src2, cst[:, at:at + 1], None, ALU.mult)\
                     .then_inc(weights_ready, 1)

            key_weights(0)

            def ln_apply(dst, src):
                wait_rstd()
                for b in range(B):
                    yield v.tensor_scalar(dst[:, b, :], src[:, b, :], mv[0:C, 2 * b:2 * b + 1],
                                          mv[0:C, 2 * b + 1:2 * b + 2], ALU.subtract, ALU.mult)

            for ins in ln_apply(ft[0], x_sb):
                ins.then_inc(ft_ready, 1)

            for i in range(8):
                dve.wait_ge(diff_d_ready, i + 1)
                if i >= 2:
                    dve.wait_ge(counted_d, i - 1)
                v.tensor_scalar(junk[i % 2], banks[(2 * i + 1) % 8], 0.0, 0.0, ALU.is_lt, ALU.add,
                                accum_out=rk[:, 2 * i + 1:2 * i + 2]).then_inc(counted_d, 1)

            def one_hot(b):
                if b == 0:
                    dve.wait_ge(counted_a, 8)
                    dve.wait_ge(counted_d, 8)
                    link(v.tensor_scalar(view(rk, 0, P, 0, [[2, 8]]), sg[:, 0:8], -0.5, (N - 1) / 2, ALU.mult, ALU.add))
                else:
                    dve.wait_ge(counted_a, 24)
                    link(v.tensor_scalar(rk[:, 16:32], sg[:, 8:24], -0.5, (N - 1) / 2, ALU.mult, ALU.add))
                for m in range(M):
                    for k in range(NK):
                        i = (b * M + m) * NK + k
                        at = ((b * NK + k) * M + m) * N
                        v.tensor_scalar(oh[:, at:at + N], iota16[:], rk[:, i:i + 1], None, ALU.is_equal)\
                         .then_inc(onehot_ready, 1)

            def split(parts, rest, src):
                link(v.tensor_copy(parts[0], src))
                link(v.tensor_tensor(rest[0], src, parts[0], ALU.subtract))
                link(v.tensor_copy(parts[1], rest[0]))
                link(v.tensor_tensor(rest[1], rest[0], parts[1], ALU.subtract))
                return v.tensor_copy(parts[2], rest[1])

            def split_features(lb):
                dve.wait_ge(ft_turned, lb + 1)
                if lb >= 1:
                    dve.wait_ge(gathered, lb)
                split([fpartb[:, i * P:(i + 1) * P] for i in range(3)], [frest[:, i * P:(i + 1) * P] for i in range(2)],
                      z_ps[:, 0:P]).then_inc(parts_ready, 1)

            def split_weights():
                link(split([wparts[:, i * 96:(i + 1) * 96] for i in range(3)],
                           [frest[:, i * P:i * P + 96] for i in range(2)], wnb[:]))
                for half in range(3):
                    for h in range(4):
                        v.tensor_copy(view(wv, 32 * h, 32, half * 3 * P + 32 * h, [[P, 3], [1, 32]]),
                                      view(wparts, 32 * h, 32, 32 * half, [[96, 3], [1, 32]])).then_inc(wv_ready, 1)

            def turn_values(g):
                if g >= 2:
                    dve.wait_ge(h_ready, 3 * (g - 1))
                c = value_chunks(g)
                oc = OUT_CH[g // (B * PIECES)]
                for half in range(1 + g // (B * PIECES)):
                    for t0, n in THIRDS:
                        dve.wait_ge(v_ready, c + 1)
                        at = (g % 2) * 2 * COLS + t0 * oc + half * SLOT
                        v.transpose(view(vt, 0, P, at, [[oc, n], [1, SLOT]]), v_ps[:, (c % 2) * 512:(c % 2) * 512 + n * SLOT])\
                         .then_inc(vt_ready, 1)
                        c += 1

            def compact(g):
                dve.wait_ge(part0_ready, g + 1)
                if g >= 1:
                    dve.wait_ge(md_ready, g)
                m0 = CONST_AT["own"][0]
                flat = view(sc, 0, P, 0, [[K, BLOCKS], [1, K]])
                for j in (1, 2):
                    link(v.scalar_tensor_tensor(flat, view(s_ps, 0, P, j * K, [[SLOT, BLOCKS], [1, K]]),
                                                cst[:, m0 + j:m0 + j + 1], flat, ALU.mult, ALU.add))
                v.tensor_reduce(mx[:], flat, AX, ALU.max).then_inc(max_ready, 1)

            def subtract(g):
                dve.wait_ge(mt_ready, g + 1)
                v.tensor_tensor(sc[:], sc[:], mt_ps[:, 0:NC], ALU.add).then_inc(sub_ready, 1)

            def normalise(g):
                dve.wait_ge(sum_ready, g + 1)
                if g >= 1:
                    dve.wait_ge(spread_ready, g)
                e = (g % 2) * NC
                link(v.reciprocal(ri[:], r_ps[:, 0:NC]))
                v.tensor_tensor(pn[:], ri[:], ex[:, e:e + NC], ALU.mult).then_inc(probs_ready, 1)

            def tail(lb):
                l, b = divmod(lb, B)
                dve.wait_ge(ft_ready, 2 + lb)
                dve.wait_ge(hs_ready, 3 * PIECES * (lb + 1))
                dve.wait_ge(gc_ready, lb + 1)
                halves = 1 + l
                w = halves * PTS
                whole = P - OUT_CH[l]
                centre = gc[:, b * 2 * PTS:b * 2 * PTS + w]
                link(v.tensor_reduce(hm[:, 0:w], view(hs, 0, P, 0, [[K, w], [1, K]]), AX, ALU.max))
                link(v.tensor_reduce(hb[:, 0:w], view(hs, 0, P, 0, [[K, w], [1, K]]), AX, ALU.add))
                link(v.tensor_scalar(hb[:, 0:w], hb[:, 0:w], 1.0 / K, None, ALU.mult))
                link(v.tensor_tensor(hu[:, 0:w], hb[:, 0:w], centre, ALU.add))

                def spans(step_, split_, short, end):
                    for half in range(halves):
                        o = half * end
                        last = half == halves - 1
                        for i in range(split_):
                            yield P, o + i * step_, o + (short if last and i == split_ - 1 else (i + 1) * step_)
                    yield whole, o + short, o + end

                for i, (np_, a, z) in enumerate(spans(PTS * K // 3, 3, PTS_LAST * K, PTS * K)):
                    link(v.bn_stats(bst[0:np_, 6 * i:6 * i + 6], hs[0:np_, a:z]))
                nst = i + 1
                for j, t in enumerate((hb, hu)):
                    for i, (np_, a, z) in enumerate(spans(PTS, 1, PTS_LAST, PTS)):
                        link(v.bn_stats(bsm[0:np_, 18 * j + 6 * i:18 * j + 6 * i + 6], t[0:np_, a:z]))
                link(v.bn_aggr(mv[:, 0:2], bst[:, 0:6 * nst]))
                link(v.bn_aggr(mv[:, 8:10], bsm[:, 0:6 * (1 + halves)]))
                link(v.bn_aggr(mv[:, 10:12], bsm[:, 18:18 + 6 * (1 + halves)]))
                v.tensor_copy(mv[:, 2:3], mv[:, 10:11]).then_inc(stat_in, 1)
                link(v.tensor_tensor(mv[:, 1:2], mv[:, 1:2], mv[:, 9:10], ALU.subtract))
                link(v.tensor_tensor(mv[:, 1:2], mv[:, 1:2], mv[:, 11:12], ALU.add))
                link(v.tensor_tensor(hm[:, 0:w], hm[:, 0:w], centre, ALU.add))
                v.tensor_scalar(hm[:, 0:w], hm[:, 0:w], bv_sb[:, l:l + 1], None, ALU.add).then_inc(hs_used, 1)

            def finish_tail(lb):
                l, b = divmod(lb, B)
                w = (1 + l) * PTS
                dve.wait_ge(stat_mean, 2 * lb + 1)
                link(v.tensor_copy(mv[:, 4:5], mt_ps[:, 440:441]))
                link(v.tensor_tensor(mv[:, 5:6], mv[:, 10:11], mv[:, 4:5], ALU.subtract))
                v.scalar_tensor_tensor(mv[:, 2:3], mv[:, 5:6], mv[:, 5:6], mv[:, 1:2], ALU.mult, ALU.add)\
                 .then_inc(stat_in, 1)
                dve.wait_ge(stat_mean, 2 * lb + 2)
                v.tensor_copy(mv[:, 3:4], mt_ps[:, 440:441]).then_inc(var_ready, 1)
                link(v.tensor_tensor(mv[:, 4:5], mv[:, 4:5], bv_sb[:, l:l + 1], ALU.add))
                wait_rstd()
                link(v.tensor_scalar(hn[:, 0:w], hm[:, 0:w], mv[:, 4:5], mv[:, 3:4], ALU.subtract, ALU.mult))
                oc = OUT_CH[l]
                for q in range(PIECES):
                    p0 = 32 * q if l == 0 else 64 * (q % 2)
                    o = 0 if l == 0 else (q // 2) * PTS
                    n = PTS if q < PIECES - 1 else PTS_LAST
                    src = hn[p0:p0 + oc, o:o + n]
                    ins = v.scalar_tensor_tensor(ft[l + 1][:, b, q * PTS:q * PTS + n], src, 0.2, src,
                                                 ALU.mult, ALU.max)
                    if q < PIECES - 1:
                        link(ins)
                ins.then_inc(ft_ready, 1)

            dve.wait_ge(pads_set, 6)
            one_hot(0)
            split_features(0)
            split_weights()
            key_weights(1)
            for t in range(STEPS + LAST_AT - PIECES + 1):
                if 1 <= t <= STEPS:
                    compact(t - 1)
                if t in TAIL_AT:
                    tail(TAIL_AT.index(t))
                if 2 <= t < STEPS + 2:
                    normalise(t - 2)
                if 2 <= t < STEPS + 2:
                    turn_values(t - 2)
                if 1 <= t <= STEPS:
                    subtract(t - 1)
                if t == 3:
                    one_hot(1)
                    split_features(1)
                if t in TAIL_AT:
                    finish_tail(TAIL_AT.index(t))
                if t in TAIL_AT[:2]:
                    split_features(2 + TAIL_AT.index(t))

            def row_stats(src):
                ln_stats(src)

            dve.wait_ge(h3_ready, 1)
            for b in range(B):
                link(v.tensor_copy(h3[:, b, :], banks[b][0:C, :]))
            ln_stats(h3)
            for ins in ln_apply(h3, h3):
                link(ins)
            for b in range(B):
                link(v.scalar_tensor_tensor(h3[:, b, :], h3[:, b, :], 0.2, h3[:, b, :], ALU.mult, ALU.max))
                link(v.tensor_tensor(x1[:, b, :], x_sb[:, b, :], h3[:, b, :], ALU.add))
            ln_stats(x1)
            for ins in ln_apply(h3, x1):
                ins.then_inc(xn_ready, 1)
            for b in range(B):
                link(v.tensor_copy(xr[C * b:C * b + C, :], x1[:, b, :]))
            dve.wait_ge(xn_turned, 1)
            v.tensor_copy(xnT, view(v_ps, 0, P, 0, [[T, NK], [1, T]])).then_inc(xnT_ready, 1)

            dve.wait_ge(gp_ready, 1)
            dve.wait_ge(edf_ready, 1)
            col = [gp[:, i * T:(i + 1) * T] for i in range(12)]
            up, delta, power, keep, tmp = col[0], col[1], col[2], col[3], col[4:4 + G]
            link(v.tensor_copy(up, banks[0][:, 0:T]))
            link(v.tensor_scalar(delta, banks[1][:, 0:T], local_sb[:, 0:1], None, ALU.subtract))
            link(v.scalar_tensor_tensor(keep, delta, -2.5, up, ALU.is_ge, ALU.mult))
            link(v.scalar_tensor_tensor(keep, delta, 2.5, keep, ALU.is_le, ALU.mult))
            link(v.tensor_copy(power, delta))
            for m in range(G):
                if m:
                    link(v.tensor_tensor(power, power, delta, ALU.mult))
                ins = v.scalar_tensor_tensor(tmp[m], power, edf[:, m:m + 1], up if m < 4 else keep,
                                             ALU.mult, ALU.mult)
                if m < G - 1:
                    link(ins)
            ins.then_inc(tmp_ready, 1)
            for i, (f0, n) in enumerate(FCH):
                bank = gu_bank(banks, i)
                dve.wait_ge(gu_exp, i + 1)
                s_ = sig[0:n, (i % 2) * T:(i % 2) * T + T]
                link(v.tensor_scalar(s_, s_, 1.0, None, ALU.add))
                link(v.reciprocal(s_, s_))
                link(v.tensor_tensor(s_, bank[0:n, 0:T], s_, ALU.mult))
                v.tensor_tensor(actT[0:n, i, :], bank[0:n, 256:256 + T], s_, ALU.mult).then_inc(gu_used, 1)
            dve.wait_ge(y_ready, 1)
            link(v.tensor_tensor(x2, z_ps[0:T, :], xr, ALU.add))
            link(v.bn_stats(rst[:, 4:10], x2))
            v.bn_aggr(rst[:, 0:2], rst[:, 4:10]).then_inc(var_ready, 1)
            wait_rstd()
            v.tensor_scalar(xn2, x2, rst[:, 0:1], rst[:, 1:2], ALU.subtract, ALU.mult).then_inc(xn2_ready, 1)
            dve.wait_ge(xn2_turned, 1)
            v.tensor_copy(xnT, view(v_ps, 0, P, 0, [[T, NK], [1, T]])).then_inc(xn2T_ready, 1)

            dve.wait_ge(moe_h, 1)
            h = mo[:, 0:32]
            g_b1, gam, bet, g_b2, rev = (rowc_sb[:, a:a + w] for a, w in ((0, 32), (32, 32), (64, 32), (96, E), (96 + E, E)))
            link(v.tensor_tensor(h, banks[0][0:T, E * R:E * R + 32], g_b1, ALU.add))
            link(v.bn_stats(rst[:, 4:10], h))
            v.bn_aggr(rst[:, 2:4], rst[:, 4:10]).then_inc(var_ready, 1)
            wait_rstd()
            link(v.tensor_scalar(h, h, rst[:, 2:3], rst[:, 3:4], ALU.subtract, ALU.mult))
            link(v.tensor_tensor(h, h, gam, ALU.mult))
            link(v.tensor_tensor(h, h, bet, ALU.add))
            v.tensor_scalar(h, h, 0.0, None, ALU.max).then_inc(moe_relu, 1)
            dve.wait_ge(moe_relu_turned, 1)
            v.tensor_copy(hT, banks[1][0:32, 0:T]).then_inc(moe_hT, 1)
            dve.wait_ge(moe_gates, 1)
            gt = mo[:, 32:40]
            top = mo[:, 40:48]
            link(v.tensor_tensor(gt, banks[2][0:T, 0:E], g_b2, ALU.add))
            link(v.max(top, gt))
            eq, pk, one = mo[:, 48:56], mo[:, 56:64], mo[:, 64:80]
            free = mo[:, 96:104]
            for k in range(2):
                link(v.tensor_scalar(eq, gt, top[:, k:k + 1], None, ALU.is_equal))
                if k == 1:
                    link(v.tensor_tensor(eq, eq, free, ALU.mult))
                link(v.tensor_tensor(pk, eq, rev, ALU.mult))
                link(v.tensor_reduce(mo[:, 80 + k:81 + k], pk, AX, ALU.max))
                link(v.tensor_scalar(one[:, 8 * k:8 * k + 8], rev, mo[:, 80 + k:81 + k], None, ALU.is_equal))
                if k == 0:
                    link(v.tensor_scalar(free, one[:, 0:8], -1.0, 1.0, ALU.mult, ALU.add))
            v.tensor_copy(mo[:, 110:126], one).then_inc(picks_ready, 1)
            v.tensor_tensor(mo[:, 199:200], top[:, 1:2], top[:, 0:1], ALU.subtract).then_inc(top_exp_in, 1)
            dve.wait_ge(top_exp, 1)
            link(v.tensor_scalar(mo[:, 201:202], mo[:, 200:201], 1.0, None, ALU.add))
            link(v.reciprocal(mo[:, 202:203], mo[:, 201:202]))
            link(v.tensor_tensor(mo[:, 203:204], mo[:, 202:203], mo[:, 200:201], ALU.mult))
            dve.wait_ge(counts_ready, 1)
            allow = mo[:, 130:146]
            link(v.tensor_scalar(allow, banks[3][0:T, 0:16], float(CAP), 1.0 / R, ALU.is_le, ALU.mult))
            link(v.tensor_tensor(allow, allow, one, ALU.mult))
            link(v.tensor_scalar(allow[:, 0:8], allow[:, 0:8], mo[:, 202:203], None, ALU.mult))
            link(v.scalar_tensor_tensor(allow[:, 0:8], allow[:, 8:16], mo[:, 203:204], allow[:, 0:8],
                                        ALU.mult, ALU.add))
            v.tensor_tensor(view(mo, 0, T, 256, [[R, E], [1, R]]), view(s_ps, 0, T, 0, [[R, E], [1, R]]),
                            view(mo, 0, T, 130, [[1, E], [0, R]]), ALU.mult).then_inc(lora_ready, 1)
            dve.wait_ge(lora_turned, 1)
            v.tensor_copy(tT, banks[1][:, 128:128 + T]).then_inc(lora_T, 1)
            dve.wait_ge(moe_out, 1)
            v.tensor_tensor(xn2, z_ps[0:T, :], x2, ALU.add).then_inc(y_out, 1)

        @block.tensor
        def _(pe):
            mm = pe.matmul
            pe.wait_ge(ld_first, 48)
            pe.wait_ge(scaled_co, 1)
            for k in range(NK):
                last = pe.transpose(z_ps[:, 6 * k:6 * k + 6], co_sb[:, k * P:(k + 1) * P], id_sb[0:6, 0:6])
            last.then_inc(co_turned, 1)
            pe.wait_ge(ld_graph, 64)
            for l in range(2):
                oc = OUT_CH[l]
                for s_ in range(2):
                    mm(r_ps[:, 192 * l + s_ * 64:192 * l + s_ * 64 + oc], wlin_sb[:, l, s_ * P:(s_ + 1) * P],
                       wconv_sb[:, l, 0:oc], start=True, stop=True)
                last = mm(r_ps[:, 192 * l + 128:192 * l + 129], wconv_sb[:, l, :], blin_sb[:, l:l + 1],
                          start=True, stop=True)
            last.then_inc(fold_ready, 1)
            pe.wait_ge(digits_ready, 1)
            for k in range(NK):
                last = pe.transpose(z_ps[0:40, k * P:(k + 1) * P], dg[:, 40 * k:40 * k + 40], id_sb[:, :])
            last.then_inc(digits_turned, 1)

            def differences(b, m, k, bank):
                pe.wait_ge(weights_ready, 2 * M * b + 2 * m + 2)
                for part in range(2):
                    at = (2 * m + part) * N + k * P
                    last = mm(bank, lw[b][:, at:at + P], rhs2[:], start=part == 0, stop=part == 1)
                return last

            for i in range(16):
                if i >= 8:
                    if i % 2 == 0:
                        pe.wait_ge(counted_a, (i - 8) // 2 + 1)
                    else:
                        pe.wait_ge(counted_d, (i - 8) // 2 + 1)
                differences(0, *divmod(i, NK), banks[i % 8]).then_inc(diff_d_ready if i % 2 else diff_a_ready, 1)
            pe.wait_ge(counted_a, 8)
            pe.wait_ge(counted_d, 8)

            def features(lb):
                l, b = divmod(lb, B)
                src = ft[l]
                pe.wait_ge(ft_ready, lb + 1)
                if lb == 1:
                    pe.wait_ge(counted_a, 24)
                if lb >= 1:
                    pe.wait_ge(gc_ready, lb)
                    pe.wait_ge(hs_ready, 3 * (1 + PIECES * (lb - 1)))
                for k in range(NK):
                    last = pe.transpose(z_ps[:, k * C:(k + 1) * C], src[:, b, k * P:(k + 1) * P], id_sb[0:C, 0:C])
                last.then_inc(ft_turned, 1)
                pe.wait_ge(parts_ready, lb + 1)
                mm(z_ps[:, :], const("rep")[0:C, :], src[:, b, :], start=True, stop=True).then_inc(rep_ready, 1)
                pe.wait_ge(rep_used, lb + 1)
                if lb < 2:
                    pe.wait_ge(onehot_ready, 16 * (b + 1))
                for pt in range(NK):
                    for m in range(M):
                        n = 0
                        for k in range(NK):
                            o = ((b * NK + k) * M + PERMS[l][m]) * N + pt * P
                            for part in range(3):
                                last = mm(z_ps[:, pt * P + m * C:pt * P + (m + 1) * C], oh[:, o:o + P],
                                          fpartb[:, part * P + k * C:part * P + (k + 1) * C],
                                          start=n == 0, stop=n == 3 * NK - 1)
                                n += 1
                last.then_inc(gathered, 1)
                pe.wait_ge(turned_ready, lb + 1)
                for k in range(NK):
                    last = pe.transpose(z_ps[:, k * P:(k + 1) * P], gs[:, k * P:(k + 1) * P], id_sb[:, :])
                last.then_inc(sorted_ready, 1)
                pe.wait_ge(fs_ready, 2 * (lb + 1))
                oc = OUT_CH[l]
                side = P // oc
                for q in range(PIECES):
                    p0, o = oc * (q % side), (q // side) * PTS
                    last = mm(z_ps[p0:p0 + oc, o:o + PTS], wn_sb[:, l, 0:oc], f16f[:, q * PTS:(q + 1) * PTS],
                              start=True, stop=True)
                last.then_inc(centre_ready, 1)

            def scores(g):
                pe.wait_ge(bd_ready, 4 * (g + 1))
                if g >= 1:
                    pe.wait_ge(max_ready, g)
                d, o = (g % 2) * BLOCKS * P, (g % 3) * COLS
                for t in range(BLOCKS):
                    last = mm(s_ps[:, t * SLOT:t * SLOT + PB * K], qbd[:, d + t * P:d + (t + 1) * P],
                              qc[:, o + t * SLOT:o + t * SLOT + PB * K], start=True, stop=True)
                last.then_inc(s_ready, 1)

            def row_max(g):
                pe.wait_ge(md_ready, g + 1)
                if g >= 1:
                    pe.wait_ge(sub_ready, g)
                mm(mt_ps[:, 0:NC], negones, md[:], start=True, stop=True).then_inc(mt_ready, 1)

            def row_sum(g):
                pe.wait_ge(exp_ready, g + 1)
                if g >= 1:
                    pe.wait_ge(probs_ready, g)
                e = (g % 2) * NC
                mm(r_ps[:, 0:NC], posones, ex[:, e:e + NC], start=True, stop=True).then_inc(sum_ready, 1)

            def project(g, i):
                half, j = divmod(i, 3)
                t0, n = THIRDS[j]
                c = value_chunks(g) + i
                if i == 0:
                    pe.wait_ge(q_ready, g + 1)
                if c >= 2:
                    pe.wait_ge(vt_ready, c - 1)
                variant = 0 if g < B * PIECES else 1 + half
                for part in range(3):
                    w = (variant * 3 + part) * P
                    o = (g % 3) * COLS + t0 * SLOT
                    last = mm(v_ps[:, (c % 2) * 512:(c % 2) * 512 + n * SLOT], wv[:, w:w + P],
                              qc[:, o:o + n * SLOT], start=part == 0, stop=part == 2)
                last.then_inc(v_ready, 1)

            def attend(g, j):
                lb, q = divmod(g, PIECES)
                l = lb // B
                oc = OUT_CH[l]
                p0 = oc * (q % (P // oc))
                i = 3 * g + j
                if j == 0:
                    pe.wait_ge(spread_ready, g + 1)
                    pe.wait_ge(vt_ready, value_chunks(g + 1))
                    pe.wait_ge(gc_ready, 1 + sum(t_ < g + 3 for t_ in (3, *TAIL_AT[:2])))
                if i >= 1:
                    pe.wait_ge(hs_ready, i)
                else:
                    pe.wait_ge(counted_a, 24)
                t0, n = THIRDS[j]
                for t in range(n):
                    w = vt[:, (g % 2) * 2 * COLS + (t0 + t) * oc:(g % 2) * 2 * COLS + (t0 + t + 1) * oc]
                    a = (g % 2) * COLS + (t0 + t) * SLOT
                    last = mm(z_ps[p0:p0 + oc, t * PB * K:(t + 1) * PB * K], w, px[:, a:a + PB * K],
                              start=True, stop=True)
                last.then_inc(h_ready, 1)

            def average(lb):
                for r in range(2):
                    pe.wait_ge(stat_in, 2 * lb + r + 1)
                    mm(mt_ps[:, 440:441], const(f"mean{lb // B}"), mv[:, 2:3], start=True, stop=True)\
                        .then_inc(stat_mean, 1)

            features(0)
            pe.wait_ge(wv_ready, 12)
            for t in range(STEPS + LAST_AT - PIECES + 1):
                values = t - 2 if 2 <= t < STEPS + 2 else None
                for i in range(6):
                    if i < 3 and 3 <= t < STEPS + 3:
                        attend(t - 3, i)
                    if values is not None and i < 3 * (1 + values // (B * PIECES)):
                        project(values, i)
                    if i == 0 and 1 <= t <= STEPS:
                        row_max(t - 1)
                if t < STEPS:
                    scores(t)
                if 1 <= t <= STEPS:
                    row_sum(t - 1)
                if t == 3:
                    features(1)
                if t in TAIL_AT:
                    average(TAIL_AT.index(t))
                if t in TAIL_AT[:2]:
                    features(2 + TAIL_AT.index(t))
                if t < 3:
                    pe.wait_ge(gc_ready, 1)
                    for i in RANKS_LATER[t]:
                        if i:
                            pe.wait_ge(counted_a, 8 + i)
                        differences(1, *divmod(i, NK), z_ps[:, :]).then_inc(diff_a_ready, 1)

            pe.wait_ge(ft_ready, 6)
            for b in range(B):
                for j in range(3):
                    kk = 64 if j == 2 else 32
                    last = mm(banks[b][0:C, :], wc3_sb[0:kk, j, :], ft[j][0:kk, b, :], start=j == 0, stop=j == 2)
            last.then_inc(h3_ready, 1)
            pe.wait_ge(xn_ready, 2)
            for b in range(B):
                for k in range(NK):
                    last = pe.transpose(v_ps[:, k * T + b * C:k * T + b * C + C], h3[:, b, k * P:(k + 1) * P],
                                        id_sb[0:C, 0:C])
            last.then_inc(xn_turned, 1)
            pe.wait_ge(xnT_ready, 1)
            pe.wait_ge(ld_ffn, 80)
            for j in range(2):
                for k in range(NK):
                    last = mm(banks[j][:, 0:T], upgate_sb[:, k, j * S:(j + 1) * S], xnT[:, k, :],
                              start=k == 0, stop=k == NK - 1)
            last.then_inc(gp_ready, 1)
            pe.wait_ge(ld_up, 16)
            for i, (f0, n) in enumerate(FCH):
                bank = gu_bank(banks, i)
                if i >= 3:
                    pe.wait_ge(gu_used, i - 2)
                for j in range(2):
                    for k in range(NK):
                        w = gate_sb[:, k, f0:f0 + n] if j == 0 else up_sb[:, k * F + f0:k * F + f0 + n]
                        last = mm(bank[0:n, 256 * j:256 * j + T], w,
                                  xnT[:, k, :], start=k == 0, stop=k == NK - 1)
                last.then_inc(gu_ready, 1)
            pe.wait_ge(tmp_ready, 1)
            pe.wait_ge(ld_late, 64)
            for m in range(G + 1):
                w = fuse_sb[:, m * N:(m + 1) * N]
                lhs = gp[:, 0:T] if m == 0 else gp[:, (3 + m) * T:(4 + m) * T]
                mm(z_ps[0:T, :], lhs, w, start=m == 0, stop=False)
            pe.wait_ge(ld_down, 32)
            for i, (f0, n) in enumerate(FCH):
                pe.wait_ge(gu_used, i + 1)
                last = mm(z_ps[0:T, :], actT[0:n, i, :], ffn2_sb[0:n, i * N:(i + 1) * N],
                          start=False, stop=i == NF - 1)
            last.then_inc(y_ready, 1)
            pe.wait_ge(xn2_ready, 1)
            for k in range(NK):
                last = pe.transpose(v_ps[:, k * T:(k + 1) * T], xn2[:, k * P:(k + 1) * P], id_sb[0:T, 0:T])
            last.then_inc(xn2_turned, 1)
            pe.wait_ge(xn2T_ready, 1)
            for k in range(NK):
                last = mm(banks[0][0:T, 0:E * R + 32], xnT[:, k, :], moe1_sb[:, k * moe1_w:(k + 1) * moe1_w], start=k == 0, stop=k == NK - 1)
            last.then_inc(moe_h, 1)
            for k in range(NK):
                mm(z_ps[0:T, :], xnT[:, k, :], moe2_sb[:, k * N:(k + 1) * N], start=k == 0, stop=False)
            pe.wait_ge(moe_relu, 1)
            pe.transpose(banks[1][0:32, 0:T], mo[:, 0:32], id_sb[0:T, 0:T]).then_inc(moe_relu_turned, 1)
            pe.wait_ge(moe_hT, 1)
            mm(banks[2][0:T, 0:E], hT, gw2_sb[:], start=True, stop=True).then_inc(moe_gates, 1)
            pe.wait_ge(picks_ready, 1)
            mm(banks[3][0:T, 0:16], const("ones")[0:T, 0:T], mo[:, 110:126], start=True, stop=True)\
                .then_inc(counts_ready, 1)
            pe.wait_ge(lora_ready, 1)
            pe.transpose(banks[1][:, 128:128 + T], mo[:, 256:256 + P], id_sb[0:T, 0:T]).then_inc(lora_turned, 1)
            pe.wait_ge(lora_T, 1)
            mm(z_ps[0:T, :], tT, moe3_sb, start=False, stop=True).then_inc(moe_out, 1)


def constants():
    import numpy as np
    p = np.arange(P)
    slot = p % SLOT
    point, o10 = slot // K, slot % K
    head = p // SLOT
    c = {}
    c["own"] = (point[:, None] == np.arange(PB)[None]).astype(np.float32)
    c["i10"] = (o10[:, None] == np.arange(K)[None]).astype(np.float32)
    same = (head[:, None] == head[None]) & (point[:, None] == point[None])
    c["posblk"] = same.astype(np.float32)
    c["negblk"] = -c["posblk"]
    c["eps"] = np.full((P, 1), EPS, np.float32)
    c["nhalf"] = np.full((P, 1), -0.5, np.float32)
    n = np.zeros((P, M, B, NK), np.int32)
    n[:] = p[:, None, None, None] + P * np.arange(NK)
    c["point"] = n.reshape(P, 32).view(np.float32)
    w = np.zeros((P, 2, B * M), np.float32)
    for bm in range(B * M):
        for digit, (part, value) in enumerate(((1, 1.0), (1, 256.0), (1, 65536.0), (0, 2.0 ** 23), (0, 2.0 ** 31))):
            w[8 * digit + bm, part, bm] = value
            w[64 + 8 * digit + bm, part, bm] = -value
    c["digit_w"] = w.reshape(P, 16)
    rep = np.zeros((P, P), np.float32)
    rep[p // M, p] = 1.0
    c["rep"] = rep
    for l in range(2):
        oc = OUT_CH[l]
        side = P // oc
        size = np.zeros(side)
        for q in range(PIECES):
            size[q % side] += PTS if q < PIECES - 1 else PTS_LAST
        c[f"mean{l}"] = ((p[:, None] % oc == p[None] % oc) * (size[p // oc] / N)[:, None]).astype(np.float32)
    c["ones"] = np.ones((P, P), np.float32)
    return np.ascontiguousarray(np.concatenate([c[name] for name, _ in CONST_WIDTHS], axis=1))


def kernel(**inputs):
    import numpy as np
    import concourse.bacc as bacc
    from concourse.bass_utils import run_bass_kernel_spmd as run

    a = {k: np.asarray(v) for k, v in inputs.items()}

    def chunks(w):
        return w.reshape(-1, P, w.shape[1]).transpose(1, 0, 2).reshape(P, -1)

    def rows(v):
        return np.broadcast_to(v, (T, v.shape[0]))

    wc3 = np.zeros((64, 3, C), np.float32)
    w3 = a["L0_xattn_W_conv3"].T
    wc3[0:32, 0], wc3[0:32, 1], wc3[:, 2] = w3[0:32], w3[32:64], w3[64:128]
    wd = a["L0_attn_ffn_down_w"].T
    whole = (NF - 1) * P
    lora_a = a["L0_ffn_lora_A"].transpose(1, 0, 2).reshape(N, E * R)
    df = a["L0_attn_discount_factor"]
    laid = {
        "x": a["x"].transpose(1, 0, 2),
        "coords": a["ctx_4096"][:, 0:3, :].reshape(6, N),
        "consts": constants(),
        "ident": np.eye(P, dtype=np.float32),
        "wlin": np.stack([a["L0_xattn_W_lin1"], a["L0_xattn_W_lin2"]], axis=1),
        "wconv": np.stack([np.tile(a["L0_xattn_W_conv1"].T, (1, 4)), np.tile(a["L0_xattn_W_conv2"].T, (1, 2))], axis=1),
        "blin": np.stack([a["L0_xattn_b_lin1"], a["L0_xattn_b_lin2"]], axis=1),
        "wc3": wc3,
        "upgate": chunks(np.concatenate([a["L0_attn_up_w"].T, a["L0_attn_gate_w"].T], axis=1)).reshape(P, NK, 2 * S),
        "local": np.concatenate([a["L0_attn_local_point"][:, None], np.broadcast_to(df, (P, G))], axis=1),
        "fuse": np.concatenate([a["L0_attn_local_approx_output"].T[:, None],
                                a["L0_attn_fuse_weight"].transpose(1, 2, 0)], axis=1).reshape(P, (G + 1) * N),
        "gate": chunks(a["L0_attn_ffn_gate_w"].T).reshape(P, NK, F),
        "up": chunks(a["L0_attn_ffn_up_w"].T),
        "ffn2a": chunks(wd[:whole]),
        "ffn2b": wd[whole:],
        "moe1": chunks(np.concatenate([lora_a, a["L0_ffn_gw1"].T], axis=1)),
        "moe2": chunks(a["L0_ffn_weight"].T),
        "moe3": a["L0_ffn_lora_B"].reshape(E * R, N),
        "rowc": np.concatenate([rows(a["L0_ffn_gb1"]), rows(a["L0_ffn_ln_gamma"]), rows(a["L0_ffn_ln_beta"]),
                                rows(a["L0_ffn_gb2"]), rows(np.arange(E, 0, -1).astype(np.float32))], axis=1),
        "gw2": a["L0_ffn_gw2"].T,
    }
    nc = bacc.Bacc("TRN2", target_bir_lowering=False, num_devices=1)
    arrays, args = {}, {}
    for name, value in laid.items():
        value = np.ascontiguousarray(value)
        arrays[f"in_{name}"] = value
        args[name] = nc.dram_tensor(f"in_{name}", value.shape, mybir.dt.from_np(value.dtype), kind="ExternalInput").ap()
    out = nc.dram_tensor("out_x", (T, N), F32, kind="ExternalOutput").ap()
    perceiver_layer(nc, out=out, **args)
    result = run(nc, [arrays], core_ids=[0])
    return result.results[0]["out_x"].reshape(B, C, N)
```

```python
import concourse.bass as bass
from concourse import mybir
from contextlib import ExitStack

F32 = mybir.dt.float32
F16 = mybir.dt.float16
BF16 = mybir.dt.bfloat16
I32 = mybir.dt.int32
ALU = mybir.AluOpType
ACT = mybir.ActivationFunctionType
AX = mybir.AxisListType.X

P = 128
B, C, N = 2, 32, 512
K = 10
LEFT = K // 2
M = 4
BITS = 10
NK = N // P
PB = 3
SLOT = 32
BLOCKS = 43
PIECES = 4
PTS = BLOCKS * PB
PTS_LAST = N - (PIECES - 1) * PTS
COLS = BLOCKS * SLOT
NC = BLOCKS * K
STEPS = 2 * B * PIECES
PERMS = ([2, 0, 3, 1], [1, 3, 0, 2])
THIRDS = [(0, 16), (16, 16), (32, 11)]
FSW = LEFT + PIECES * PTS + K
OUT_CH = [C, 2 * C]
QBUF = 5
LINE = list(range(2 * B * PIECES))
RANKS_LATER = [[0, 2, 4, 6, 8, 10], [1, 3, 5], [7, 12, 9], [14, 11, 13, 15]]
LATER_BANKS = [0, 1, 2, 3, 4, 5, 3, 4, 5, 3, 4, 7, 3, 4, 7, 3]
LATER_ORDER = sum(RANKS_LATER, [])
TAIL_AT = [LINE.index(PIECES * i + PIECES - 1) + 4 for i in range(2 * B)]
TAIL_AT[B] += 2
HALF_AT = {t: [] for t in range(TAIL_AT[-1] + 1)}
for i, t in enumerate((0, 0, 1, 2, 2, 3)):
    HALF_AT[LINE.index(PIECES * B + 1) + 4 + t].append((B, *divmod(i, 3)))
HALF_AT[TAIL_AT[B] + 1] = [(2 * B - 1, 0, i) for i in range(3)]
FEATURES_AT = [2] + TAIL_AT[:B]
LAST_STEP = TAIL_AT[-1]
WINDOWS_AT = [[g for g in range(2, STEPS)
               if max(LINE.index(g) - (2 if g % PIECES else 1), 0 if g < PIECES else FEATURES_AT[g // PIECES - 1]) == t]
              for t in range(LAST_STEP + 1)]


def piece_at(t):
    return LINE[t] if 0 <= t < len(LINE) else None


def pieces_up_to(t):
    return sum(g is not None for g in LINE[:max(t + 1, 0)])


def fresh(t):
    ahead = piece_at(t + 1)
    return t in FEATURES_AT and ahead is not None and ahead == PIECES * (1 + FEATURES_AT.index(t))


def value_chunks(g):
    first = B * PIECES
    return 3 * min(g, first) + 6 * max(0, g - first)


F = 1248
FCH = [(i * P, min(P, F - i * P)) for i in range((F + P - 1) // P)]
NF = len(FCH)
FBANKS = [(0, 512, 0), (512, 512, 4), (1024, F - 1024, 8)]
S = 128
G = 6
E = 8
R = 16
T = B * C
CAP = int(3.0 * T / E)
EPS = 1e-5
SCALE = float(1.0 / 32 ** 0.5)
CONST_WIDTHS = [("own", PB), ("i10", K), ("negblk", P), ("posblk", P), ("eps", 1), ("nhalf", 1), ("point", 32),
                ("digit_w", 16), ("rep", P), ("mean0", P), ("mean1", P), ("ones", P), ("off", PB)]
CONST_AT = {name: (sum(w for _, w in CONST_WIDTHS[:i]), w) for i, (name, w) in enumerate(CONST_WIDTHS)}
CONST_W = sum(w for _, w in CONST_WIDTHS)


def gate_up(banks, j):
    n = FBANKS[j][1]
    if j == 2:
        return banks[6][0:T, 0:n], banks[6][0:T, n:2 * n]
    return banks[2 + 2 * j][0:T, 0:n], banks[3 + 2 * j][0:T, 0:n]


def perceiver_layer(nc, x, coords, consts, ident, wlin, wconv, blin, wc3, upgate, local, fuse, gate, up, ffn2a, ffn2b,
                    moe1, moe2, moe3, rowc, gw2, out):
    ctx = ExitStack()
    with ctx:
        def sb(name, shape, dt=F32):
            return ctx.enter_context(nc.sbuf_tensor(name, shape, dt))

        def sem(name):
            return ctx.enter_context(nc.semaphore(name))

        def view(t, p0, np_, off, dims):
            base = t[p0:p0 + np_, :]
            return bass.AP(base.tensor, base.offset + off, [list(base.ap[0])] + [list(d) for d in dims])

        cst = sb("cst", [P, CONST_W])

        def const(name):
            a, w = CONST_AT[name]
            return cst[:, a:a + w]

        id_sb = sb("id_sb", [P, P])
        iota16 = sb("iota16", [P, N], F16)
        negones = const("negblk")
        posones = const("posblk")

        x_sb = sb("x_sb", [C, B, N])
        co_sb = sb("co_sb", [6, N])
        wlin_sb = sb("wlin_sb", [64, 2, 256])
        wconv_sb = sb("wconv_sb", [64, 2, 128])
        blin_sb = sb("blin_sb", [64, 2])
        wc3_sb = sb("wc3_sb", [64, 3, C])
        upgate_sb = sb("upgate_sb", [P, NK, 2 * S])
        local_sb = sb("local_sb", [P, 1 + G])
        gate_sb = sb("gate_sb", [P, NK, F])
        rowc_sb = sb("rowc_sb", [T, 3 * 32 + E + E])
        gw2_sb = sb("gw2_sb", [32, E])
        oh = sb("oh", [P, B * NK * M * N], BF16)
        qbd = sb("qbd", [P, 2 * BLOCKS * P], F16)
        vt = sb("vt", [P, 2 * 2 * COLS])
        hs = sb("hs", [P, 2 * PTS * K])
        qc = sb("qc", [P, QBUF * COLS], F16)
        wv = sb("wv", [P, 3 * 3 * P], BF16)
        wparts = sb("wparts", [P, 3 * 96], BF16)
        gs = sb("gs", [P, NK * P])
        fs = sb("fs", [P, B * FSW])
        f4 = sb("f4", [P, B * PIECES * PTS])
        f16h = sb("f16h", [P, N], F16)
        f16f = sb("f16f", [P, PIECES * PTS])
        sc = sb("sc", [P, 2 * NC])
        mx = sb("mx", [P, BLOCKS])
        md = sb("md", [P, NC])
        ex = sb("ex", [P, NC])
        lr = sb("lr", [P, NC])
        pn = sb("pn", [P, NC])
        px = sb("px", [P, 2 * COLS])
        hm = sb("hm", [P, 2 * PTS])
        hn = sb("hn", [P, 2 * PTS])
        gc = sb("gc", [P, B * 2 * PTS])
        hb = sb("hb", [P, 2 * PTS])
        hu = sb("hu", [P, 2 * PTS])
        bst = sb("bst", [P, 7 * 6])
        bsm = sb("bsm", [P, 2 * 3 * 6])
        mv = sb("mv", [P, 16])
        wn_sb = sb("wn_sb", [P, 2, 64])
        wnb = sb("wnb", [P, 96])
        bv_sb = sb("bv_sb", [P, 2])
        ft = [sb("ft0", [C, B, N]), sb("ft1", [C, B, N]), sb("ft2", [2 * C, B, N])]
        frest = sb("frest", [P, 2 * P])
        fpartb = sb("fpartb", [P, 3 * P], BF16)
        qv = sb("qv", [P, 3 * 24])
        qvi = sb("qvi", [P, 24], I32)
        rhs2 = sb("rhs2", [P, N], BF16)
        rk = sb("rk", [P, 32])
        sg = sb("sg", [P, 24])
        qs = sb("qs", [6, 8])
        px_halves = px[:, :].bitcast(BF16)
        src2, *junk = (px_halves[:, i * N:(i + 1) * N] for i in range(3))
        junk_sign = [gs[:, 0:256].bitcast(BF16), gs[:, 256:512].bitcast(BF16)]
        kx = px[:, 1536:1632].bitcast(I32)
        kt = px[:, 1632:2016].bitcast(I32)
        hx = px[:, 2176:2176 + 16 * 16].bitcast(I32)
        A, Z2, T1, A_NEXT, W, X2, X1, X0, D0, Y0, M2, M1, M0, T2 = 0, 3, 5, 6, 7, 7, 8, 9, 10, 11, 12, 13, 14, 15
        dg = px[:, 2016:2016 + NK * 40]
        lw = [t[:, 0:8 * 256].bitcast(BF16) for t in (vt, hs)]

        def laid_over(t, *shapes):
            at, tiles = 0, []
            for parts, *dims in shapes:
                w = 1
                for d in dims:
                    w *= d
                v = t[0:parts, at:at + w]
                tiles.append(v if len(dims) == 1 else v.rearrange("p (a b) -> p a b", a=dims[0]))
                at += w
            return tiles

        moe1_w = E * R + 32
        fuse_sb, moe2_sb, moe3_sb, moe1_sb = laid_over(oh[:, :].bitcast(F32), (P, (G + 1) * N), (P, NK * N), (P, N),
                                                       (P, NK * moe1_w))
        up_sb, = laid_over(qbd[:, :].bitcast(F32), (P, NK * F))
        ffn2_sb, = laid_over(vt, (P, NF * N))
        act_rows, sig, hT, tT = laid_over(hs, (T, F), (T, 512), (32, T), (P, T))
        x2, xn2, mo, gp = laid_over(px, (T, N), (T, N), (T, N), (P, 12 * T))
        x1, = laid_over(f4, (T, N))
        h3, = laid_over(fs, (T, N))
        xr, = laid_over(gs, (T, N))
        xnT, = laid_over(f16h[:, :].bitcast(F32), (P, NK, T))
        actT, = laid_over(qc[:, :].bitcast(F32), (P, NF, T))
        edf = sb("edf", [P, G])
        rst = sb("rst", [T, 16])

        s_ps = ctx.enter_context(nc.psum_tensor("s_ps", [P, 3 * 512], F32))
        v_ps = ctx.enter_context(nc.psum_tensor("v_ps", [P, 2 * 512], F32))
        mt_ps = ctx.enter_context(nc.psum_tensor("mt_ps", [P, 512], F32))
        r_ps = ctx.enter_context(nc.psum_tensor("r_ps", [P, 512], F32))
        z_ps = ctx.enter_context(nc.psum_tensor("z_ps", [P, 512], F32))

        banks = [s_ps[:, 0:512], s_ps[:, 512:1024], s_ps[:, 1024:1536], v_ps[:, 0:512], v_ps[:, 512:1024],
                 mt_ps[:, :], r_ps[:, :], z_ps[:, :]]

        def later_bank_at(i):
            return LATER_BANKS[LATER_ORDER.index(i)]

        def later_bank(i):
            return banks[later_bank_at(i)]

        ld_first = sem("ld_first")
        ld_const = sem("ld_const")
        ld_graph = sem("ld_graph")
        ld_ffn = sem("ld_ffn")
        ld_late = sem("ld_late")
        ld_down = sem("ld_down")
        ld_up = sem("ld_up")
        ld_x_rows = sem("ld_x_rows")
        stored = sem("stored")
        dve_step = sem("dve_step")
        act_step = sem("act_step")
        pool_step = sem("pool_step")
        pads_set = sem("pads_set")
        scaled_co = sem("scaled_co")
        co_turned = sem("co_turned")
        digits_ready = sem("digits_ready")
        digits_turned = sem("digits_turned")
        keys_ready = sem("keys_ready")
        weights_ready = sem("weights_ready")
        late_weights_ready = sem("late_weights_ready")
        diff_a_ready = sem("diff_a_ready")
        diff_d_ready = sem("diff_d_ready")
        counted_a = sem("counted_a")
        counted_d = sem("counted_d")
        onehot_ready = sem("onehot_ready")
        var_ready = sem("var_ready")
        rstd_ready = sem("rstd_ready")
        ft_ready = sem("ft_ready")
        ft_turned = sem("ft_turned")
        parts_ready = sem("parts_ready")
        wv_ready = sem("wv_ready")
        turned_ready = sem("turned_ready")
        gathered = sem("gathered")
        rep_ready = sem("rep_ready")
        rep_used = sem("rep_used")
        sorted_ready = sem("sorted_ready")
        fs_ready = sem("fs_ready")
        fold_ready = sem("fold_ready")
        q_ready = sem("q_ready")
        q_first_ready = sem("q_first_ready")
        bd_act_ready = sem("bd_act_ready")
        bd_dve_ready = sem("bd_dve_ready")
        s_ready = sem("s_ready")
        max_ready = sem("max_ready")
        md_ready = sem("md_ready")
        mt_ready = sem("mt_ready")
        sub_ready = sem("sub_ready")
        exp_ready = sem("exp_ready")
        sum_ready = sem("sum_ready")
        log_ready = sem("log_ready")
        logit_ready = sem("logit_ready")
        spread_ready = sem("spread_ready")
        part0_ready = sem("part0_ready")
        v_ready = sem("v_ready")
        vt_ready = sem("vt_ready")
        h_ready = sem("h_ready")
        hs_ready = sem("hs_ready")
        hs_used = sem("hs_used")
        gc_used = sem("gc_used")
        centre_ready = sem("centre_ready")
        gc_ready = sem("gc_ready")
        stat_in = sem("stat_in")
        stat_mean = sem("stat_mean")
        h3_ready = sem("h3_ready")
        xn_ready = sem("xn_ready")
        xn_turned = sem("xn_turned")
        xnT_ready = sem("xnT_ready")
        gp_ready = sem("gp_ready")
        edf_ready = sem("edf_ready")
        tmp_ready = sem("tmp_ready")
        gu_ready = sem("gu_ready")
        gu_exp = sem("gu_exp")
        gu_used = sem("gu_used")
        act_in = sem("act_in")
        actT_ready = sem("actT_ready")
        y_ready = sem("y_ready")
        xn2_ready = sem("xn2_ready")
        xn2_turned = sem("xn2_turned")
        xn2T_ready = sem("xn2T_ready")
        moe_h = sem("moe_h")
        moe_relu = sem("moe_relu")
        moe_relu_turned = sem("moe_relu_turned")
        moe_hT = sem("moe_hT")
        moe_gates = sem("moe_gates")
        top_exp_in = sem("top_exp_in")
        top_exp = sem("top_exp")
        picks_ready = sem("picks_ready")
        counts_ready = sem("counts_ready")
        lora_ready = sem("lora_ready")
        lora_turned = sem("lora_turned")
        lora_T = sem("lora_T")
        moe_out = sem("moe_out")
        y_out = sem("y_out")

        block = ctx.enter_context(nc.Block())

        def wait_features(eng, g):
            eng.wait_ge(fs_ready, 2 * (g // PIECES + 1))
            if g >= QBUF:
                eng.wait_ge(bd_act_ready, 2 * (g - QBUF + 1))
                eng.wait_ge(bd_dve_ready, 2 * (g - QBUF + 1))
                eng.wait_ge(v_ready, value_chunks(g - QBUF + 1))

        def windows_of(eng, g):
            lb, q = divmod(g, PIECES)
            b, first = lb % B, q * PTS
            near = view(fs, 0, P, b * FSW + first, [[PB, BLOCKS], [1, PB], [1, K]])
            mid = view(f4, 0, P, b * PIECES * PTS + first, [[PB, BLOCKS], [1, PB], [0, K]])
            dst = view(qc, 0, P, (g % QBUF) * COLS, [[SLOT, BLOCKS], [K, PB], [1, K]])
            return eng.tensor_tensor(dst, near, mid, ALU.subtract)

        def wait_windows(eng, g):
            lb, q = divmod(g, PIECES)
            if q:
                eng.wait_ge(q_ready, (PIECES - 1) * lb + q)
            else:
                eng.wait_ge(q_first_ready, lb + 1)

        @block.sync
        def _(sp):
            sp.dma_start(co_sb[:], coords).then_inc(ld_first, 16)
            sp.dma_start(x_sb[:], x).then_inc(ld_first, 16)
            sp.dma_start(id_sb[:], ident).then_inc(ld_first, 16)
            sp.dma_start(cst[:], consts).then_inc(ld_const, 16)
            sp.dma_start(wlin_sb[:], wlin).then_inc(ld_graph, 16)
            sp.dma_start(wconv_sb[:], wconv).then_inc(ld_graph, 16)
            sp.dma_start(blin_sb[:], blin).then_inc(ld_graph, 16)
            sp.dma_start(wc3_sb[:], wc3).then_inc(ld_graph, 16)
            sp.dma_start(upgate_sb[:], upgate).then_inc(ld_ffn, 16)
            sp.dma_start(local_sb[:], local).then_inc(ld_ffn, 16)
            sp.dma_start(gate_sb[:], gate).then_inc(ld_ffn, 16)
            sp.dma_start(rowc_sb[:], rowc).then_inc(ld_ffn, 16)
            sp.dma_start(gw2_sb[:], gw2).then_inc(ld_ffn, 16)
            sp.wait_ge(gathered, 4)
            sp.dma_start(fuse_sb, fuse).then_inc(ld_late, 16)
            sp.dma_start(moe1_sb, moe1).then_inc(ld_late, 16)
            sp.dma_start(moe2_sb, moe2).then_inc(ld_late, 16)
            sp.dma_start(moe3_sb, moe3).then_inc(ld_late, 16)
            sp.wait_ge(sorted_ready, 2 * B)
            for b in range(B):
                sp.dma_start(xr[b * C:b * C + C, :], x[:, b, :]).then_inc(ld_x_rows, 16)
            sp.wait_ge(s_ready, STEPS)
            sp.dma_start(up_sb, up).then_inc(ld_up, 16)
            sp.wait_ge(h_ready, 3 * STEPS)
            sp.dma_start(ffn2_sb[:, 0:(NF - 1) * N], ffn2a).then_inc(ld_down, 16)
            sp.dma_start(ffn2_sb[0:FCH[-1][1], (NF - 1) * N:NF * N], ffn2b).then_inc(ld_down, 16)
            sp.wait_ge(y_out, 1)
            sp.dma_start(out, xn2).then_inc(stored, 16)
            sp.wait_ge(stored, 16)

        @block.gpsimd
        def _(pool):
            step = [0]

            def link(ins):
                step[0] += 1
                ins.then_inc(pool_step, 1)
                pool.wait_ge(pool_step, step[0])

            pool.memset(bst[:], 0.0).then_inc(pads_set, 1)
            pool.memset(bsm[:], 0.0).then_inc(pads_set, 1)
            pool.iota(iota16[:], [[1, N]], base=0, channel_multiplier=0,
                      allow_small_or_imprecise_dtypes=True).then_inc(pads_set, 1)
            pool.memset(src2, 0.0).then_inc(pads_set, 1)
            pool.memset(rhs2[:], 0.0).then_inc(pads_set, 1)
            pool.memset(wv[:], 0.0).then_inc(pads_set, 1)
            pool.memset(fs[:], 0.0).then_inc(pads_set, 1)
            pool.memset(f4[:], 0.0).then_inc(pads_set, 1)
            pool.memset(f16f[:], 0.0).then_inc(pads_set, 1)
            pool.memset(qc[:].bitcast(F32), 0.0).then_inc(pads_set, 1)
            pool.memset(qbd[:].bitcast(F32), 0.0).then_inc(pads_set, 1)
            pool.wait_ge(ld_const, 16)

            def rstd(n, col, np_):
                pool.wait_ge(var_ready, n + 1)
                t, w = col
                link(pool.tensor_tensor(t, t, eps_of(np_, w), ALU.add))
                pool.tensor_tensor(t, t, half_of(np_, w), ALU.pow).then_inc(rstd_ready, 1)

            def eps_of(np_, w):
                return view(cst, 0, np_, CONST_AT["eps"][0], [[0, w]])

            def half_of(np_, w):
                return view(cst, 0, np_, CONST_AT["nhalf"][0], [[0, w]])

            def windows(g):
                wait_features(pool, g)
                windows_of(pool, g).then_inc(q_ready, 1)

            def spread_max(g):
                pool.wait_ge(max_ready, g + 1)
                if g >= 1:
                    pool.wait_ge(mt_ready, g)
                pool.tensor_tensor(view(md, 0, P, 0, [[K, BLOCKS], [1, K]]),
                                   view(mx, 0, P, 0, [[1, BLOCKS], [0, K]]),
                                   view(cst, 0, P, CONST_AT["i10"][0], [[0, BLOCKS], [1, K]]),
                                   ALU.mult).then_inc(md_ready, 1)

            rstd(0, (mv[0:C, 1:4:2], 2), C)
            pool.wait_ge(keys_ready, 1)
            for i in range(2 * M):
                at = CONST_AT["digit_w"][0] + (i % 2) * B * M + M + i // 2
                pool.tensor_scalar(lw[1][:, i * N:(i + 1) * N], src2, cst[:, at:at + 1], None, ALU.mult)\
                    .then_inc(late_weights_ready, 1)
            windows(1)
            for t in range(LAST_STEP + 1):
                if piece_at(t - 1) is not None and t not in TAIL_AT[:B]:
                    spread_max(piece_at(t - 1))
                if t in TAIL_AT:
                    rstd(1 + TAIL_AT.index(t), (mv[:, 3:4], 1), P)
                if t in TAIL_AT[:B]:
                    spread_max(piece_at(t - 1))
                for g in WINDOWS_AT[t]:
                    if g % PIECES:
                        windows(g)
            for i, col in enumerate((11, 13, 1, 3)):
                rstd(5 + i, (rst[:, col:col + 1], 1), T)

        @block.scalar
        def _(act):
            nc.scalar.preload_act_table_set("natural_log_exp_and_others")
            step = [0]

            def link(ins):
                step[0] += 1
                ins.then_inc(act_step, 1)
                act.wait_ge(act_step, step[0])

            counted = [0]

            def count_smaller(i, bank):
                n = counted[0]
                act.wait_ge(diff_a_ready, n + 1)
                if n >= 2:
                    act.wait_ge(counted_a, n - 1)
                act.activation(junk_sign[n % 2], bank, ACT.Sign, accum_out=sg[:, i:i + 1]).then_inc(counted_a, 1)
                counted[0] += 1

            def repeated_features(lb):
                b = lb % B
                act.wait_ge(rep_ready, lb + 1)
                if lb >= 2:
                    act.wait_ge(q_ready, (PIECES - 1) * (lb - 1))
                    act.wait_ge(q_first_ready, lb - 1)
                    act.wait_ge(centre_ready, lb - 1)
                at = b * PIECES * PTS
                act.activation(f4[:, at:at + N], r_ps[:, :], ACT.Copy).then_inc(rep_used, 1)
                link(act.activation(f16h[:], r_ps[:, :], ACT.Copy))
                act.activation(f16f[:, 0:N], f16h[:], ACT.Copy).then_inc(rep_used, 1)

            def sorted_features(lb):
                b = lb % B
                act.wait_ge(gathered, lb + 1)
                if lb < 2:
                    act.wait_ge(counted_a, (8 + len(RANKS_LATER[0]), 16)[lb])
                act.activation(view(gs, 0, P, 0, [[P, NK], [1, M], [M, C]]),
                               view(z_ps, 0, P, 0, [[P, NK], [C, M], [1, C]]), ACT.Copy).then_inc(turned_ready, 1)
                act.wait_ge(sorted_ready, lb + 1)
                at = b * FSW
                act.activation(fs[:, at + LEFT:at + LEFT + N], z_ps[:, :], ACT.Copy).then_inc(fs_ready, 1)
                act.activation(fs[:, at + LEFT + N:at + FSW], view(z_ps, 0, P, N - 1, [[0, FSW - LEFT - N]]),
                               ACT.Copy).then_inc(fs_ready, 1)

            def centre_part(lb):
                b = lb % B
                act.wait_ge(centre_ready, lb + 1)
                if lb >= 2:
                    act.wait_ge(gc_used, lb - 1)
                w = 2 * PTS if lb >= B else PTS
                act.activation(gc[:, b * 2 * PTS:b * 2 * PTS + w], z_ps[:, 0:w], ACT.Copy).then_inc(gc_ready, 1)

            def front(g, h):
                wait_windows(act, g)
                if g >= 2:
                    act.wait_ge(s_ready, g - 1)
                act.activation(view(qbd, 32 * h, 32, (g % 2) * BLOCKS * P + 32 * h, [[P, BLOCKS], [1, SLOT]]),
                               view(qc, 32 * h, 32, (g % QBUF) * COLS, [[SLOT, BLOCKS], [1, SLOT]]),
                               ACT.Copy).then_inc(bd_act_ready, 1)

            def first_of_three(g):
                act.wait_ge(s_ready, g + 1)
                if g >= 2:
                    act.wait_ge(logit_ready, g - 1)
                o = CONST_AT["own"][0]
                act.activation(view(sc, 0, P, (g % 2) * NC, [[K, BLOCKS], [1, K]]),
                               view(s_ps, 0, P, 0, [[SLOT, BLOCKS], [1, K]]), ACT.Copy,
                               scale=cst[:, o:o + 1]).then_inc(part0_ready, 1)

            def exps(g):
                act.wait_ge(sub_ready, g + 1)
                if g >= 1:
                    act.wait_ge(sum_ready, g)
                act.activation(ex[:], sc[:, (g % 2) * NC:(g % 2) * NC + NC], ACT.Exp, scale=SCALE)\
                   .then_inc(exp_ready, 1)

            def logs(g):
                act.wait_ge(sum_ready, g + 1)
                if g >= 1:
                    act.wait_ge(logit_ready, g)
                act.activation(lr[:], r_ps[:, 0:NC], ACT.Ln).then_inc(log_ready, 1)

            def probabilities(g):
                act.wait_ge(logit_ready, g + 1)
                if g >= 2:
                    act.wait_ge(h_ready, 3 * (g - 1))
                o = CONST_AT["off"][0]
                for j in range(PB):
                    act.activation(view(px, 0, P, (g % 2) * COLS + j * K, [[SLOT, BLOCKS], [1, K]]),
                                   view(pn, 0, P, 0, [[K, BLOCKS], [1, K]]), ACT.Exp,
                                   bias=cst[:, o + j:o + j + 1]).then_inc(spread_ready, 1)

            def evacuate(g, j):
                lb, q = divmod(g, PIECES)
                oc = OUT_CH[lb // B]
                side = P // oc
                t0, n = THIRDS[j]
                half = q // side if lb >= B else lb
                if lb >= B and q % side == 0 and j == 0:
                    act.wait_ge(hs_used, 2 * (lb - B) + 1 + half)
                p0 = oc * (q % side)
                act.wait_ge(h_ready, 3 * g + j + 1)
                o = half * PTS * K + t0 * PB * K
                act.activation(hs[p0:p0 + oc, o:o + n * PB * K], z_ps[p0:p0 + oc, 0:n * PB * K], ACT.Copy)\
                   .then_inc(hs_ready, 1)

            for i in range(8):
                count_smaller(i, banks[2 * i % 7])
            act.wait_ge(pads_set, 11)
            repeated_features(0)
            for i in RANKS_LATER[0]:
                count_smaller(8 + i // 2, later_bank(i))
            sorted_features(0)
            centre_part(0)
            for h in range(2):
                front(0, h)
            for t in range(LAST_STEP + 1):
                ahead, now, last, second, third = (piece_at(t + i) for i in (1, 0, -1, -2, -3))
                feats = 1 + FEATURES_AT.index(t) if t in FEATURES_AT else None
                if last is not None and last > 0:
                    first_of_three(last)
                if second is not None and not (t - 1 in FEATURES_AT and t - 1 not in TAIL_AT):
                    logs(second)
                if t - 1 == FEATURES_AT[0]:
                    sorted_features(1)
                for j in range(2):
                    if third is not None:
                        evacuate(third, j)
                    if fresh(t - 1):
                        front(now, j)
                if second is not None:
                    probabilities(second)
                urgent = feats and t in TAIL_AT
                if urgent:
                    evacuate(third, 2)
                    repeated_features(feats)
                    sorted_features(feats)
                if last is not None:
                    exps(last)
                if third is not None and not urgent:
                    evacuate(third, 2)
                if t == 0:
                    first_of_three(now)
                if ahead is not None and not fresh(t):
                    front(ahead, 0)
                    front(ahead, 1)
                if feats and not urgent:
                    logs(last)
                    repeated_features(feats)
                if t < 2:
                    for i in RANKS_LATER[2 + t]:
                        if i % 2 == 0:
                            count_smaller(8 + i // 2, later_bank(i))
                if urgent:
                    centre_part(feats)
                elif t - 1 == FEATURES_AT[0]:
                    centre_part(1)
            act.wait_ge(xn_turned, 1)
            act.activation(xnT, view(banks[2], 0, P, 0, [[T, NK], [1, T]]), ACT.Copy).then_inc(xnT_ready, 1)

            act.wait_ge(ld_ffn, 80)
            act.activation(edf[:], local_sb[:, 1:1 + G], ACT.Exp, scale=-1.0).then_inc(edf_ready, 1)
            for j, (_, n, _) in enumerate(FBANKS):
                act.wait_ge(gu_ready, j + 1)
                if j >= 1:
                    act.wait_ge(gu_used, j)
                act.activation(sig[:, 0:n], gate_up(banks, j)[0], ACT.Exp, scale=-1.0).then_inc(gu_exp, 1)
            act.wait_ge(top_exp_in, 1)
            act.activation(mo[:, 200:201], mo[:, 199:200], ACT.Exp).then_inc(top_exp, 1)

        @block.vector
        def _(dve):
            step = [0]

            def link(ins):
                step[0] += 1
                ins.then_inc(dve_step, 1)
                dve.wait_ge(dve_step, step[0])

            def mark(ins):
                step[0] += 1
                ins.then_inc(dve_step, 1)

            def settle():
                dve.wait_ge(dve_step, step[0])

            v = dve
            norm = [0]

            def wait_rstd():
                norm[0] += 1
                dve.wait_ge(rstd_ready, norm[0])

            dve.wait_ge(ld_first, 48)
            lo, hi, rng, rc, sca, er = (qs[:, i:i + 1] for i in range(6))
            link(v.tensor_reduce(lo, co_sb[:], AX, ALU.min))
            link(v.tensor_reduce(hi, co_sb[:], AX, ALU.max))
            link(v.tensor_tensor(rng, hi, lo, ALU.subtract))
            link(v.tensor_scalar(rng, rng, 1e-6, None, ALU.add))
            link(v.reciprocal(rc, rng))
            link(v.tensor_scalar(sca, rc, float(2 ** BITS - 1), None, ALU.mult))
            v.tensor_scalar(co_sb[:], co_sb[:], lo, sca, ALU.subtract, ALU.mult).then_inc(scaled_co, 1)

            def ln_stats(src):
                for b in range(B):
                    link(v.bn_stats(bst[0:C, 6 * b:6 * b + 6], src[:, b, :]))
                    v.bn_aggr(mv[0:C, 2 * b:2 * b + 2], bst[0:C, 6 * b:6 * b + 6]).then_inc(
                        var_ready if b == B - 1 else dve_step, 1)
                    if b < B - 1:
                        step[0] += 1
                        dve.wait_ge(dve_step, step[0])

            dve.wait_ge(pads_set, 1)
            ln_stats(x_sb)

            dve.wait_ge(co_turned, 1)
            vq, vf, vg = (qv[:, 24 * i:24 * i + 24] for i in range(3))
            link(v.tensor_copy(vq, z_ps[:, 0:24]))
            link(v.tensor_copy(qvi[:], vq))
            link(v.tensor_copy(vf, qvi[:]))
            link(v.tensor_tensor(vg, vf, vq, ALU.is_gt))
            link(v.tensor_tensor(vf, vf, vg, ALU.subtract))
            link(v.tensor_scalar(vf, vf, 0.0, float(2 ** BITS - 1), ALU.max, ALU.min))
            def slot(i, n=1):
                return hx[:, 16 * i:16 * (i + n)]

            def slots(first, step_, n):
                return view(hx, 0, P, 16 * first, [[16 * step_, n], [1, 16]])

            def repeated(i, n):
                return view(hx, 0, P, 16 * i, [[0, n], [1, 16]])

            for c in range(3):
                for o in range(2):
                    d = c if c == 2 else c ^ o
                    src = view(qv, 0, P, 24 + d, [[3, B], [6, NK]])
                    mark(v.tensor_copy(view(kx, 0, P, 32 * (2 - c) + 8 * o, [[4, B], [1, NK]]), src))
                    mark(v.tensor_copy(view(hx, 0, P, 16 * (X2 + 2 - c) + 8 * o, [[4, B], [1, NK]]), src))
            settle()

            hilbert = view(kx, 0, P, 16, [[32, 3], [1, 16]])
            for b in range(BITS - 1, -1, -1):
                bit = slots(X2, 1, 3)
                if b == BITS - 1:
                    mark(v.tensor_scalar(hilbert, bit, 1 << b, None, ALU.bitwise_and))
                else:
                    mark(v.scalar_tensor_tensor(hilbert, bit, 1 << b, hilbert, ALU.bitwise_and, ALU.bitwise_or))
                if b == 0:
                    settle()
                    break
                if b == BITS - 1:
                    mark(v.tensor_tensor(slot(Y0), slot(X0), slot(X2), ALU.bitwise_xor))
                mark(v.tensor_tensor(slot(D0), slot(X0), slot(X1), ALU.bitwise_xor))
                link(v.tensor_scalar(slots(M2, 1, 3), bit, 31 - b, 31, ALU.logical_shift_left, ALU.arith_shift_right))
                mark(v.tensor_tensor(slots(Z2, 1, 2), slots(X2, 1, 2), slots(M2, 1, 2), ALU.bitwise_xor))
                link(v.tensor_tensor(slots(A, 1, 3), slots(X0, 1, 3), repeated(M0, 3), ALU.bitwise_xor))
                link(v.tensor_tensor(slot(T1), slot(A + 1), slot(M1), ALU.bitwise_or))
                link(v.tensor_tensor(slots(A_NEXT, 1, 3), slots(A, 2, 3), repeated(T1, 3), ALU.bitwise_xor))
                mark(v.tensor_tensor(slot(Y0), slot(A_NEXT), slot(Z2), ALU.bitwise_xor))
                link(v.tensor_tensor(slot(T2), slot(W), slot(M2), ALU.bitwise_or))
                link(v.tensor_tensor(slots(X2, 2, 2), slots(Z2, 3, 2), repeated(T2, 2), ALU.bitwise_xor))
            X = [kx[:, 32 * (2 - c) + 16:32 * (2 - c) + 32] for c in range(3)]
            ma, mb = kt[:, 0:16], kt[:, 32:48]
            link(v.tensor_tensor(X[1], X[1], X[0], ALU.bitwise_xor))
            link(v.tensor_tensor(X[2], X[2], X[1], ALU.bitwise_xor))
            link(v.tensor_scalar(ma, X[2], 1, None, ALU.logical_shift_right))
            for sh in (1, 2, 4, 8):
                link(v.scalar_tensor_tensor(mb, ma, sh, ma, ALU.logical_shift_right, ALU.bitwise_xor))
                ma, mb = mb, ma
            at = ma.offset - kt.offset
            link(v.tensor_tensor(hilbert, hilbert, view(kt, 0, P, at, [[0, 3], [1, 16]]), ALU.bitwise_xor))
            ka, kb = kx, kt[:, 96:192]
            for sh, mask in ((16, 0x030000FF), (8, 0x0300F00F), (4, 0x030C30C3), (2, 0x09249249)):
                link(v.scalar_tensor_tensor(kb, ka, sh, ka, ALU.logical_shift_left, ALU.bitwise_or))
                link(v.tensor_scalar(ka, kb, mask, None, ALU.bitwise_and))
            key, ky2 = kt[:, 0:32], kt[:, 32:64]
            link(v.scalar_tensor_tensor(ky2, kx[:, 64:96], 1, kx[:, 32:64], ALU.logical_shift_left, ALU.bitwise_or))
            link(v.scalar_tensor_tensor(key, ky2, 1, kx[:, 0:32], ALU.logical_shift_left, ALU.bitwise_or))
            dve.wait_ge(ld_const, 16)
            low14 = kt[:, 64:96]
            link(v.tensor_scalar(low14, key, 0x3FFF, 9, ALU.bitwise_and, ALU.logical_shift_left))
            link(v.tensor_tensor(low14, low14, const("point").bitcast(I32), ALU.bitwise_or))
            digs = [(low14, 0, 255), (low14, 8, 255), (low14, 16, 127), (key, 14, 255), (key, 22, 255)]
            for i, (src, sh, mask) in enumerate(digs):
                mark(v.tensor_scalar(kt[:, 96 + 32 * i:128 + 32 * i], src, sh, mask,
                                     ALU.logical_shift_right, ALU.bitwise_and))
            settle()
            for i in range(5):
                ins = v.tensor_copy(view(dg, 0, P, 8 * i, [[1, M], [4, B], [40, NK]]),
                                    view(kt, 0, P, 96 + 32 * i, [[8, M], [4, B], [1, NK]]))
                if i < 4:
                    mark(ins)
            settle()
            ins.then_inc(digits_ready, 1)

            dve.wait_ge(fold_ready, 1)
            for l in range(2):
                oc = OUT_CH[l]
                mark(v.tensor_copy(wn_sb[:, l, 0:oc], r_ps[:, 192 * l:192 * l + oc]))
                mark(v.tensor_copy(bv_sb[:, l:l + 1], r_ps[:, 192 * l + 128:192 * l + 129]))
                mark(v.tensor_copy(wnb[:, 32 * l:32 * l + oc], r_ps[:, 192 * l + 64:192 * l + 64 + oc]))

            dve.wait_ge(digits_turned, 1)
            dve.wait_ge(pads_set, 5)
            mark(v.tensor_scalar(rhs2[64:128, :], rhs2[64:128, :], 1.0, None, ALU.add))
            link(v.tensor_copy(rhs2[0:40, :], z_ps[0:40, :]))
            mark(v.tensor_copy(src2[64:104, :], rhs2[0:40, :]))
            settle()
            v.tensor_scalar(src2[0:40, :], src2[0:40, :], 1.0, None, ALU.add).then_inc(keys_ready, 1)
            dve.wait_ge(keys_ready, 1)

            for i in range(2 * M):
                m, part = divmod(i, 2)
                at = CONST_AT["digit_w"][0] + part * B * M + m
                v.tensor_scalar(lw[0][:, i * N:(i + 1) * N], src2, cst[:, at:at + 1], None, ALU.mult)\
                 .then_inc(weights_ready, 1)

            def ln_apply(dst, src):
                wait_rstd()
                for b in range(B):
                    yield v.tensor_scalar(dst[:, b, :], src[:, b, :], mv[0:C, 2 * b:2 * b + 1],
                                          mv[0:C, 2 * b + 1:2 * b + 2], ALU.subtract, ALU.mult)

            for ins in ln_apply(ft[0], x_sb):
                ins.then_inc(ft_ready, 1)

            def split(parts, rest, src):
                link(v.tensor_copy(parts[0], src))
                link(v.tensor_tensor(rest[0], src, parts[0], ALU.subtract))
                link(v.tensor_copy(parts[1], rest[0]))
                link(v.tensor_tensor(rest[1], rest[0], parts[1], ALU.subtract))
                return v.tensor_copy(parts[2], rest[1])

            def split_features(lb):
                dve.wait_ge(ft_turned, lb + 1)
                if lb >= 1:
                    dve.wait_ge(gathered, lb)
                split([fpartb[:, i * P:(i + 1) * P] for i in range(3)], [frest[:, i * P:(i + 1) * P] for i in range(2)],
                      z_ps[:, 0:P]).then_inc(parts_ready, 1)

            counted = [0]

            def count_below(i, bank):
                n = counted[0]
                dve.wait_ge(diff_d_ready, n + 1)
                if n >= 2:
                    dve.wait_ge(counted_d, n - 1)
                v.tensor_scalar(junk[n % 2], bank, 0.0, 0.0, ALU.is_lt, ALU.add,
                                accum_out=rk[:, i:i + 1]).then_inc(counted_d, 1)
                counted[0] += 1

            for i in range(8):
                count_below(2 * i + 1, banks[(2 * i + 1) % 7])
                if i == 2:
                    split_features(0)

            def one_hot(b):
                dve.wait_ge(counted_a, 8 * (b + 1))
                dve.wait_ge(counted_d, 8 * (b + 1))
                link(v.tensor_scalar(view(rk, 0, P, 16 * b, [[2, 8]]), sg[:, 8 * b:8 * b + 8], -0.5, (N - 1) / 2,
                                     ALU.mult, ALU.add))
                for m in range(M):
                    for k in range(NK):
                        i = (b * M + m) * NK + k
                        at = ((b * NK + k) * M + m) * N
                        v.tensor_scalar(oh[:, at:at + N], iota16[:], rk[:, i:i + 1], None, ALU.is_equal)\
                         .then_inc(onehot_ready, 1)

            def split_weights():
                link(split([wparts[:, i * 96:(i + 1) * 96] for i in range(3)],
                           [frest[:, i * P:i * P + 96] for i in range(2)], wnb[:]))
                for half in range(3):
                    for h in range(4):
                        v.tensor_copy(view(wv, 32 * h, 32, half * 3 * P + 32 * h, [[P, 3], [1, 32]]),
                                      view(wparts, 32 * h, 32, 32 * half, [[96, 3], [1, 32]])).then_inc(wv_ready, 1)

            def turn_values(g, third):
                if g >= 2:
                    dve.wait_ge(h_ready, 3 * (g - 1))
                halves = 1 + g // (B * PIECES)
                oc = OUT_CH[g // (B * PIECES)]
                t0, n = THIRDS[third]
                for half in range(halves):
                    c = value_chunks(g) + halves * third + half
                    dve.wait_ge(v_ready, c + 1)
                    at = (g % 2) * 2 * COLS + t0 * oc + half * SLOT
                    v.transpose(view(vt, 0, P, at, [[oc, n], [1, SLOT]]),
                                v_ps[:, (c % 2) * 512:(c % 2) * 512 + n * SLOT]).then_inc(vt_ready, 1)

            def compact(g):
                dve.wait_ge(part0_ready, g + 1)
                if g >= 1:
                    dve.wait_ge(md_ready, g)
                m0 = CONST_AT["own"][0]
                flat = view(sc, 0, P, (g % 2) * NC, [[K, BLOCKS], [1, K]])
                for j in (1, 2):
                    link(v.scalar_tensor_tensor(flat, view(s_ps, 0, P, j * K, [[SLOT, BLOCKS], [1, K]]),
                                                cst[:, m0 + j:m0 + j + 1], flat, ALU.mult, ALU.add))
                v.tensor_reduce(mx[:], flat, AX, ALU.max).then_inc(max_ready, 1)

            def subtract(g):
                dve.wait_ge(mt_ready, g + 1)
                own = sc[:, (g % 2) * NC:(g % 2) * NC + NC]
                v.tensor_tensor(own, own, mt_ps[:, 0:NC], ALU.add).then_inc(sub_ready, 1)

            def first_windows(g):
                b = g // PIECES % B
                wait_features(dve, g)
                link(windows_of(v, g))
                for i in range(LEFT):
                    w = LEFT - i
                    at = (g % QBUF) * COLS + (i // PB) * SLOT + (i % PB) * K
                    ins = v.tensor_tensor(view(qc, 0, P, at, [[1, w]]),
                                          view(fs, 0, P, b * FSW + LEFT + i + LEFT, [[0, w]]),
                                          view(f4, 0, P, b * PIECES * PTS + i, [[0, w]]), ALU.subtract)
                    if i < LEFT - 1:
                        mark(ins)
                settle()
                ins.then_inc(q_first_ready, 1)

            def front(g, h):
                wait_windows(dve, g)
                if g >= 2:
                    dve.wait_ge(s_ready, g - 1)
                v.tensor_copy(view(qbd, 32 * h, 32, (g % 2) * BLOCKS * P + 32 * h, [[P, BLOCKS], [1, SLOT]]),
                              view(qc, 32 * h, 32, (g % QBUF) * COLS, [[SLOT, BLOCKS], [1, SLOT]]))\
                 .then_inc(bd_dve_ready, 1)

            def logits(g):
                dve.wait_ge(log_ready, g + 1)
                if g >= 1:
                    dve.wait_ge(spread_ready, 3 * g)
                v.scalar_tensor_tensor(pn[:], sc[:, (g % 2) * NC:(g % 2) * NC + NC], SCALE, lr[:], ALU.mult,
                                       ALU.subtract).then_inc(logit_ready, 1)

            def records(layer, half, width, split_, short):
                last = half == layer
                for i in range(split_):
                    a = half * width + i * width // split_
                    z = half * width + (short if last and i == split_ - 1 else (i + 1) * width // split_)
                    yield P, a, z
                if last:
                    yield P - OUT_CH[layer], half * width + short, (half + 1) * width

            def tail_half(lb, half, parts=range(3)):
                l = lb // B
                if half == 0 and 0 in parts:
                    dve.wait_ge(ft_ready, 2 + lb)
                dve.wait_ge(hs_ready, 3 * PIECES * (lb + 1) - (6 if half < l else 0))
                at = (half if l else lb) * PTS * K
                pts = slice(half * PTS, half * PTS + PTS)
                for i, (t, op) in enumerate(((hm, ALU.max), (hb, ALU.add))):
                    if i in parts:
                        mark(v.tensor_reduce(t[:, pts], view(hs, 0, P, at, [[K, PTS], [1, K]]), AX, op))
                if 2 not in parts:
                    return
                shift = at - half * PTS * K
                for i, (np_, a, z) in enumerate(records(l, half, PTS * K, 3, PTS_LAST * K)):
                    n = 3 * half + i
                    ins = v.bn_stats(bst[0:np_, 6 * n:6 * n + 6], hs[0:np_, shift + a:shift + z])
                    if i < 2 + (half == l):
                        mark(ins)
                settle()
                ins.then_inc(hs_used, 1)
                dve.wait_ge(hs_used, lb + 1 if l == 0 else 2 * (lb - B) + 3 + half)

            def tail(lb):
                l, b = divmod(lb, B)
                halves = 1 + l
                w = halves * PTS
                dve.wait_ge(gc_ready, lb + 1)
                centre = gc[:, b * 2 * PTS:b * 2 * PTS + w]
                if lb != B:
                    tail_half(lb, l)
                link(v.scalar_tensor_tensor(hu[:, 0:w], hb[:, 0:w], 1.0 / K, centre, ALU.mult, ALU.add))
                for j, t in enumerate((hb, hu)):
                    n = 0
                    for half in range(halves):
                        for np_, a, z in records(l, half, PTS, 1, PTS_LAST):
                            mark(v.bn_stats(bsm[0:np_, 18 * j + 6 * n:18 * j + 6 * n + 6], t[0:np_, a:z]))
                            n += 1
                settle()
                mark(v.bn_aggr(mv[:, 10:12], bsm[:, 18:18 + 6 * n]))
                mark(v.bn_aggr(mv[:, 8:10], bsm[:, 0:6 * n]))
                link(v.bn_aggr(mv[:, 0:2], bst[:, 0:6 * (3 * halves + 1)]))
                v.tensor_copy(mv[:, 2:3], mv[:, 10:11]).then_inc(stat_in, 1)
                link(v.scalar_tensor_tensor(mv[:, 1:2], mv[:, 9:10], -1.0 / K ** 2, mv[:, 1:2], ALU.mult, ALU.add))
                mark(v.tensor_tensor(mv[:, 1:2], mv[:, 1:2], mv[:, 11:12], ALU.add))
                link(v.tensor_tensor(hm[:, 0:w], hm[:, 0:w], centre, ALU.add))
                v.tensor_scalar(hm[:, 0:w], hm[:, 0:w], bv_sb[:, l:l + 1], None, ALU.add).then_inc(gc_used, 1)

            def tail_mean(lb):
                dve.wait_ge(stat_mean, 2 * lb + 1)
                link(v.tensor_copy(mv[:, 4:5], mt_ps[:, 440:441]))
                link(v.tensor_tensor(mv[:, 5:6], mv[:, 10:11], mv[:, 4:5], ALU.subtract))
                v.scalar_tensor_tensor(mv[:, 2:3], mv[:, 5:6], mv[:, 5:6], mv[:, 1:2], ALU.mult, ALU.add)\
                 .then_inc(stat_in, 1)

            def tail_variance(lb):
                dve.wait_ge(stat_mean, 2 * lb + 2)
                v.tensor_copy(mv[:, 3:4], mt_ps[:, 440:441]).then_inc(var_ready, 1)
                link(v.tensor_tensor(mv[:, 4:5], mv[:, 4:5], bv_sb[:, lb // B:lb // B + 1], ALU.add))

            def tail_norm(lb):
                l, b = divmod(lb, B)
                w = (1 + l) * PTS
                wait_rstd()
                link(v.tensor_scalar(hn[:, 0:w], hm[:, 0:w], mv[:, 4:5], mv[:, 3:4], ALU.subtract, ALU.mult))
                oc = OUT_CH[l]
                for q in range(PIECES):
                    p0 = 32 * q if l == 0 else 64 * (q % 2)
                    o = 0 if l == 0 else (q // 2) * PTS
                    n = PTS if q < PIECES - 1 else PTS_LAST
                    src = hn[p0:p0 + oc, o:o + n]
                    ins = v.scalar_tensor_tensor(ft[l + 1][:, b, q * PTS:q * PTS + n], src, 0.2, src,
                                                 ALU.mult, ALU.max)
                    if q < PIECES - 1:
                        mark(ins)
                settle()
                ins.then_inc(ft_ready, 1)

            dve.wait_ge(pads_set, 6)
            one_hot(0)
            split_weights()
            first_windows(0)
            front(0, 2)
            front(0, 3)
            for i in RANKS_LATER[1]:
                count_below(16 + i, later_bank(i))
            for t in range(LAST_STEP + 1):
                ahead, last, second = (piece_at(t + i) for i in (1, -1, -2))
                lb = TAIL_AT.index(t) if t in TAIL_AT else None
                if t in TAIL_AT[:B]:
                    tail(lb)
                    logits(second)
                    tail_mean(lb)
                    turn_values(second, 0)
                    tail_variance(lb)
                    turn_values(second, 1)
                    tail_norm(lb)
                    split_features(1 + FEATURES_AT.index(t))
                    compact(last)
                    turn_values(second, 2)
                    subtract(last)
                else:
                    if last is not None:
                        compact(last)
                    if last == 0:
                        for i in RANKS_LATER[2]:
                            if i % 2:
                                count_below(16 + i, later_bank(i))
                    if second is not None:
                        logits(second)
                        if PIECES in WINDOWS_AT[t]:
                            first_windows(PIECES)
                        turn_values(second, 0)
                        if lb == B:
                            tail(lb)
                        turn_values(second, 1)
                        if lb == B:
                            tail_mean(lb)
                    if last is not None:
                        subtract(last)
                    for half_of, half, part in HALF_AT[t]:
                        tail_half(half_of, half, [part])
                    if second is not None:
                        turn_values(second, 2)
                for g in WINDOWS_AT[t]:
                    if g % PIECES == 0 and g > PIECES:
                        first_windows(g)
                if ahead is not None and not fresh(t):
                    front(ahead, 2)
                    front(ahead, 3)
                if t in FEATURES_AT and lb is None:
                    one_hot(1)
                    split_features(1 + FEATURES_AT.index(t))
                if lb == B:
                    tail_variance(lb)
                    tail_norm(lb)
                if lb == 2 * B - 1:
                    tail(lb)
                    tail_mean(lb)
                    tail_variance(lb)
                    tail_norm(lb)
                if t == 1:
                    for i in RANKS_LATER[3]:
                        if i % 2:
                            count_below(16 + i, later_bank(i))
                if fresh(t):
                    front(ahead, 2)
                    front(ahead, 3)

            def row_stats(src, at):
                link(v.bn_stats(rst[:, 4:10], src))
                v.bn_aggr(rst[:, at:at + 2], rst[:, 4:10]).then_inc(var_ready, 1)

            dve.wait_ge(h3_ready, 1)
            h3_ps = banks[0][0:T, :]
            row_stats(h3_ps, 10)
            wait_rstd()
            link(v.tensor_scalar(h3, h3_ps, rst[:, 10:11], rst[:, 11:12], ALU.subtract, ALU.mult))
            link(v.scalar_tensor_tensor(h3, h3, 0.2, h3, ALU.mult, ALU.max))
            dve.wait_ge(ld_x_rows, 32)
            link(v.tensor_tensor(x1, xr, h3, ALU.add))
            row_stats(x1, 12)
            wait_rstd()
            v.tensor_scalar(h3, x1, rst[:, 12:13], rst[:, 13:14], ALU.subtract, ALU.mult).then_inc(xn_ready, 1)

            dve.wait_ge(gp_ready, 1)
            dve.wait_ge(edf_ready, 1)
            col = [gp[:, i * T:(i + 1) * T] for i in range(12)]
            up, delta, power, keep, tmp = col[0], col[1], col[2], col[3], col[4:4 + G]
            link(v.tensor_copy(up, banks[0][:, 0:T]))
            link(v.tensor_scalar(delta, banks[1][:, 0:T], local_sb[:, 0:1], None, ALU.subtract))
            link(v.scalar_tensor_tensor(keep, delta, -2.5, up, ALU.is_ge, ALU.mult))
            link(v.scalar_tensor_tensor(keep, delta, 2.5, keep, ALU.is_le, ALU.mult))
            link(v.tensor_copy(power, delta))
            for m in range(G):
                if m:
                    link(v.tensor_tensor(power, power, delta, ALU.mult))
                ins = v.scalar_tensor_tensor(tmp[m], power, edf[:, m:m + 1], up if m < 4 else keep,
                                             ALU.mult, ALU.mult)
                if m < G - 1:
                    link(ins)
            ins.then_inc(tmp_ready, 1)
            def act_turned(j):
                _, n, c0 = FBANKS[j]
                dve.wait_ge(act_in, j + 1)
                nb = (n + P - 1) // P
                whole = n // P
                v.tensor_copy(actT[:, c0:c0 + whole, :], view(banks[j % 2], 0, P, 0, [[T, whole], [1, T]]))\
                 .then_inc(actT_ready, 1)
                if whole < nb:
                    w = n - whole * P
                    v.tensor_copy(actT[0:w, c0 + whole, :], banks[j % 2][0:w, whole * T:nb * T]).then_inc(actT_ready, 1)

            for j, (f0, n, _) in enumerate(FBANKS):
                gate_ps, up_ps = gate_up(banks, j)
                dve.wait_ge(gu_exp, j + 1)
                s_ = sig[:, 0:n]
                link(v.tensor_scalar(s_, s_, 1.0, None, ALU.add))
                link(v.reciprocal(s_, s_))
                link(v.tensor_tensor(s_, gate_ps, s_, ALU.mult))
                v.tensor_tensor(act_rows[:, f0:f0 + n], up_ps, s_, ALU.mult).then_inc(gu_used, 1)
                if j >= 1:
                    act_turned(j - 1)
            act_turned(2)
            dve.wait_ge(y_ready, 1)
            link(v.tensor_tensor(x2, z_ps[0:T, :], x1, ALU.add))
            link(v.bn_stats(rst[:, 4:10], x2))
            v.bn_aggr(rst[:, 0:2], rst[:, 4:10]).then_inc(var_ready, 1)
            wait_rstd()
            v.tensor_scalar(xn2, x2, rst[:, 0:1], rst[:, 1:2], ALU.subtract, ALU.mult).then_inc(xn2_ready, 1)
            dve.wait_ge(xn2_turned, 1)
            v.tensor_copy(xnT, view(v_ps, 0, P, 0, [[T, NK], [1, T]])).then_inc(xn2T_ready, 1)

            dve.wait_ge(moe_h, 1)
            h = mo[:, 0:32]
            g_b1, gam, bet, g_b2, rev = (rowc_sb[:, a:a + w]
                                         for a, w in ((0, 32), (32, 32), (64, 32), (96, E), (96 + E, E)))
            link(v.tensor_tensor(h, banks[0][0:T, E * R:E * R + 32], g_b1, ALU.add))
            link(v.bn_stats(rst[:, 4:10], h))
            v.bn_aggr(rst[:, 2:4], rst[:, 4:10]).then_inc(var_ready, 1)
            wait_rstd()
            link(v.tensor_scalar(h, h, rst[:, 2:3], rst[:, 3:4], ALU.subtract, ALU.mult))
            link(v.tensor_tensor(h, h, gam, ALU.mult))
            link(v.tensor_tensor(h, h, bet, ALU.add))
            v.tensor_scalar(h, h, 0.0, None, ALU.max).then_inc(moe_relu, 1)
            dve.wait_ge(moe_relu_turned, 1)
            v.tensor_copy(hT, banks[1][0:32, 0:T]).then_inc(moe_hT, 1)
            dve.wait_ge(moe_gates, 1)
            gt = mo[:, 32:40]
            top = mo[:, 40:48]
            link(v.tensor_tensor(gt, banks[2][0:T, 0:E], g_b2, ALU.add))
            link(v.max(top, gt))
            eq, pk, one = mo[:, 48:56], mo[:, 56:64], mo[:, 64:80]
            free = mo[:, 96:104]
            for k in range(2):
                link(v.tensor_scalar(eq, gt, top[:, k:k + 1], None, ALU.is_equal))
                if k == 1:
                    link(v.tensor_tensor(eq, eq, free, ALU.mult))
                link(v.tensor_tensor(pk, eq, rev, ALU.mult))
                link(v.tensor_reduce(mo[:, 80 + k:81 + k], pk, AX, ALU.max))
                link(v.tensor_scalar(one[:, 8 * k:8 * k + 8], rev, mo[:, 80 + k:81 + k], None, ALU.is_equal))
                if k == 0:
                    link(v.tensor_scalar(free, one[:, 0:8], -1.0, 1.0, ALU.mult, ALU.add))
            v.tensor_copy(mo[:, 110:126], one).then_inc(picks_ready, 1)
            v.tensor_tensor(mo[:, 199:200], top[:, 1:2], top[:, 0:1], ALU.subtract).then_inc(top_exp_in, 1)
            dve.wait_ge(top_exp, 1)
            link(v.tensor_scalar(mo[:, 201:202], mo[:, 200:201], 1.0, None, ALU.add))
            link(v.reciprocal(mo[:, 202:203], mo[:, 201:202]))
            link(v.tensor_tensor(mo[:, 203:204], mo[:, 202:203], mo[:, 200:201], ALU.mult))
            dve.wait_ge(counts_ready, 1)
            allow = mo[:, 130:146]
            link(v.tensor_scalar(allow, banks[3][0:T, 0:16], float(CAP), 1.0 / R, ALU.is_le, ALU.mult))
            link(v.tensor_tensor(allow, allow, one, ALU.mult))
            link(v.tensor_scalar(allow[:, 0:8], allow[:, 0:8], mo[:, 202:203], None, ALU.mult))
            link(v.scalar_tensor_tensor(allow[:, 0:8], allow[:, 8:16], mo[:, 203:204], allow[:, 0:8],
                                        ALU.mult, ALU.add))
            v.tensor_tensor(view(mo, 0, T, 256, [[R, E], [1, R]]), view(s_ps, 0, T, 0, [[R, E], [1, R]]),
                            view(mo, 0, T, 130, [[1, E], [0, R]]), ALU.mult).then_inc(lora_ready, 1)
            dve.wait_ge(lora_turned, 1)
            v.tensor_copy(tT, banks[1][:, 128:128 + T]).then_inc(lora_T, 1)
            dve.wait_ge(moe_out, 1)
            v.tensor_tensor(xn2, z_ps[0:T, :], x2, ALU.add).then_inc(y_out, 1)

        @block.tensor
        def _(pe):
            mm = pe.matmul
            pe.wait_ge(ld_first, 48)
            pe.wait_ge(scaled_co, 1)
            for k in range(NK):
                last = pe.transpose(z_ps[:, 6 * k:6 * k + 6], co_sb[:, k * P:(k + 1) * P], id_sb[0:6, 0:6])
            last.then_inc(co_turned, 1)
            pe.wait_ge(ld_graph, 64)
            for l in range(2):
                oc = OUT_CH[l]
                for s_ in range(2):
                    mm(r_ps[:, 192 * l + s_ * 64:192 * l + s_ * 64 + oc], wlin_sb[:, l, s_ * P:(s_ + 1) * P],
                       wconv_sb[:, l, 0:oc], start=True, stop=True)
                last = mm(r_ps[:, 192 * l + 128:192 * l + 129], wconv_sb[:, l, :], blin_sb[:, l:l + 1],
                          start=True, stop=True)
            last.then_inc(fold_ready, 1)
            pe.wait_ge(digits_ready, 1)
            for k in range(NK):
                last = pe.transpose(z_ps[0:40, k * P:(k + 1) * P], dg[:, 40 * k:40 * k + 40], id_sb[:, :])
            last.then_inc(digits_turned, 1)

            def differences(b, m, k, bank):
                pe.wait_ge((weights_ready, late_weights_ready)[b], 2 * m + 2)
                for part in range(2):
                    at = (2 * m + part) * N + k * P
                    last = mm(bank, lw[b][:, at:at + P], rhs2[:], start=part == 0, stop=part == 1)
                return last

            def turn_features(lb):
                l, b = divmod(lb, B)
                pe.wait_ge(ft_ready, lb + 1)
                if lb >= 1:
                    pe.wait_ge(gc_ready, lb)
                if lb >= 2:
                    pe.wait_ge(hs_ready, 3 * pieces_up_to(FEATURES_AT[lb - 1] - 3))
                for k in range(NK):
                    last = pe.transpose(z_ps[:, k * C:(k + 1) * C], ft[l][:, b, k * P:(k + 1) * P],
                                        id_sb[0:C, 0:C])
                last.then_inc(ft_turned, 1)

            for i in range(16):
                if i >= 7:
                    pe.wait_ge((counted_d, counted_a)[(i - 7) % 2 == 0], (i - 7) // 2 + 1)
                if i == 7:
                    turn_features(0)
                differences(0, *divmod(i, NK), banks[i % 7]).then_inc(diff_d_ready if i % 2 else diff_a_ready, 1)
            pe.wait_ge(counted_a, 8)
            pe.wait_ge(counted_d, 8)

            def repeat_features(lb):
                l, b = divmod(lb, B)
                if lb >= 2:
                    pe.wait_ge(log_ready, pieces_up_to(FEATURES_AT[lb - 1] - 2))
                elif lb == 1:
                    pe.wait_ge(log_ready, pieces_up_to(FEATURES_AT[0] - 1))
                mm(r_ps[:, :], const("rep")[0:C, :], ft[l][:, b, :], start=True, stop=True).then_inc(rep_ready, 1)

            def gather(lb):
                l, b = divmod(lb, B)
                pe.wait_ge(parts_ready, lb + 1)
                if lb < 2:
                    pe.wait_ge(onehot_ready, 16 * (b + 1))
                for pt in range(NK):
                    for m in range(M):
                        n = 0
                        for k in range(NK):
                            o = ((b * NK + k) * M + PERMS[l][m]) * N + pt * P
                            for part in range(3):
                                last = mm(z_ps[:, pt * P + m * C:pt * P + (m + 1) * C], oh[:, o:o + P],
                                          fpartb[:, part * P + k * C:part * P + (k + 1) * C],
                                          start=n == 0, stop=n == 3 * NK - 1)
                                n += 1
                last.then_inc(gathered, 1)

            def sort_features(lb):
                pe.wait_ge(turned_ready, lb + 1)
                for k in range(NK):
                    last = pe.transpose(z_ps[:, k * P:(k + 1) * P], gs[:, k * P:(k + 1) * P], id_sb[:, :])
                last.then_inc(sorted_ready, 1)

            def centre(lb):
                l = lb // B
                if lb == 1:
                    pe.wait_ge(hs_ready, 3 * pieces_up_to(FEATURES_AT[0] - 2))
                pe.wait_ge(rep_used, 2 * (lb + 1))
                pe.wait_ge(fs_ready, 2 * (lb + 1))
                oc = OUT_CH[l]
                side = P // oc
                for q in range(PIECES):
                    p0, o = oc * (q % side), (q // side) * PTS
                    last = mm(z_ps[p0:p0 + oc, o:o + PTS], wn_sb[:, l, 0:oc], f16f[:, q * PTS:(q + 1) * PTS],
                              start=True, stop=True)
                last.then_inc(centre_ready, 1)

            def scores(g):
                pe.wait_ge(bd_act_ready, 2 * (g + 1))
                pe.wait_ge(bd_dve_ready, 2 * (g + 1))
                if g >= 1:
                    pe.wait_ge(max_ready, g)
                d, o = (g % 2) * BLOCKS * P, (g % QBUF) * COLS
                for t in range(BLOCKS):
                    last = mm(s_ps[:, t * SLOT:t * SLOT + PB * K], qbd[:, d + t * P:d + (t + 1) * P],
                              qc[:, o + t * SLOT:o + t * SLOT + PB * K], start=True, stop=True)
                last.then_inc(s_ready, 1)

            def row_max(g):
                pe.wait_ge(md_ready, g + 1)
                if g >= 1:
                    pe.wait_ge(sub_ready, g)
                mm(mt_ps[:, 0:NC], negones, md[:], start=True, stop=True).then_inc(mt_ready, 1)

            def row_sum(g):
                pe.wait_ge(exp_ready, g + 1)
                if g >= 1:
                    pe.wait_ge(log_ready, g)
                at = LINE.index(g) + 1
                made = sum(t_ < at or at == t_ in TAIL_AT for t_ in FEATURES_AT)
                pe.wait_ge(rep_used, 2 * (1 + made))
                mm(r_ps[:, 0:NC], posones, ex[:], start=True, stop=True).then_inc(sum_ready, 1)

            def project(g, i):
                halves = 1 + g // (B * PIECES)
                j, half = divmod(i, halves)
                t0, n = THIRDS[j]
                c = value_chunks(g) + i
                if i == 0:
                    wait_windows(pe, g)
                if c >= 2:
                    pe.wait_ge(vt_ready, c - 1)
                variant = 0 if halves == 1 else 1 + half
                for part in range(3):
                    w = (variant * 3 + part) * P
                    o = (g % QBUF) * COLS + t0 * SLOT
                    last = mm(v_ps[:, (c % 2) * 512:(c % 2) * 512 + n * SLOT], wv[:, w:w + P],
                              qc[:, o:o + n * SLOT], start=part == 0, stop=part == 2)
                last.then_inc(v_ready, 1)

            def attend(g, j):
                lb, q = divmod(g, PIECES)
                l = lb // B
                oc = OUT_CH[l]
                p0 = oc * (q % (P // oc))
                i = 3 * g + j
                at = LINE.index(g) + 3
                if j == 0:
                    pe.wait_ge(spread_ready, 3 * (g + 1))
                    pe.wait_ge(vt_ready, value_chunks(g + 1))
                    pe.wait_ge(gc_ready, 1 + sum(t_ + (t_ == FEATURES_AT[0]) < at for t_ in FEATURES_AT))
                    if at - 1 == FEATURES_AT[0]:
                        pe.wait_ge(fs_ready, 4)
                if i >= 1:
                    pe.wait_ge(hs_ready, i)
                t0, n = THIRDS[j]
                for t in range(n):
                    w = vt[:, (g % 2) * 2 * COLS + (t0 + t) * oc:(g % 2) * 2 * COLS + (t0 + t + 1) * oc]
                    a = (g % 2) * COLS + (t0 + t) * SLOT
                    last = mm(z_ps[p0:p0 + oc, t * PB * K:(t + 1) * PB * K], w, px[:, a:a + PB * K],
                              start=True, stop=True)
                last.then_inc(h_ready, 1)

            def conv3(b, parts):
                pe.wait_ge(ft_ready, 5 + (2 in parts and b))
                for j in parts:
                    kk = 64 if j == 2 else 32
                    last = mm(banks[0][b * C:b * C + C, :], wc3_sb[0:kk, j, :], ft[j][0:kk, b, :],
                              start=j == 0, stop=j == 2)
                return last

            def average(lb, r):
                pe.wait_ge(stat_in, 2 * lb + r + 1)
                mm(mt_ps[:, 440:441], const(f"mean{lb // B}"), mv[:, 2:3], start=True, stop=True)\
                    .then_inc(stat_mean, 1)

            def later_differences(part):
                for i in RANKS_LATER[part]:
                    n = LATER_ORDER.index(i)
                    before = [j for j in LATER_ORDER[:n] if later_bank_at(j) == later_bank_at(i)]
                    if before:
                        same = [j for j in LATER_ORDER[:LATER_ORDER.index(before[-1]) + 1] if j % 2 == before[-1] % 2]
                        pe.wait_ge(counted_d if before[-1] % 2 else counted_a, 8 + len(same))
                    differences(1, *divmod(i, NK), later_bank(i)).then_inc(diff_d_ready if i % 2 else diff_a_ready, 1)

            repeat_features(0)
            later_differences(0)
            gather(0)
            sort_features(0)
            later_differences(1)
            centre(0)
            pe.wait_ge(wv_ready, 12)
            for t in range(LAST_STEP + 1):
                now, last, second, third = (piece_at(t - i) for i in range(4))
                feats = 1 + FEATURES_AT.index(t) if t in FEATURES_AT else None

                def values(j):
                    if second is not None:
                        halves = 1 + second // (B * PIECES)
                        for i in range(halves * j, halves * j + halves):
                            project(second, i)

                def outputs(j):
                    if third is not None:
                        attend(third, j)

                tail = TAIL_AT.index(t) if t in TAIL_AT else None
                urgent = feats and tail is not None
                if t - 1 == FEATURES_AT[0]:
                    sort_features(1)
                outputs(0)
                values(0)
                outputs(1)
                if urgent:
                    average(tail, 0)
                values(1)
                if urgent:
                    average(tail, 1)
                    outputs(2)
                    values(2)
                    turn_features(feats)
                    repeat_features(feats)
                    gather(feats)
                    row_max(last)
                    sort_features(feats)
                else:
                    if last is not None:
                        row_max(last)
                    if tail == B:
                        average(tail, 0)
                    outputs(2)
                    values(2)
                    if tail == B:
                        average(tail, 1)
                if last is not None:
                    row_sum(last)
                if now == 0:
                    pe.wait_ge(counted_a, 8 + len(RANKS_LATER[0]))
                if now is not None:
                    scores(now)
                if now == 0:
                    pe.wait_ge(gc_ready, 1)
                    later_differences(2)
                    pe.wait_ge(counted_d, 8 + len(RANKS_LATER[1]))
                if now == 1:
                    later_differences(3)
                    pe.wait_ge(counted_a, 16)
                    pe.wait_ge(counted_d, 16)
                if feats and not urgent:
                    turn_features(feats)
                    repeat_features(feats)
                    gather(feats)
                if urgent:
                    centre(feats)
                elif t - 1 == FEATURES_AT[0]:
                    centre(1)
                if tail == 2 * B - 1:
                    average(tail, 0)
                    average(tail, 1)
                if t == LAST_STEP - 1:
                    pe.wait_ge(max_ready, STEPS)
                    conv3(0, [0, 1, 2])
                    conv3(1, [0, 1])
            conv3(1, [2]).then_inc(h3_ready, 1)
            pe.wait_ge(xn_ready, 1)
            for k in range(NK):
                last = pe.transpose(banks[2][:, k * T:(k + 1) * T], h3[:, k * P:(k + 1) * P], id_sb[0:T, 0:T])
            last.then_inc(xn_turned, 1)
            pe.wait_ge(xnT_ready, 1)
            pe.wait_ge(ld_ffn, 80)
            for j in range(2):
                for k in range(NK):
                    last = mm(banks[j][:, 0:T], upgate_sb[:, k, j * S:(j + 1) * S], xnT[:, k, :],
                              start=k == 0, stop=k == NK - 1)
            last.then_inc(gp_ready, 1)

            def hidden(j):
                f0, n, _ = FBANKS[j]
                for which, bank in enumerate(gate_up(banks, j)):
                    for k in range(NK):
                        w = up_sb[:, k * F + f0:k * F + f0 + n] if which else gate_sb[:, k, f0:f0 + n]
                        last = mm(bank, xnT[:, k, :], w, start=k == 0, stop=k == NK - 1)
                last.then_inc(gu_ready, 1)

            def turn_hidden(j):
                f0, n, _ = FBANKS[j]
                pe.wait_ge(gu_used, j + 1)
                pe.wait_ge(tmp_ready, 1)
                if j == 2:
                    pe.wait_ge(actT_ready, 1)
                for i in range((n + P - 1) // P):
                    w = min(P, n - i * P)
                    last = pe.transpose(banks[j % 2][0:w, i * T:(i + 1) * T], act_rows[:, f0 + i * P:f0 + i * P + w],
                                        id_sb[0:T, 0:T])
                last.then_inc(act_in, 1)

            def down(j):
                _, n, c0 = FBANKS[j]
                pe.wait_ge(actT_ready, j + 1 if j < 2 else 4)
                for i in range(c0, c0 + (n + P - 1) // P):
                    w = FCH[i][1]
                    last = mm(z_ps[0:T, :], actT[0:w, i, :], ffn2_sb[0:w, i * N:(i + 1) * N],
                              start=False, stop=i == NF - 1)
                return last

            pe.wait_ge(ld_up, 16)
            hidden(0)
            hidden(1)
            turn_hidden(0)
            hidden(2)
            pe.wait_ge(ld_late, 64)
            for m in range(G + 1):
                w = fuse_sb[:, m * N:(m + 1) * N]
                lhs = gp[:, 0:T] if m == 0 else gp[:, (3 + m) * T:(4 + m) * T]
                mm(z_ps[0:T, :], lhs, w, start=m == 0, stop=False)
            turn_hidden(1)
            pe.wait_ge(ld_down, 32)
            down(0)
            turn_hidden(2)
            down(1)
            down(2).then_inc(y_ready, 1)
            pe.wait_ge(xn2_ready, 1)
            for k in range(NK):
                last = pe.transpose(v_ps[:, k * T:(k + 1) * T], xn2[:, k * P:(k + 1) * P], id_sb[0:T, 0:T])
            last.then_inc(xn2_turned, 1)
            pe.wait_ge(xn2T_ready, 1)
            for k in range(NK):
                last = mm(banks[0][0:T, 0:E * R + 32], xnT[:, k, :], moe1_sb[:, k * moe1_w:(k + 1) * moe1_w],
                          start=k == 0, stop=k == NK - 1)
            last.then_inc(moe_h, 1)

            def main_product(k):
                mm(z_ps[0:T, :], xnT[:, k, :], moe2_sb[:, k * N:(k + 1) * N], start=k == 0, stop=False)

            main_product(0)
            main_product(1)
            pe.wait_ge(moe_relu, 1)
            pe.transpose(banks[1][0:32, 0:T], mo[:, 0:32], id_sb[0:T, 0:T]).then_inc(moe_relu_turned, 1)
            pe.wait_ge(moe_hT, 1)
            mm(banks[2][0:T, 0:E], hT, gw2_sb[:], start=True, stop=True).then_inc(moe_gates, 1)
            main_product(2)
            main_product(3)
            pe.wait_ge(picks_ready, 1)
            mm(banks[3][0:T, 0:16], const("ones")[0:T, 0:T], mo[:, 110:126], start=True, stop=True)\
                .then_inc(counts_ready, 1)
            pe.wait_ge(lora_ready, 1)
            pe.transpose(banks[1][:, 128:128 + T], mo[:, 256:256 + P], id_sb[0:T, 0:T]).then_inc(lora_turned, 1)
            pe.wait_ge(lora_T, 1)
            mm(z_ps[0:T, :], tT, moe3_sb, start=False, stop=True).then_inc(moe_out, 1)


def constants():
    import numpy as np
    p = np.arange(P)
    slot = p % SLOT
    point, o10 = slot // K, slot % K
    head = p // SLOT
    c = {}
    c["own"] = (point[:, None] == np.arange(PB)[None]).astype(np.float32)
    c["i10"] = (o10[:, None] == np.arange(K)[None]).astype(np.float32)
    same = (head[:, None] == head[None]) & (point[:, None] == point[None])
    c["posblk"] = same.astype(np.float32)
    c["negblk"] = -c["posblk"]
    c["off"] = np.where(point[:, None] == np.arange(PB)[None], 0.0, -1e30).astype(np.float32)
    c["eps"] = np.full((P, 1), EPS, np.float32)
    c["nhalf"] = np.full((P, 1), -0.5, np.float32)
    n = np.zeros((P, M, B, NK), np.int32)
    n[:] = p[:, None, None, None] + P * np.arange(NK)
    c["point"] = n.reshape(P, 32).view(np.float32)
    w = np.zeros((P, 2, B * M), np.float32)
    for bm in range(B * M):
        for digit, (part, value) in enumerate(((1, 1.0), (1, 256.0), (1, 65536.0), (0, 2.0 ** 23), (0, 2.0 ** 31))):
            w[8 * digit + bm, part, bm] = value
            w[64 + 8 * digit + bm, part, bm] = -value
    c["digit_w"] = w.reshape(P, 16)
    rep = np.zeros((P, P), np.float32)
    rep[p // M, p] = 1.0
    c["rep"] = rep
    for l in range(2):
        oc = OUT_CH[l]
        side = P // oc
        size = np.zeros(side)
        for q in range(PIECES):
            size[q % side] += PTS if q < PIECES - 1 else PTS_LAST
        c[f"mean{l}"] = ((p[:, None] % oc == p[None] % oc) * (size[p // oc] / N)[:, None]).astype(np.float32)
    c["ones"] = np.ones((P, P), np.float32)
    return np.ascontiguousarray(np.concatenate([c[name] for name, _ in CONST_WIDTHS], axis=1))


def kernel(**inputs):
    import numpy as np
    import concourse.bacc as bacc
    from concourse.bass_utils import run_bass_kernel_spmd as run

    a = {k: np.asarray(v) for k, v in inputs.items()}

    def chunks(w):
        return w.reshape(-1, P, w.shape[1]).transpose(1, 0, 2).reshape(P, -1)

    def rows(v):
        return np.broadcast_to(v, (T, v.shape[0]))

    wc3 = np.zeros((64, 3, C), np.float32)
    w3 = a["L0_xattn_W_conv3"].T
    wc3[0:32, 0], wc3[0:32, 1], wc3[:, 2] = w3[0:32], w3[32:64], w3[64:128]
    wd = a["L0_attn_ffn_down_w"].T
    whole = (NF - 1) * P
    lora_a = a["L0_ffn_lora_A"].transpose(1, 0, 2).reshape(N, E * R)
    df = a["L0_attn_discount_factor"]
    laid = {
        "x": a["x"].transpose(1, 0, 2),
        "coords": a["ctx_4096"][:, 0:3, :].reshape(6, N),
        "consts": constants(),
        "ident": np.eye(P, dtype=np.float32),
        "wlin": np.stack([a["L0_xattn_W_lin1"], a["L0_xattn_W_lin2"]], axis=1),
        "wconv": np.stack([np.tile(a["L0_xattn_W_conv1"].T, (1, 4)), np.tile(a["L0_xattn_W_conv2"].T, (1, 2))], axis=1),
        "blin": np.stack([a["L0_xattn_b_lin1"], a["L0_xattn_b_lin2"]], axis=1),
        "wc3": wc3,
        "upgate": chunks(np.concatenate([a["L0_attn_up_w"].T, a["L0_attn_gate_w"].T], axis=1)).reshape(P, NK, 2 * S),
        "local": np.concatenate([a["L0_attn_local_point"][:, None], np.broadcast_to(df, (P, G))], axis=1),
        "fuse": np.concatenate([a["L0_attn_local_approx_output"].T[:, None],
                                a["L0_attn_fuse_weight"].transpose(1, 2, 0)], axis=1).reshape(P, (G + 1) * N),
        "gate": chunks(a["L0_attn_ffn_gate_w"].T).reshape(P, NK, F),
        "up": chunks(a["L0_attn_ffn_up_w"].T),
        "ffn2a": chunks(wd[:whole]),
        "ffn2b": wd[whole:],
        "moe1": chunks(np.concatenate([lora_a, a["L0_ffn_gw1"].T], axis=1)),
        "moe2": chunks(a["L0_ffn_weight"].T),
        "moe3": a["L0_ffn_lora_B"].reshape(E * R, N),
        "rowc": np.concatenate([rows(a["L0_ffn_gb1"]), rows(a["L0_ffn_ln_gamma"]), rows(a["L0_ffn_ln_beta"]),
                                rows(a["L0_ffn_gb2"]), rows(np.arange(E, 0, -1).astype(np.float32))], axis=1),
        "gw2": a["L0_ffn_gw2"].T,
    }
    nc = bacc.Bacc("TRN2", target_bir_lowering=False, num_devices=1)
    arrays, args = {}, {}
    for name, value in laid.items():
        value = np.ascontiguousarray(value)
        arrays[f"in_{name}"] = value
        args[name] = nc.dram_tensor(f"in_{name}", value.shape, mybir.dt.from_np(value.dtype), kind="ExternalInput").ap()
    out = nc.dram_tensor("out_x", (T, N), F32, kind="ExternalOutput").ap()
    perceiver_layer(nc, out=out, **args)
    result = run(nc, [arrays], core_ids=[0])
    return result.results[0]["out_x"].reshape(B, C, N)
```
